# Optimizing a Trainium2 kernel written in Bass

```python
import numpy as np
import jax
import jax.numpy as jnp

def _softmax(x, axis=-1):
    return jax.nn.softmax(x, axis=axis)

def _gelu(x):
    return jax.nn.gelu(x, approximate=True)

def _silu(x):
    return jax.nn.silu(x)

def _sigmoid(x):
    return jax.nn.sigmoid(x)

def _layernorm(x, axis=-1, eps=1e-05):
    m = jnp.mean(x, axis=axis, keepdims=True)
    v = jnp.var(x, axis=axis, keepdims=True)
    return (x - m) / jnp.sqrt(v + eps)

def _scatter_add(tgt, idx, src, axis=0):
    return tgt.at[idx].add(src)

def _segment_sum(src, seg, n):
    return jax.ops.segment_sum(src, seg, n)
kernel_name = 'mk_perceiver_d1_seqx_r4_1c950a'

def setup_inputs(seed: int=0):
    np.random.seed(seed)
    _w = jnp.asarray

    def _rec_inputs():
        import jax
        import jax.numpy as jnp
        _rk = jax.random.key(seed)
        x = -0.0002928 + 1 * jax.random.normal(jax.random.fold_in(_rk, 1), (64, 64, 256), jnp.float32)
        _lenS = 64 - jax.random.randint(jax.random.fold_in(_rk, 7), (64,), 0, max(1, 64 // 4) + 1, jnp.int32)
        _lenS2 = 256 - jax.random.randint(jax.random.fold_in(_rk, 8), (64,), 0, max(1, 256 // 4) + 1, jnp.int32)
        _ctx_1024P = jax.random.normal(jax.random.fold_in(_rk, 11), (64, 16, 256), jnp.float32)
        _ctx_1024c = jax.random.dirichlet(jax.random.fold_in(_rk, 511), 0.3 * jnp.ones((16,), jnp.float32), (64, 256))
        _ctx_1024t = jnp.einsum('bsk,bkd->bsd', _ctx_1024c, _ctx_1024P)
        _ctx_1024t = _ctx_1024t * jax.lax.rsqrt(jnp.mean(jnp.square(_ctx_1024t)) + 1e-12) * 0.953939
        ctx_1024 = -1.39393e-06 + 0.999914 * (_ctx_1024t + 0.3 * jax.random.normal(jax.random.fold_in(_rk, 611), (64, 256, 256), jnp.float32))
        return (x, ctx_1024)
    x, ctx_1024 = _rec_inputs()

    def _L0_xattn_setup():
        import jax, jax.numpy as jnp
        import numpy as np
        DIM = 256
        H = 16
        D = DIM // H
        SCALE = D ** (-0.5)
        LN_EPS = 1e-05

        def _layernorm(t, gamma, beta):
            mu = jnp.mean(t, axis=-1, keepdims=True)
            var = jnp.var(t, axis=-1, keepdims=True)
            return (t - mu) * jax.lax.rsqrt(var + LN_EPS) * gamma + beta
        key = jax.random.key(seed)
        ks = jax.random.split(key, 8)
        s = DIM ** (-0.5)
        return {'x': jax.random.normal(ks[0], (2, 512, DIM), dtype=jnp.float32), 'y': jax.random.normal(ks[1], (2, 512, DIM), dtype=jnp.float32), 'Wq': jax.random.normal(ks[2], (DIM, DIM), dtype=jnp.float32) * s, 'bq': jnp.zeros((DIM,), dtype=jnp.float32), 'Wkv': jax.random.normal(ks[3], (2 * DIM, DIM), dtype=jnp.float32) * s, 'bkv': jnp.zeros((2 * DIM,), dtype=jnp.float32), 'q_gamma': jnp.ones((D,), dtype=jnp.float32), 'q_beta': jnp.zeros((D,), dtype=jnp.float32), 'k_gamma': jnp.ones((D,), dtype=jnp.float32), 'k_beta': jnp.zeros((D,), dtype=jnp.float32), 'Wproj': jax.random.normal(ks[4], (DIM, DIM), dtype=jnp.float32) * s, 'bproj': jnp.zeros((DIM,), dtype=jnp.float32)}
    _L0_xattn_all = _L0_xattn_setup()
    _L0_xattn_in = {k: v for k, v in _L0_xattn_all.items() if k in ('Wq', 'bq', 'Wkv', 'bkv', 'q_gamma', 'q_beta', 'k_gamma', 'k_beta', 'Wproj', 'bproj')}
    del _L0_xattn_all

    def _L0_attn_setup():
        import jax, jax.numpy as jnp
        import numpy as np
        EMBED_DIM = 256
        NUM_HEADS = 16
        HEAD_DIM = EMBED_DIM // NUM_HEADS
        LAMBDA_ENTANGLE = 0.35
        key = jax.random.key(seed)
        ks = jax.random.split(key, 10)
        B, S, D = (2, 512, EMBED_DIM)
        init = 1.0 / np.sqrt(D)
        x = jax.random.normal(ks[0], (B, S, D), dtype=jnp.float32)
        Wq = jax.random.uniform(ks[1], (D, D), jnp.float32, -init, init)
        bq = jax.random.uniform(ks[2], (D,), jnp.float32, -init, init)
        Wk = jax.random.uniform(ks[3], (D, D), jnp.float32, -init, init)
        bk = jax.random.uniform(ks[4], (D,), jnp.float32, -init, init)
        Wv = jax.random.uniform(ks[5], (D, D), jnp.float32, -init, init)
        bv = jax.random.uniform(ks[6], (D,), jnp.float32, -init, init)
        Wo = jax.random.uniform(ks[7], (D, D), jnp.float32, -init, init)
        bo = jax.random.uniform(ks[8], (D,), jnp.float32, -init, init)
        J_attn = jax.random.normal(ks[9], (NUM_HEADS, HEAD_DIM, HEAD_DIM), dtype=jnp.float32) * 0.02
        lambda_attn = jnp.asarray(LAMBDA_ENTANGLE, dtype=jnp.float32)
        return {'x': x, 'Wq': Wq, 'bq': bq, 'Wk': Wk, 'bk': bk, 'Wv': Wv, 'bv': bv, 'Wo': Wo, 'bo': bo, 'J_attn': J_attn, 'lambda_attn': lambda_attn}
    _L0_attn_all = _L0_attn_setup()
    _L0_attn_in = {k: v for k, v in _L0_attn_all.items() if k in ('Wq', 'bq', 'Wk', 'bk', 'Wv', 'bv', 'Wo', 'bo', 'J_attn', 'lambda_attn')}
    del _L0_attn_all

    def _L0_ffn_setup():
        import jax, jax.numpy as jnp
        import numpy as np
        B, S, H = (2, 512, 256)
        E, K, F_EXP, F_SHARED = (16, 2, 128, 256)
        key = jax.random.key(seed)
        ks = jax.random.split(key, 9)
        sc = 1.0 / np.sqrt(H)
        scf = 1.0 / np.sqrt(F_EXP)
        scfs = 1.0 / np.sqrt(F_SHARED)
        return {'x': jax.random.normal(ks[0], (B, S, H), dtype=jnp.float32), 'router_w': jax.random.normal(ks[1], (H, E), dtype=jnp.float32) * sc, 'gate_w': jax.random.normal(ks[2], (E, H, F_EXP), dtype=jnp.float32) * sc, 'up_w': jax.random.normal(ks[3], (E, H, F_EXP), dtype=jnp.float32) * sc, 'down_w': jax.random.normal(ks[4], (E, F_EXP, H), dtype=jnp.float32) * scf, 'shared_gate_w': jax.random.normal(ks[5], (H, F_SHARED), dtype=jnp.float32) * sc, 'shared_up_w': jax.random.normal(ks[6], (H, F_SHARED), dtype=jnp.float32) * sc, 'shared_down_w': jax.random.normal(ks[7], (F_SHARED, H), dtype=jnp.float32) * scfs}
    _L0_ffn_all = _L0_ffn_setup()
    _L0_ffn_in = {k: v for k, v in _L0_ffn_all.items() if k in ('router_w', 'gate_w', 'up_w', 'down_w', 'shared_gate_w', 'shared_up_w', 'shared_down_w')}
    del _L0_ffn_all
    return {'x': x, 'ctx_1024': ctx_1024, 'L0_xattn_Wq': _L0_xattn_in['Wq'], 'L0_xattn_bq': _L0_xattn_in['bq'], 'L0_xattn_Wkv': _L0_xattn_in['Wkv'], 'L0_xattn_bkv': _L0_xattn_in['bkv'], 'L0_xattn_q_gamma': _L0_xattn_in['q_gamma'], 'L0_xattn_q_beta': _L0_xattn_in['q_beta'], 'L0_xattn_k_gamma': _L0_xattn_in['k_gamma'], 'L0_xattn_k_beta': _L0_xattn_in['k_beta'], 'L0_xattn_Wproj': _L0_xattn_in['Wproj'], 'L0_xattn_bproj': _L0_xattn_in['bproj'], 'L0_attn_Wq': _L0_attn_in['Wq'], 'L0_attn_bq': _L0_attn_in['bq'], 'L0_attn_Wk': _L0_attn_in['Wk'], 'L0_attn_bk': _L0_attn_in['bk'], 'L0_attn_Wv': _L0_attn_in['Wv'], 'L0_attn_bv': _L0_attn_in['bv'], 'L0_attn_Wo': _L0_attn_in['Wo'], 'L0_attn_bo': _L0_attn_in['bo'], 'L0_attn_J_attn': _L0_attn_in['J_attn'], 'L0_attn_lambda_attn': _L0_attn_in['lambda_attn'], 'L0_ffn_router_w': _L0_ffn_in['router_w'], 'L0_ffn_gate_w': _L0_ffn_in['gate_w'], 'L0_ffn_up_w': _L0_ffn_in['up_w'], 'L0_ffn_down_w': _L0_ffn_in['down_w'], 'L0_ffn_shared_gate_w': _L0_ffn_in['shared_gate_w'], 'L0_ffn_shared_up_w': _L0_ffn_in['shared_up_w'], 'L0_ffn_shared_down_w': _L0_ffn_in['shared_down_w']}

def reference(x, ctx_1024, L0_xattn_Wq, L0_xattn_bq, L0_xattn_Wkv, L0_xattn_bkv, L0_xattn_q_gamma, L0_xattn_q_beta, L0_xattn_k_gamma, L0_xattn_k_beta, L0_xattn_Wproj, L0_xattn_bproj, L0_attn_Wq, L0_attn_bq, L0_attn_Wk, L0_attn_bk, L0_attn_Wv, L0_attn_bv, L0_attn_Wo, L0_attn_bo, L0_attn_J_attn, L0_attn_lambda_attn, L0_ffn_router_w, L0_ffn_gate_w, L0_ffn_up_w, L0_ffn_down_w, L0_ffn_shared_gate_w, L0_ffn_shared_up_w, L0_ffn_shared_down_w):
    import jax
    import jax.numpy as jnp

    def _L0_xattn_ref(x, y, Wq, bq, Wkv, bkv, q_gamma, q_beta, k_gamma, k_beta, Wproj, bproj):
        import jax, jax.numpy as jnp
        import numpy as np
        DIM = 256
        H = 16
        D = DIM // H
        SCALE = D ** (-0.5)
        LN_EPS = 1e-05

        def _layernorm(t, gamma, beta):
            mu = jnp.mean(t, axis=-1, keepdims=True)
            var = jnp.var(t, axis=-1, keepdims=True)
            return (t - mu) * jax.lax.rsqrt(var + LN_EPS) * gamma + beta
        B, N, C = x.shape
        M = y.shape[1]
        q = (x @ Wq.T + bq).reshape(B, N, H, D).transpose(0, 2, 1, 3)
        kv = (y @ Wkv.T + bkv).reshape(B, M, 2, H, D).transpose(2, 0, 3, 1, 4)
        k, v = (kv[0], kv[1])
        q = _layernorm(q, q_gamma, q_beta) * SCALE
        k = _layernorm(k, k_gamma, k_beta)
        attn = jax.nn.softmax(jnp.einsum('bhnd,bhmd->bhnm', q, k), axis=-1)
        out = jnp.einsum('bhnm,bhmd->bhnd', attn, v)
        out = out.transpose(0, 2, 1, 3).reshape(B, N, C)
        return out @ Wproj.T + bproj

    def _L0_attn_ref(x, Wq, bq, Wk, bk, Wv, bv, Wo, bo, J_attn, lambda_attn):
        import jax, jax.numpy as jnp
        import numpy as np
        EMBED_DIM = 256
        NUM_HEADS = 16
        HEAD_DIM = EMBED_DIM // NUM_HEADS
        LAMBDA_ENTANGLE = 0.35
        B, S, D = x.shape
        H, Hd = (NUM_HEADS, HEAD_DIM)
        scale = jnp.sqrt(jnp.asarray(Hd, dtype=x.dtype))

        def heads(W, b):
            y = jnp.einsum('bsd,ed->bse', x, W) + b
            return y.reshape(B, S, H, Hd).transpose(0, 2, 1, 3)
        Q = heads(Wq, bq)
        K = heads(Wk, bk)
        V = heads(Wv, bv)
        scores = jnp.einsum('bhid,bhjd->bhij', Q, K) / scale
        QJ = jnp.einsum('bhid,hde->bhie', jnp.tanh(Q), J_attn)
        delta = jnp.einsum('bhie,bhje->bhij', QJ, jnp.tanh(K))
        scores = scores + lambda_attn * delta
        causal = jnp.triu(jnp.ones((S, S), dtype=bool), k=1)
        scores = jnp.where(causal, -jnp.inf, scores)
        probs = jax.nn.softmax(scores, axis=-1)
        out = jnp.einsum('bhij,bhjd->bhid', probs, V)
        out = out.transpose(0, 2, 1, 3).reshape(B, S, D)
        return jnp.einsum('bsd,ed->bse', out, Wo) + bo

    def _L0_ffn_ref(x, router_w, gate_w, up_w, down_w, shared_gate_w, shared_up_w, shared_down_w):
        import jax, jax.numpy as jnp
        import numpy as np
        B, S, H = (2, 512, 256)
        E, K, F_EXP, F_SHARED = (16, 2, 128, 256)
        b, s, h = x.shape
        T = b * s
        x_flat = x.reshape(T, h)
        shared_out = jax.nn.silu(x @ shared_gate_w) * (x @ shared_up_w) @ shared_down_w
        router_probs = jax.nn.softmax(x_flat @ router_w, axis=-1)
        topk_probs, topk_idx = jax.lax.top_k(router_probs, K)
        coeff = jnp.einsum('tk,tke->te', topk_probs, jax.nn.one_hot(topk_idx, E, dtype=x.dtype))

        def expert_step(acc, ws):
            g, u, d, c = ws
            inter = jax.nn.silu(x_flat @ g) * (x_flat @ u)
            return (acc + inter @ d * c[:, None], None)
        routed, _ = jax.lax.scan(expert_step, jnp.zeros((T, h), dtype=x.dtype), (gate_w, up_w, down_w, coeff.T))
        return routed.reshape(b, s, h) + shared_out
    x = x + _L0_xattn_ref(_layernorm(x, axis=-1), ctx_1024, L0_xattn_Wq, L0_xattn_bq, L0_xattn_Wkv, L0_xattn_bkv, L0_xattn_q_gamma, L0_xattn_q_beta, L0_xattn_k_gamma, L0_xattn_k_beta, L0_xattn_Wproj, L0_xattn_bproj)
    x = x + _L0_attn_ref(_layernorm(x, axis=-1), L0_attn_Wq, L0_attn_bq, L0_attn_Wk, L0_attn_bk, L0_attn_Wv, L0_attn_bv, L0_attn_Wo, L0_attn_bo, L0_attn_J_attn, L0_attn_lambda_attn)
    x = x + _L0_ffn_ref(_layernorm(x, axis=-1), L0_ffn_router_w, L0_ffn_gate_w, L0_ffn_up_w, L0_ffn_down_w, L0_ffn_shared_gate_w, L0_ffn_shared_up_w, L0_ffn_shared_down_w)
    return x

_drawn_inputs = setup_inputs


def setup_inputs(seed=0):
    import zlib

    import numpy as np

    out = dict(_drawn_inputs(seed))
    spreads = {'L0_xattn_bq': (0.0, 0.351),
     'L0_xattn_bkv': (0.0, 0.1),
     'L0_xattn_q_gamma': (1.0, 0.2),
     'L0_xattn_q_beta': (0.0, 0.347),
     'L0_xattn_k_gamma': (1.0, 0.2),
     'L0_xattn_k_beta': (0.0, 2.0),
     'L0_xattn_bproj': (0.0, 0.1)}
    factors = {'L0_attn_bq': 31.065, 'L0_attn_bk': 64.0, 'L0_attn_J_attn': 29.857}
    for name, (base, spread) in spreads.items():
        noise = np.random.default_rng([zlib.crc32(name.encode()), seed]).standard_normal(out[name].shape)
        drawn = base * np.exp(spread * noise) if base else spread * noise
        out[name] = jnp.asarray(drawn.astype(out[name].dtype))
    for name, factor in factors.items():
        out[name] = (out[name] * factor).astype(out[name].dtype)
    return out
```

```python
from contextlib import ExitStack

import numpy as np

import concourse.bass as bass
from concourse import mybir

ALU = mybir.AluOpType
ACT = mybir.ActivationFunctionType
AX = mybir.AxisListType
F32 = mybir.dt.float32
BF16 = mybir.dt.bfloat16
I32 = mybir.dt.int32
U32 = mybir.dt.uint32

P = 128
DIM = 256
H, HD = 16, 16
B, N, M = 64, 64, 256
TOK = B * N
TILES = TOK // P
KD = DIM // P
HG = P // HD
G = H // HG
HP = H // 2
E, F = 16, 128
PAIRS = 2 * TOK
SLOTS = PAIRS // P + E
DEEP = 4
EPS = 1e-5
MASKED = -1e30
MAGIC = 1597463007.0

A_K = (0, 2)
A_V = (1, 3)
A_XT, A_Q = 4, 5
A_KT = (6, 7)
A_QT = 8
A_MAX = 9
A_S = 17
A_OT, A_PROJ = 25, 26
A_USES, A_BANKS = 27, 3
B_XT, B_QK, B_V, B_QJ = 0, 1, 2, 3
B_S, B_PT, B_O = (4, 5), (6, 7), (8, 9)
B_WO, B_HT, B_ROUTE, B_GU, B_ST, B_Y = 10, 11, 12, 13, 14, 15
B_USES, B_BANKS = 16, 4


class Event:

    def __init__(self, sem, k=1, per=1):
        self.sem, self.k, self.per = sem, k, per

    def of(self, tile):
        return tile * self.per + self.k


def freed(eng, event, tile):
    if not isinstance(tile, int) or tile > 0:
        eng.wait_ge(event.sem, tile * event.per + (event.k - event.per))


def ahead(eng, event, j, lag):
    if not isinstance(j, int) or j >= lag:
        eng.wait_ge(event.sem, event.of(j - lag))


def column(t, j):
    return t[:, j:j + 1] if isinstance(j, int) else t[:, bass.ds(j, 1)]


def row(t, j):
    return t[:, j, :] if isinstance(j, int) else t[:, bass.ds(j, 1), :].rearrange("p o m -> p (o m)")


def block_of(t, j):
    return t[j] if isinstance(j, int) else t[bass.ds(j, 1), :, :].rearrange("o p m -> p (o m)")


def perceiver_block(nc, w, out):
    x, ctxT = w["x"], w["ctxT"]
    with ExitStack() as ctx:
        def sb(name, shape, dt=F32):
            return ctx.enter_context(nc.sbuf_tensor(name, shape, dt))

        def sem(name):
            return ctx.enter_context(nc.semaphore(name))

        wx_q = sb("wx_q", [P, KD, DIM])
        wx_kv = sb("wx_kv", [P, KD, 2 * DIM])
        wx_o = sb("wx_o", [P, 2, DIM])
        wa = {n: sb("wa_" + n, [P, KD, DIM]) for n in "qkvo"}
        jmix = sb("jmix", [P, G, P])
        w_route = sb("w_route", [P, KD, E])
        ws_gu = sb("ws_gu", [P, KD, 2 * DIM])
        ws_down = sb("ws_down", [P, KD, DIM])
        cols = sb("cols", [P, 15])
        rows = sb("rows", [P, 4, DIM])
        ident = sb("ident", [P, P])
        headmask = sb("headmask", [P, HG])
        causal = sb("causal", [P, N])
        negones = sb("negones", [P, P], BF16)
        minushalf = sb("minushalf", [P, 1])
        before = sb("before", [P, P])
        ones = sb("ones", [P, P])
        numbers = sb("numbers", [P, E + P + 2 * SLOTS + TILES])
        lane_no = sb("lane_no", [P, 1])
        idle = sb("idle", [P, 1])
        w_gu = sb("w_gu", [P, KD, E, 2 * F])
        w_down = sb("w_down", [P, E, DIM])
        bcol = sb("bcol", [P, 4, P])
        wmean = sb("wmean", [P, KD, 3 * H])

        xt = sb("xt", [P, DIM])
        ct = sb("ct", [P, KD, 2, M])
        lnA = sb("lnA", [P, 16])
        xn = sb("xn", [P, DIM])
        xres = sb("xres", [P, DIM])
        xnT = sb("xnT", [P, KD, P])
        qc = sb("qc", [P, DIM])
        qsq = sb("qsq", [P, DIM])
        kc = sb("kc", [P, 4, DIM])
        ksq = sb("ksq", [P, 4, DIM])
        va = sb("va", [P, 4, HP, 34])
        ss = sb("ss", [P, 5 * H])
        rr = sb("rr", [P, 5 * H])
        nt = sb("nt", [P, 5 * H])
        qn = sb("qn", [P, DIM])
        kn = ksq
        kT = sb("kT", [P, G, 2 * M])
        kTb = sb("kTb", [P, G, 2 * M], BF16)
        qT = sb("qT", [P, G, P])
        qbd = sb("qbd", [P, G, 2, HG, N])
        qbdb = sb("qbdb", [P, G, 2, HG, N], BF16)
        mx = sb("mx", [P, 2, HP])
        shift = sb("shift", [P, 2, HP, P], BF16)
        pt = sb("pt", [P, 2, 2, HG * N])
        rz = sb("rz", [P, 2, HP])
        on = sb("on", [P, 2, HP, HD])
        oT = sb("oT", [P, 2, 2, N])
        x1 = sb("x1", [P, DIM])

        lnB = sb("lnB", [P, 16])
        x1n = sb("x1n", [P, DIM])
        x1b = sb("x1b", [P, DIM])
        x1T = sb("x1T", [P, KD, P])
        qkT = sb("qkT", [P, 2, G, P])
        tqk = sb("tqk", [P, 2, G, P])
        v2 = sb("v2", [P, HP, 2, 2 * HD])
        bd = sb("bd", [P, 2, G, 2, HG, N])
        sc = sb("sc", [P, HP * 2, N])
        sh = sc
        ex = pn = sc
        mx2 = sb("mx2", [P, HP * 2])
        z2 = sb("z2", [P, HP * 2])
        rz2 = sb("rz2", [P, HP * 2])
        pT = sb("pT", [P, HP, P])
        o2T = sb("o2T", [P, G, 2, N])
        x2 = sb("x2", [P, DIM])
        lnC = sb("lnC", [P, 16])
        h = sb("h", [P, DIM])
        hT = sb("hT", [P, KD, P])
        th = sb("th", [P, DIM])
        sg = sb("sg", [P, DIM])
        su = sb("su", [P, DIM])
        suT = sb("suT", [P, KD, P])
        base = sb("base", [P, DIM])
        logits = sb("logits", [P, TILES, E])

        tables = bd[:, :, :, :, :, :].rearrange("p s g b h n -> p (s g b h n)").rearrange("p (k n) -> p k n", k=8)
        prob, first, second, tmp, tmp2, sel, cnt, incl = (tables[:, k, 0:TILES * E] for k in range(8))
        carry = sb("carry", [P, TILES * E])
        most = sb("most", [P, 7, TILES])
        per_expert = sb("per_expert", [P, 5, E])
        per_int = sb("per_int", [P, 2, E], I32)
        pos = sb("pos", [P, 2, TILES])
        pos_i = sb("pos_i", [P, 2, 2, TILES], I32)
        pos_u = sb("pos_u", [P, 2 * TILES], U32)
        in_tile = sb("in_tile", [P, 2, TILES])
        of_tile = sb("of_tile", [P, 2, TILES])
        coef = sb("coef", [P, 2, TILES])
        past = kT[:, :, :].rearrange("p g m -> p (g m)")
        weights_at = sb("weights_at", [P, SLOTS])
        weights_at_i = sb("weights_at_i", [P, SLOTS], I32)
        at_slot = sb("at_slot", [P, 4, P], BF16)
        at_column = sb("at_column", [P, 4, 2 * SLOTS], BF16)
        ids_f = sb("ids_f", [P, 2 * SLOTS])
        ids = sb("ids", [P, SLOTS], U32)
        now_ids = sb("now_ids", [P, DEEP], U32)
        now_pos = sb("now_pos", [P, 2 * DEEP], U32)
        xg = pt[:, :, :, :].rearrange("p a b n -> p (a b n)")[:, 0:DEEP * DIM].rearrange("p (c d) -> p c d", c=DEEP)
        xgT = sb("xgT", [P, 2, DIM])
        eth = sb("eth", [P, 2, F])
        esg = sb("esg", [P, 2, F])
        esu = sb("esu", [P, 2, F])
        esuT = sb("esuT", [P, 2, P])
        y = kc[:, :, :]
        yg = qbd[:, :, :, :, :].rearrange("p g b h n -> p (g b h n)")[:, 0:DEEP * 2 * DIM].rearrange("p (c k d) -> p c k d", c=DEEP, k=2)
        res = kn[:, :, :]
        base4 = kT[:, :, :].rearrange("p g (c d) -> p (g c) d", d=DIM)
        rows_d = nc.dram_tensor("normalised_rows", (TOK, DIM), F32, kind="Internal").ap()
        base_d = nc.dram_tensor("rows_without_experts", (TOK, DIM), F32, kind="Internal").ap()
        y_d = nc.dram_tensor("expert_rows", (SLOTS * P, DIM), F32, kind="Internal").ap()

        ringA = ctx.enter_context(nc.psum_tensor("ringA", [P, A_BANKS, 512], F32))
        oA = ctx.enter_context(nc.psum_tensor("oA", [P, 512], F32))
        ringB = ctx.enter_context(nc.psum_tensor("ringB", [P, B_BANKS, 512], F32))

        def bankA(u):
            return ringA[:, u % A_BANKS, :]

        def bankB(u):
            return ringB[:, u % B_BANKS, :]

        def ring(name, banks, uses):
            full = [sem(f"full{name}{k}") for k in range(banks)]
            free = [sem(f"free{name}{k}") for k in range(banks)]
            return ([Event(full[u % banks], u // banks + 1, uses // banks) for u in range(uses)],
                    [Event(free[u % banks], u // banks + 1, uses // banks) for u in range(uses)])

        fullA, freeA = ring("A", A_BANKS, A_USES)
        fullB, freeB = ring("B", B_BANKS, B_USES)

        def claim(pe, free, banks, u, tile):
            if u >= banks:
                pe.wait_ge(free[u - banks].sem, free[u - banks].of(tile))
            else:
                freed(pe, free[u + len(free) - banks], tile)

        def claimA(pe, u, tile):
            claim(pe, freeA, A_BANKS, u, tile)

        def claimB(pe, u, tile):
            claim(pe, freeB, B_BANKS, u, tile)

        x1_ready, x2_ready, su_ready, qkT_ready = freeA[A_PROJ], freeB[B_WO], freeB[B_GU], freeB[B_QK]
        bdt_ready, o2T_ready = freeB[B_QJ], freeB[B_O[1]]
        mx_ready = (freeA[A_MAX + 3], freeA[A_MAX + 7])

        weights_in = sem("weights_in")
        weights_set = sem("weights_set")
        setup_dve = sem("setup_dve")
        setup_pe = sem("setup_pe")
        x_in, h_out, base_out = sem("x_in"), sem("h_out"), sem("base_out")
        base_in = [sem(f"base_in{c}") for c in range(DEEP)]
        routed, exps_ready, sel_ready, counted = sem("routed"), sem("exps_ready"), sem("sel_ready"), sem("counted")
        positions_ready, ids_summed, ids_ready = sem("positions_ready"), sem("ids_summed"), sem("ids_ready")
        ranks_read, hots_used_all = sem("ranks_read"), sem("hots_used_all")
        rows_in = [sem(f"rows_in{c}") for c in range(DEEP)]
        y_out = [sem(f"y_out{c}") for c in range(DEEP)]
        yg_in = [sem(f"yg_in{c}") for c in range(DEEP)]
        out_done = [sem(f"out_done{c}") for c in range(DEEP)]
        ctx_in = [sem(f"ctx_in{k}") for k in range(KD)]
        def chain(name, *steps):
            one = sem(name)
            return {n: Event(one, k + 1, len(steps)) for k, n in enumerate(steps)}

        ev = {}
        for ln in "abc":
            ev.update(chain(f"{ln}_norm", f"{ln}_stats", f"{ln}_meanvar", f"{ln}_veps"))
            ev.update(chain(f"{ln}_rstd", f"{ln}_rstd"))
        ev.update(chain("newton", "s_eps", "s_shift", "newton_y0", *(f"newton_{s}" for n in range(3)
                        for s in (f"t{n}", f"u{n}", f"y{n + 1}"))))
        ev.update(chain("k_sq", "k_sq01", "k_sq23"))
        ev.update(chain("k_sum", "k_sum01", "k_sum23"))
        ev.update(chain("kn_ready", "kn01_ready", "kn23_ready"))
        ev.update(chain("qbd_ready", "qbd0_ready", "qbd1_ready"))
        ev.update(chain("shift_ready", "shift0_ready", "shift1_ready"))
        ev.update(chain("pv", "pv0", "pv1", "pv2", "pv3"))
        ev.update(chain("heads_out", "rz0", "onlo0", "on0_ready", "rz1", "onlo1", "on1_ready"))
        ev.update(chain("z2", "z2_ready", "rz2_ready"))
        for n in ("xn_ready xres_ready q_sq q_sum qn_ready kTb_ready qbdb_ready x1n_ready x1b_ready qq_ready tq_ready"
                  " bdq_ready mx2_ready sh_ready ex_ready pn_ready h_ready th_ready sg_ready").split():
            ev.update(chain(n, n))

        for n in ("hot_ready hot_used ids_copied rows_turned rowsT_ready gu_ready eth_ready esg_ready esu_ready"
                  " esu_turned esuT_ready y_summed y_ready pos_copied half_summed res_ready").split():
            ev.update(chain(n, n))

        def bank(k):
            return ringA[:, k, :] if k < A_BANKS else oA[:, :] if k == A_BANKS else ringB[:, k - A_BANKS - 1, :]

        block = ctx.enter_context(nc.Block())

        def rounds(eng, count, body, drain=0):
            for c in range(DEEP):
                body(c, c, 0)
            with eng.Fori(1, count // DEEP) as n:
                for c in range(DEEP):
                    body(n * DEEP + c, c, n)
            for c in range(drain):
                body(count + c, c, count // DEEP)

        def tiles(eng, stage_ab):
            stage_ab(0, None)
            stage_ab(1, 0)
            with eng.Fori(2, TILES) as i:
                stage_ab(i, i - 1)
            stage_ab(None, TILES - 1)

        x_d = x.rearrange("(t p) d -> t p d", p=P)
        ctx_d = ctxT.rearrange("(t b) (k p) m -> t k p b m", b=2, p=P)

        @block.sync
        def _(sp):
            def load(dst, src):
                sp.dma_start(dst, src).then_inc(weights_in, 16)

            for dst, name in ((wx_q, "wx_q"), (wx_kv, "wx_kv"), (wa["q"], "wa_q"), (wa["k"], "wa_k"),
                              (wa["v"], "wa_v"), (wa["o"], "wa_o"), (w_route, "w_route"),
                              (ws_down, "ws_down")):
                load(dst[:, :, :], w[name].rearrange("(k p) n -> p k n", p=P))
            load(ws_gu[:, :, 0:DIM], w["ws_gate"].rearrange("(k p) n -> p k n", p=P))
            load(ws_gu[:, :, DIM:2 * DIM], w["ws_up"].rearrange("(k p) n -> p k n", p=P))
            load(wx_o[:, :, :], w["wx_o"])
            load(jmix[:, :, :], w["jmix"])
            load(cols[:, :], w["cols"])
            load(rows[:, :, :], w["rows"].partition_broadcast(P))
            load(ident[:, :], w["ident"])
            load(headmask[:, :], w["headmask"])
            load(causal[:, :], w["causal"])
            load(before[:, :], w["before"])
            load(numbers[:, :], w["numbers"].partition_broadcast(P))
            load(lane_no[:, :], w["lane_no"])
            load(w_down[:, :, :], w["e_down"].rearrange("e f d -> f e d"))
            for k in range(KD):
                load(w_gu[:, k, :, 0:F], w["e_gate"][:, k * P:(k + 1) * P, :].rearrange("e p f -> p e f"))
                load(w_gu[:, k, :, F:2 * F], w["e_up"][:, k * P:(k + 1) * P, :].rearrange("e p f -> p e f"))

            def load_tile(a):
                if True:
                    freed(sp, fullA[A_V[1]], a)
                    for k in range(KD):
                        here = ctx_d[a, k] if isinstance(a, int) else \
                            ctx_d[bass.ds(a, 1), k, :, :, :].rearrange("o p b m -> p (o b) m")
                        sp.dma_start(ct[:, k, :, :], here).then_inc(ctx_in[k], 16)
                    freed(sp, ev["xn_ready"], a)
                    freed(sp, ev["xres_ready"], a)
                    sp.dma_start(xt[:, :], block_of(x_d, a)).then_inc(x_in, 16)
            def store(b):
                if True:
                    sp.wait_ge(ev["h_ready"].sem, ev["h_ready"].of(b))
                    sp.dma_start(block_of(rows_t, b), h[:, :]).then_inc(h_out, 16)
                    sp.wait_ge(freeB[B_Y].sem, freeB[B_Y].of(b))
                    sp.dma_start(block_of(base_t, b), base[:, :]).then_inc(base_out, 16)
            rows_t = rows_d.rearrange("(t p) d -> t p d", p=P)
            base_t = base_d.rearrange("(t p) d -> t p d", p=P)
            y_t = y_d.rearrange("(t p) d -> t p d", p=P)
            out_t = out.rearrange("(t p) d -> t p d", p=P)
            load_tile(0)
            load_tile(1)
            with sp.Fori(1, TILES - 1) as i:
                load_tile(i + 1)
                store(i - 1)
            store(TILES - 2)
            store(TILES - 1)

            def store_y(j, c, n):
                sp.wait_ge(ev["y_ready"].sem, ev["y_ready"].of(j))
                sp.dma_start(block_of(y_t, j), y[:, c, :]).then_inc(y_out[c], 16)
            rounds(sp, SLOTS, store_y)

            def store_out(t, c, n):
                ahead(sp, ev["half_summed"], t, DEEP)
                sp.dma_start(base4[:, c, :], block_of(base_t, t)).then_inc(base_in[c], 16)
                if not isinstance(t, int) or t >= 2:
                    store_last(t - 2, (c - 2) % DEEP, n)

            def store_last(t, c, n):
                sp.wait_ge(ev["res_ready"].sem, ev["res_ready"].of(t))
                sp.dma_start(block_of(out_t, t), res[:, c, :]).then_inc(out_done[c], 16)
            sp.wait_ge(base_out, 16 * TILES)
            rounds(sp, TILES, store_out)
            for t in (TILES - 2, TILES - 1):
                store_last(t, t % DEEP, 0)
            for c in range(DEEP):
                sp.wait_ge(out_done[c], 16 * TILES // DEEP)

        @block.tensor
        def _(pe):
            pe.wait_ge(setup_dve, 1)
            for side, wo in ((0, wx_o), (1, wa["o"])):
                for k in range(2):
                    mm = pe.matmul(ringA[:, side, 0:DIM], bcol[:, 2 * side + k, :], wo[:, k, :], start=(k == 0), stop=(k == 1))
            mm.then_inc(setup_pe, 1)
            pe.wait_ge(weights_set, 1)

            def kv(a, jj):
                if jj == 0:
                    for k in range(KD):
                        pe.wait_ge(ctx_in[k], a * 16 + 16)
                for part, u in ((0, A_K[jj]), (1, A_V[jj])):
                    claimA(pe, u, a)
                    for c in range(2):
                        j = 2 * jj + c
                        for k in range(KD):
                            mm = pe.matmul(bankA(u)[:, c * DIM:(c + 1) * DIM],
                                           ct[:, k, j // 2, (j % 2) * P:(j % 2 + 1) * P],
                                           wx_kv[:, k, part * DIM:(part + 1) * DIM], start=(k == 0), stop=(k == 1))
                    mm.then_inc(fullA[u].sem, 1)

            def turn(claim_, u, bank, full, src, tile):
                claim_(pe, u, tile)
                for k in range(KD):
                    mm = pe.transpose(bank(u)[:, k * P:(k + 1) * P], src[:, k * P:(k + 1) * P], ident[:, :])
                mm.then_inc(full[u].sem, 1)

            def project(claim_, u, bank, full, lhs, rhs, tile, n=DIM):
                claim_(pe, u, tile)
                for k in range(KD):
                    mm = pe.matmul(bank(u)[:, 0:n], lhs(k), rhs[:, k, 0:n], start=(k == 0), stop=(k == 1))
                mm.then_inc(full[u].sem, 1)

            def keys_turned(a):
                for g in range(G):
                    claimA(pe, A_KT[g], a)
                    if g == 0:
                        pe.wait_ge(ev["kn23_ready"].sem, ev["kn23_ready"].of(a))
                    for j in range(4):
                        mm = pe.transpose(bankA(A_KT[g])[:, j * P:(j + 1) * P], kn[:, j, g * P:(g + 1) * P], ident[:, :])
                    mm.then_inc(fullA[A_KT[g]].sem, 1)

            def rough_scores(a):
                pe.wait_ge(ev["kTb_ready"].sem, ev["kTb_ready"].of(a))
                pe.wait_ge(ev["qbdb_ready"].sem, ev["qbdb_ready"].of(a))
                for r in range(8):
                    b, g, half = r // 4, r // 2 % 2, r % 2
                    u = A_MAX + r
                    claimA(pe, u, a)
                    for c in range(2):
                        hh = 4 * half + 2 * c
                        mm = pe.matmul(bankA(u)[:, c * M:(c + 1) * M], qbdb[:, g, b, hh:hh + 2, :].rearrange("p a n -> p (a n)"),
                                       kTb[:, g, b * M:(b + 1) * M], start=True, stop=True)
                    mm.then_inc(fullA[u].sem, 1)

            def scores(a, r):
                b, g, mc = r // 4, r // 2 % 2, r % 2
                u = A_S + r
                claimA(pe, u, a)
                pe.matmul(bankA(u), kT[:, g, b * M + mc * P:b * M + (mc + 1) * P],
                          qbd[:, g, b, :, :].rearrange("p a n -> p (a n)"), start=True, stop=False)
                pe.wait_ge(ev[f"shift{b}_ready"].sem, ev[f"shift{b}_ready"].of(a))
                pe.matmul(bankA(u), negones[:, :], shift[:, b, 4 * g:4 * g + 4, :].rearrange("p a n -> p (a n)"),
                          start=False, stop=True).then_inc(fullA[u].sem, 1)

            def weighted(a, q):
                b, g = q // 2, q % 2
                pe.wait_ge(freeA[A_S + 2 * q + 1].sem, freeA[A_S + 2 * q + 1].of(a))
                if q == 0:
                    freed(pe, ev["on1_ready"], a)
                if q == 2:
                    pe.wait_ge(ev["on0_ready"].sem, ev["on0_ready"].of(a))
                for p4 in range(4):
                    hp = 4 * g + p4
                    for mc in range(2):
                        mm = pe.matmul(oA[:, hp * 34:hp * 34 + 33], pt[:, q % 2, mc, p4 * P:(p4 + 1) * P],
                                       va[:, 2 * b + mc, hp, 0:33], start=(mc == 0), stop=(mc == 1))
                mm.then_inc(ev[f"pv{q}"].sem, 1)

            def heads_turned(a):
                claimA(pe, A_OT, a)
                for b in range(2):
                    pe.wait_ge(ev[f"on{b}_ready"].sem, ev[f"on{b}_ready"].of(a))
                    mm = pe.transpose(bankA(A_OT)[:, b * P:(b + 1) * P], on[:, b, :, :].rearrange("p a d -> p (a d)"), ident[:, :])
                mm.then_inc(fullA[A_OT].sem, 1)

            def self_qk(b):
                claimB(pe, B_QK, b)
                pe.wait_ge(freeB[B_XT].sem, freeB[B_XT].of(b))
                for s, wt in enumerate((wa["q"], wa["k"])):
                    for g in range(G):
                        at = (s * G + g) * P
                        for k in range(KD):
                            mm = pe.matmul(bankB(B_QK)[:, at:at + P], wt[:, k, g * P:(g + 1) * P], x1T[:, k, :],
                                           start=(k == 0), stop=(k == 1))
                mm.then_inc(fullB[B_QK].sem, 1)

            def self_mix(b):
                claimB(pe, B_QJ, b)
                pe.wait_ge(ev["tq_ready"].sem, ev["tq_ready"].of(b))
                for g in range(G):
                    mm = pe.matmul(bankB(B_QJ)[:, g * P:(g + 1) * P], jmix[:, g, :], tqk[:, 0, g, :], start=True, stop=True)
                mm.then_inc(fullB[B_QJ].sem, 1)

            def self_scores(b, g):
                claimB(pe, B_S[g], b)
                pe.wait_ge(ev["bdq_ready"].sem, ev["bdq_ready"].of(b))
                pe.wait_ge(bdt_ready.sem, bdt_ready.of(b))
                pe.wait_ge(qkT_ready.sem, qkT_ready.of(b))
                for p4 in range(4):
                    for bb in range(2):
                        at = (p4 * 2 + bb) * N
                        for s, right in enumerate((qkT, tqk)):
                            mm = pe.matmul(bankB(B_S[g])[:, at:at + N],
                                           bd[:, s, g, bb, 2 * p4:2 * p4 + 2, :].rearrange("p a n -> p (a n)"),
                                           right[:, 1, g, bb * N:(bb + 1) * N], start=(s == 0), stop=(s == 1))
                mm.then_inc(fullB[B_S[g]].sem, 1)

            def probs_turned(b, g):
                claimB(pe, B_PT[g], b)
                pe.wait_ge(ev["pn_ready"].sem, ev["pn_ready"].of(b))
                for p4 in range(4):
                    hp = 4 * g + p4
                    mm = pe.transpose(bankB(B_PT[g])[:, p4 * P:(p4 + 1) * P],
                                      pn[:, 2 * hp:2 * hp + 2, :].rearrange("p a n -> p (a n)"), ident[:, :])
                mm.then_inc(fullB[B_PT[g]].sem, 1)

            def self_weighted(b, bb):
                claimB(pe, B_O[bb], b)
                if bb == 0:
                    pe.wait_ge(freeB[B_V].sem, freeB[B_V].of(b))
                    pe.wait_ge(freeB[B_PT[1]].sem, freeB[B_PT[1]].of(b))
                pe.matmul(bankB(B_O[bb])[0:32, 0:HD], v2[:, 0, 0, :], v2[:, 0, 0, 0:HD], start=True, stop=True)
                lo = bb * N
                for g in range(G):
                    for odd in range(2):
                        for p4 in range(4):
                            hp = 4 * g + p4
                            mm = pe.matmul(bankB(B_O[bb])[32 * p4:32 * p4 + 32, g * N:(g + 1) * N],
                                           v2[lo:lo + N, hp, odd, :], pT[lo:lo + N, hp, odd * N:(odd + 1) * N],
                                           start=(odd == 0), stop=(odd == 1))
                mm.then_inc(fullB[B_O[bb]].sem, 1)

            def step(a, b):
                if a is not None:
                    kv(a, 0)
                if b is not None:
                    pe.wait_ge(ev["x1n_ready"].sem, ev["x1n_ready"].of(b))
                    turn(claimB, B_XT, bankB, fullB, x1n, b)
                if a is not None:
                    kv(a, 1)
                if b is not None:
                    self_qk(b)
                    project(claimB, B_V, bankB, fullB, lambda k: x1T[:, k, :], wa["v"], b)
                if a is not None:
                    pe.wait_ge(ev["xn_ready"].sem, ev["xn_ready"].of(a))
                    turn(claimA, A_XT, bankA, fullA, xn, a)
                if b is not None:
                    self_mix(b)
                if a is not None:
                    pe.wait_ge(freeA[A_XT].sem, freeA[A_XT].of(a))
                    project(claimA, A_Q, bankA, fullA, lambda k: xnT[:, k, :], wx_q, a)
                if b is not None:
                    self_scores(b, 0)
                    self_scores(b, 1)
                if a is not None:
                    keys_turned(a)
                    pe.wait_ge(ev["qn_ready"].sem, ev["qn_ready"].of(a))
                    turn(claimA, A_QT, bankA, fullA, qn, a)
                if b is not None:
                    probs_turned(b, 0)
                    probs_turned(b, 1)
                if a is not None:
                    rough_scores(a)
                if b is not None:
                    self_weighted(b, 0)
                    self_weighted(b, 1)
                if a is not None:
                    for r in range(3):
                        scores(a, r)
                    weighted(a, 0)
                if b is not None:
                    pe.wait_ge(o2T_ready.sem, o2T_ready.of(b))
                    project(claimB, B_WO, bankB, fullB, lambda k: o2T[:, k, :, :].rearrange("p a n -> p (a n)"), wa["o"], b)
                if a is not None:
                    scores(a, 3)
                    scores(a, 4)
                    weighted(a, 1)
                    scores(a, 5)
                if b is not None:
                    pe.wait_ge(ev["h_ready"].sem, ev["h_ready"].of(b))
                    turn(claimB, B_HT, bankB, fullB, h, b)
                if a is not None:
                    scores(a, 6)
                    weighted(a, 2)
                if b is not None:
                    pe.wait_ge(freeB[B_HT].sem, freeB[B_HT].of(b))
                    project(claimB, B_ROUTE, bankB, fullB, lambda k: hT[:, k, :], w_route, b, E)
                    project(claimB, B_GU, bankB, fullB, lambda k: hT[:, k, :], ws_gu, b, 2 * DIM)
                if a is not None:
                    scores(a, 7)
                    weighted(a, 3)
                if b is not None:
                    pe.wait_ge(su_ready.sem, su_ready.of(b))
                    turn(claimB, B_ST, bankB, fullB, su, b)
                if a is not None:
                    heads_turned(a)
                if b is not None:
                    pe.wait_ge(freeB[B_ST].sem, freeB[B_ST].of(b))
                    project(claimB, B_Y, bankB, fullB, lambda k: suT[:, k, :], ws_down, b)
                if a is not None:
                    pe.wait_ge(freeA[A_OT].sem, freeA[A_OT].of(a))
                    project(claimA, A_PROJ, bankA, fullA, lambda k: oT[:, k, :, :].rearrange("p a n -> p (a n)"), wx_o, a)
            tiles(pe, step)

            pe.wait_ge(sel_ready, 1)
            pe.matmul(bank(0)[:, 0:TILES * E], before[:, :], sel, start=True, stop=True)
            pe.matmul(bank(1)[:, 0:TILES * E], ones[:, :], sel, start=True, stop=True).then_inc(counted, 1)
            pe.wait_ge(positions_ready, 1)
            for lo in range(0, 2 * SLOTS, P):
                n = min(P, 2 * SLOTS - lo)
                pe.matmul(bank(2)[:, lo:lo + n], ones[:, :], v2[:, 0:n // HD, 0, HD:2 * HD], start=(lo == 0), stop=False,
                          skip_group_check=True)

            def place(t, c, n):
                for k in range(2):
                    q = 2 * (c % 2) + k
                    if k == 0:
                        pe.wait_ge(ev["hot_ready"].sem, ev["hot_ready"].of(t))
                    mm = pe.matmul(bank(2)[:, 0:2 * SLOTS], at_slot[:, q, :], at_column[:, q, :], start=False, stop=False,
                                   skip_group_check=True)
                mm.then_inc(ev["hot_used"].sem, 1)
            rounds(pe, TILES, place)
            pe.matmul(bank(2)[:, 0:HD], ones[:, :], v2[:, 0, 0, HD:2 * HD], start=False, stop=True, skip_group_check=True).then_inc(ids_summed, 1)

            def expert(j, c, n):
                def now(lag):
                    i = j - lag
                    return not isinstance(i, int) or 0 <= i < SLOTS, i, (c - lag) % DEEP

                go, i, s = now(0)
                if go:
                    pe.wait_ge(rows_in[s], 16 * n + 16)
                    ahead(pe, ev["rowsT_ready"], i, 2)
                    for k in range(KD):
                        mm = pe.transpose(bank(s % 2)[:, k * P:(k + 1) * P], xg[:, s, k * P:(k + 1) * P], ident[:, :])
                    mm.then_inc(ev["rows_turned"].sem, 1)
                go, i, s = now(1)
                if go:
                    col = pe.value_load(column(weights_at_i[0:1, :], i), min_val=0, max_val=(E - 1) * DIM)
                    pe.wait_ge(ev["rowsT_ready"].sem, ev["rowsT_ready"].of(i))
                    ahead(pe, ev["esu_ready"], i, 2)
                    for k in range(KD):
                        mm = pe.matmul(bank(2 + s % 2)[:, 0:2 * F], xgT[:, s % 2, k * P:(k + 1) * P],
                                       w_gu[:, k, :, :].rearrange("p e f -> p (e f)")[:, bass.ds(col, 2 * F)],
                                       start=(k == 0), stop=(k == 1))
                    mm.then_inc(ev["gu_ready"].sem, 1)
                go, i, s = now(2)
                if go:
                    pe.wait_ge(ev["esu_ready"].sem, ev["esu_ready"].of(i))
                    ahead(pe, ev["esuT_ready"], i, 2)
                    pe.transpose(bank(4 + s % 2)[:, 0:P], esu[:, s % 2, :], ident[:, :]).then_inc(ev["esu_turned"].sem, 1)
                go, i, s = now(3)
                if go:
                    col = pe.value_load(column(weights_at_i[0:1, :], i), min_val=0, max_val=(E - 1) * DIM)
                    pe.wait_ge(ev["esuT_ready"].sem, ev["esuT_ready"].of(i))
                    ahead(pe, ev["y_ready"], i, 2)
                    pe.matmul(bank(6 + s % 2)[:, 0:DIM], esuT[:, s % 2, :],
                              w_down[:, :, :].rearrange("p e d -> p (e d)")[:, bass.ds(col, DIM)], start=True, stop=True)\
                        .then_inc(ev["y_summed"].sem, 1)
            pe.wait_ge(ids_ready, 1)
            rounds(pe, SLOTS, expert, 3)

        @block.scalar
        def _(act):
            act.wait_ge(weights_set, 1)

            def values(a, jj):
                u = A_V[jj]
                act.wait_ge(fullA[u].sem, fullA[u].of(a))
                if jj == 0:
                    freed(act, ev["pv3"], a)
                act.activation(va[:, 2 * jj:2 * jj + 2, :, 0:32],
                               bankA(u).rearrange("p (j h d) -> p j h d", j=2, d=32), ACT.Copy).then_inc(freeA[u].sem, 1)

            def squares(a, jj):
                u = A_K[jj]
                act.wait_ge(freeA[u].sem, freeA[u].of(a))
                if True:
                    freed(act, ev[("k_sum01", "k_sum23")[jj]], a)
                act.activation(ksq[:, 2 * jj:2 * jj + 2, :], kc[:, 2 * jj:2 * jj + 2, :], ACT.Square)\
                    .then_inc(ev[("k_sq01", "k_sq23")[jj]].sem, 1)

            def step(a, b):
                if a is not None:
                    values(a, 0)
                    squares(a, 0)
                if b is not None:
                    act.wait_ge(fullB[B_XT].sem, fullB[B_XT].of(b))
                    freed(act, fullB[B_V], b)
                    act.copy(x1T[:, :, :].rearrange("p k n -> p (k n)"), bankB(B_XT)[:, 0:DIM]).then_inc(freeB[B_XT].sem, 1)
                if a is not None:
                    values(a, 1)
                    squares(a, 1)
                if b is not None:
                    act.wait_ge(fullB[B_QK].sem, fullB[B_QK].of(b))
                    freed(act, fullB[B_S[1]], b)
                    for s, fn, dst, done in ((0, ACT.Tanh, tqk, ev["tq_ready"]), (0, ACT.Identity, qkT, ev["qq_ready"]),
                                             (1, ACT.Identity, qkT, None), (1, ACT.Tanh, tqk, qkT_ready)):
                        for g in range(G):
                            at = (s * G + g) * P
                            ins = act.activation(dst[:, s, g, :], bankB(B_QK)[:, at:at + P], fn,
                                                 scale=HD ** -0.5 if (s, fn) == (0, ACT.Identity) else 1.0,
                                                 bias=cols[:, 13 + g:14 + g] if (s, fn) == (0, ACT.Identity)
                                                 else cols[:, 4 + 2 * s + g:5 + 2 * s + g])
                            if g == 1 and done:
                                ins.then_inc(done.sem, 1)
                    act.wait_ge(fullB[B_V].sem, fullB[B_V].of(b))
                    freed(act, fullB[B_O[1]], b)
                    vv = bankB(B_V)[:, 0:DIM].rearrange("p (h o d) -> p h o d", o=2, d=HD)
                    act.activation(v2[:, :, 0, 0:HD], vv[:, :, 0, :], ACT.Copy)
                    act.activation(v2[:, :, 1, HD:2 * HD], vv[:, :, 1, :], ACT.Copy).then_inc(freeB[B_V].sem, 1)
                if a is not None:
                    act.wait_ge(fullA[A_XT].sem, fullA[A_XT].of(a))
                    freed(act, fullA[A_Q], a)
                    act.copy(xnT[:, :, :].rearrange("p k n -> p (k n)"), bankA(A_XT)[:, 0:DIM]).then_inc(freeA[A_XT].sem, 1)
                    act.wait_ge(freeA[A_Q].sem, freeA[A_Q].of(a))
                    freed(act, ev["q_sum"], a)
                    act.activation(qsq[:, :], qc[:, :], ACT.Square).then_inc(ev["q_sq"].sem, 1)
                    for g in range(G):
                        act.wait_ge(fullA[A_KT[g]].sem, fullA[A_KT[g]].of(a))
                        if g == 0:
                            freed(act, fullA[A_S + 7], a)
                            freed(act, ev["kTb_ready"], a)
                        act.activation(kT[:, g, :], bankA(A_KT[g]), ACT.Identity, bias=cols[:, 3:4], scale=cols[:, 2:3])\
                            .then_inc(freeA[A_KT[g]].sem, 1)
                    act.wait_ge(fullA[A_QT].sem, fullA[A_QT].of(a))
                    freed(act, ev["qbd1_ready"], a)
                    act.activation(qT[:, :, :].rearrange("p k n -> p (k n)"), bankA(A_QT)[:, 0:DIM], ACT.Identity,
                                   bias=cols[:, 1:2], scale=cols[:, 0:1]).then_inc(freeA[A_QT].sem, 1)
                if b is not None:
                    act.wait_ge(ev["sh_ready"].sem, ev["sh_ready"].of(b))
                    freed(act, ev["pn_ready"], b)
                    act.activation(ex[:, :, :], sh[:, :, :], ACT.Exp).then_inc(ev["ex_ready"].sem, 1)
                    for g in range(G):
                        act.wait_ge(fullB[B_PT[g]].sem, fullB[B_PT[g]].of(b))
                        if g == 0:
                            freed(act, fullB[B_O[1]], b)
                        act.copy(pT[:, 4 * g:4 * g + 4, :].rearrange("p a n -> p (a n)"), bankB(B_PT[g])).then_inc(freeB[B_PT[g]].sem, 1)
                    freed(act, fullB[B_WO], b)
                    for bb in range(2):
                        act.wait_ge(fullB[B_O[bb]].sem, fullB[B_O[bb]].of(b))
                        ins = act.activation(o2T[:, :, bb, :], bankB(B_O[bb])[:, 0:P].rearrange("p (g n) -> p g n", g=G), ACT.Copy)
                        ins.then_inc(freeB[B_O[bb]].sem, 1)

                def exponentials(rounds):
                    for r in rounds:
                        act.wait_ge(fullA[A_S + r].sem, fullA[A_S + r].of(a))
                        q = r // 2
                        if r % 2 == 0:
                            if q >= 2:
                                act.wait_ge(ev[f"pv{q - 2}"].sem, ev[f"pv{q - 2}"].of(a))
                            else:
                                freed(act, ev[f"pv{q + 2}"], a)
                        act.activation(pt[:, q % 2, r % 2, :], bankA(A_S + r), ACT.Exp).then_inc(freeA[A_S + r].sem, 1)
                if a is not None:
                    exponentials(range(0, 6))
                if b is not None:
                    act.wait_ge(fullB[B_HT].sem, fullB[B_HT].of(b))
                    freed(act, fullB[B_GU], b)
                    act.copy(hT[:, :, :].rearrange("p k n -> p (k n)"), bankB(B_HT)[:, 0:DIM]).then_inc(freeB[B_HT].sem, 1)
                if a is not None:
                    exponentials(range(6, 7))
                if b is not None:
                    act.wait_ge(fullB[B_GU].sem, fullB[B_GU].of(b))
                    freed(act, ev["sg_ready"], b)
                    act.activation(th[:, :], bankB(B_GU)[:, 0:DIM], ACT.Tanh, scale=0.5).then_inc(ev["th_ready"].sem, 1)
                if a is not None:
                    exponentials(range(7, 8))
                if b is not None:
                    act.wait_ge(fullB[B_ST].sem, fullB[B_ST].of(b))
                    freed(act, fullB[B_Y], b)
                    act.copy(suT[:, :, :].rearrange("p k n -> p (k n)"), bankB(B_ST)[:, 0:DIM]).then_inc(freeB[B_ST].sem, 1)
                if a is not None:
                    act.wait_ge(fullA[A_OT].sem, fullA[A_OT].of(a))
                    freed(act, fullA[A_PROJ], a)
                    act.activation(oT[:, :, :, :].rearrange("p o b n -> p b o n"),
                                   bankA(A_OT)[:, 0:DIM].rearrange("p (b o n) -> p b o n", b=2, o=2), ACT.Copy)\
                        .then_inc(freeA[A_OT].sem, 1)
            tiles(act, step)
            act.wait_ge(routed, 2)
            act.activation(prob, tmp, ACT.Exp).then_inc(exps_ready, 1)
            act.wait_ge(ids_ready, 1)

            def expert(j, c, n):
                def now(lag):
                    i = j - lag
                    return not isinstance(i, int) or 0 <= i < SLOTS, i, (c - lag) % DEEP

                go, i, s = now(0)
                if go:
                    act.wait_ge(ev["rows_turned"].sem, ev["rows_turned"].of(i))
                    ahead(act, ev["gu_ready"], i, 2)
                    act.copy(xgT[:, s % 2, :], bank(s % 2)[:, 0:DIM]).then_inc(ev["rowsT_ready"].sem, 1)
                go, i, s = now(1)
                if go:
                    act.wait_ge(ev["gu_ready"].sem, ev["gu_ready"].of(i))
                    ahead(act, ev["esg_ready"], i, 2)
                    act.activation(eth[:, s % 2, :], bank(2 + s % 2)[:, 0:F], ACT.Tanh, scale=0.5).then_inc(ev["eth_ready"].sem, 1)
                go, i, s = now(2)
                if go:
                    act.wait_ge(ev["esu_turned"].sem, ev["esu_turned"].of(i))
                    ahead(act, ev["y_summed"], i, 2)
                    act.copy(esuT[:, s % 2, :], bank(4 + s % 2)[:, 0:P]).then_inc(ev["esuT_ready"].sem, 1)
            rounds(act, SLOTS, expert, 2)

        @block.gpsimd
        def _(pool):
            pool.wait_ge(weights_set, 1)

            def step(a, b):
                if b is not None:
                    pool.wait_ge(ev["b_veps"].sem, ev["b_veps"].of(b))
                    pool.tensor_tensor(lnB[:, 9:10], lnB[:, 8:9], minushalf[:, :], ALU.pow).then_inc(ev["b_rstd"].sem, 1)
                    freed(pool, x2_ready, b)
                    pool.tensor_tensor(x1b[:, :], x1[:, :], rows[:, 3, :], ALU.add).then_inc(ev["x1b_ready"].sem, 1)
                if a is not None:
                    pool.wait_ge(ev["a_veps"].sem, ev["a_veps"].of(a))
                    pool.tensor_tensor(lnA[:, 9:10], lnA[:, 8:9], minushalf[:, :], ALU.pow).then_inc(ev["a_rstd"].sem, 1)
                    freed(pool, x1_ready, a)
                    pool.tensor_tensor(xres[:, :], xt[:, :], rows[:, 2, :], ALU.add).then_inc(ev["xres_ready"].sem, 1)
                    pool.wait_ge(ev["newton_y3"].sem, ev["newton_y3"].of(a))
                    freed(pool, fullA[A_KT[1]], a)
                    for jj in range(2):
                        pool.tensor_tensor(kn[:, 2 * jj:2 * jj + 2, :].rearrange("p j (h d) -> p (j h) d", d=HD),
                                           kc[:, 2 * jj:2 * jj + 2, :].rearrange("p j (h d) -> p (j h) d", d=HD),
                                           rr[:, H * (1 + 2 * jj):H * (3 + 2 * jj)].unsqueeze(2).to_broadcast([P, 2 * H, HD]),
                                           ALU.mult).then_inc(ev[("kn01_ready", "kn23_ready")[jj]].sem, 1)
                if b is not None:
                    pool.wait_ge(ev["mx2_ready"].sem, ev["mx2_ready"].of(b))
                    freed(pool, ev["ex_ready"], b)
                    pool.tensor_tensor(sh[:, :, :], sc[:, :, :], mx2[:, :].unsqueeze(2).to_broadcast([P, 2 * HP, N]),
                                       ALU.subtract).then_inc(ev["sh_ready"].sem, 1)
                    pool.wait_ge(ev["rz2_ready"].sem, ev["rz2_ready"].of(b))
                    freed(pool, fullB[B_PT[1]], b)
                    pool.tensor_tensor(pn[:, :, :], ex[:, :, :], rz2[:, :].unsqueeze(2).to_broadcast([P, 2 * HP, N]),
                                       ALU.mult).then_inc(ev["pn_ready"].sem, 1)
                if a is not None:
                    for bb in range(2):
                        pool.wait_ge(mx_ready[bb].sem, mx_ready[bb].of(a))
                        freed(pool, fullA[A_S + 4 * bb + 3], a)
                        pool.tensor_tensor(shift[:, bb, :, :], ident[:, :].unsqueeze(1).to_broadcast([P, HP, P]),
                                           mx[:, bb, :].unsqueeze(2).to_broadcast([P, HP, P]), ALU.mult)\
                            .then_inc(ev[f"shift{bb}_ready"].sem, 1)
                if b is not None:
                    pool.wait_ge(ev["c_veps"].sem, ev["c_veps"].of(b))
                    pool.tensor_tensor(lnC[:, 9:10], lnC[:, 8:9], minushalf[:, :], ALU.pow).then_inc(ev["c_rstd"].sem, 1)
            tiles(pool, step)
            pool.wait_ge(ids_ready, 1)
            pool.wait_ge(h_out, 16 * TILES)

            def gather(j, c, n):
                if not (isinstance(n, int) and n == 0):
                    pool.wait_ge(rows_in[c], 16 * n)
                pool.tensor_copy(now_ids[:, c:c + 1], column(ids, j)).then_inc(ev["ids_copied"].sem, 1)
                pool.wait_ge(ev["ids_copied"].sem, ev["ids_copied"].of(j))
                ahead(pool, ev["rows_turned"], j, DEEP)
                pool.tensor_tensor(idle[:, :], lane_no[:, :], lane_no[:, :], ALU.add)
                pool.indirect_dma_start(out=xg[:, c, :], out_offset=None, in_=rows_d[:, :],
                                        in_offset=bass.IndirectOffsetOnAxis(ap=now_ids[:, c:c + 1], axis=0)).then_inc(rows_in[c], 16)
            rounds(pool, SLOTS, gather)
            for c in range(DEEP):
                pool.wait_ge(y_out[c], 16 * SLOTS // DEEP)

            def gather_y(t, c, n):
                if not (isinstance(n, int) and n == 0):
                    pool.wait_ge(yg_in[c], 32 * n)
                for k in range(2):
                    ins = pool.tensor_copy(now_pos[:, 2 * c + k:2 * c + k + 1], column(pos_u, k * TILES + t))
                ins.then_inc(ev["pos_copied"].sem, 1)
                pool.wait_ge(ev["pos_copied"].sem, ev["pos_copied"].of(t))
                ahead(pool, ev["res_ready"], t, DEEP)
                pool.tensor_tensor(idle[:, :], lane_no[:, :], lane_no[:, :], ALU.add)
                for k in range(2):
                    pool.indirect_dma_start(out=yg[:, c, k, :], out_offset=None, in_=y_d[:, :],
                                            in_offset=bass.IndirectOffsetOnAxis(ap=now_pos[:, 2 * c + k:2 * c + k + 1], axis=0))\
                        .then_inc(yg_in[c], 16)
            rounds(pool, TILES, gather_y)

        @block.vector
        def _(dve):
            dve.memset(negones[:, :], -1.0)
            dve.memset(minushalf[:, :], -0.5)
            dve.memset(ones[:, :], 1.0)
            dve.memset(va[:, :, :, :], 1.0)
            dve.memset(v2[:, :, :, :], 0.0)
            dve.wait_ge(weights_in, 16 * 25)
            dve.tensor_copy(bcol[:, :, :], cols[:, 9:13].unsqueeze(2).to_broadcast([P, 4, P])).then_inc(setup_dve, 1)
            dve.tensor_reduce(wmean[:, :, 0:H], wx_q[:, :, :].rearrange("p k (h d) -> p k h d", d=HD), AX.X, ALU.add)
            dve.tensor_reduce(wmean[:, :, H:2 * H], wx_kv[:, :, 0:DIM].rearrange("p k (h d) -> p k h d", d=HD), AX.X, ALU.add)
            dve.tensor_reduce(wmean[:, :, 2 * H:3 * H], rows[:, 0:2, :].rearrange("p k (h d) -> p k h d", d=HD), AX.X, ALU.add)\
                .then_inc(setup_dve, 1)
            dve.wait_ge(setup_dve, 2)
            dve.tensor_scalar(wmean[:, :, :], wmean[:, :, :], -1.0 / HD, None, ALU.mult).then_inc(setup_dve, 1)
            dve.wait_ge(setup_dve, 3)
            for k in range(KD):
                for n, t in enumerate((wx_q[:, k, :], wx_kv[:, k, 0:DIM], rows[:, k, :])):
                    tv = t.rearrange("p (h d) -> p h d", d=HD)
                    dve.tensor_tensor(tv, tv, wmean[:, k, n * H:(n + 1) * H].unsqueeze(2).to_broadcast([P, H, HD]), ALU.add)
            dve.tensor_scalar(cols[:, 0:2], cols[:, 0:2], HD ** -0.5, None, ALU.mult)
            dve.tensor_scalar(cols[:, 13:15], cols[:, 4:6], HD ** -0.5, None, ALU.mult)
            dve.tensor_scalar(jmix[:, :, :], jmix[:, :, :], cols[:, 8:9], None, ALU.mult)
            dve.tensor_scalar(ws_down[:, :, :], ws_down[:, :, :], 0.5, None, ALU.mult)
            dve.tensor_scalar(w_down[:, :, :], w_down[:, :, :], 0.5, None, ALU.mult)
            dve.wait_ge(setup_pe, 1)
            dve.tensor_tensor(rows[:, 2:4, :], ringA[:, 0:2, 0:DIM], rows[:, 2:4, :], ALU.add).then_inc(weights_set, 1)
            dve.wait_ge(weights_set, 1)

            def normalise(t, ln, src, dst, pre, done):
                dve.bn_stats(ln[:, 0:6], src[:, :]).then_inc(ev[pre + "_stats"].sem, 1)
                dve.wait_ge(ev[pre + "_stats"].sem, ev[pre + "_stats"].of(t))
                dve.memset(ln[:, 15:16], 0.0)
                dve.bn_aggr(ln[:, 6:8], ln[:, 0:6]).then_inc(ev[pre + "_meanvar"].sem, 1)
                dve.wait_ge(ev[pre + "_meanvar"].sem, ev[pre + "_meanvar"].of(t))
                dve.tensor_scalar(ln[:, 8:9], ln[:, 7:8], EPS, None, ALU.add).then_inc(ev[pre + "_veps"].sem, 1)

            def normalised(t, ln, src, dst, pre, done):
                dve.wait_ge(ev[pre + "_rstd"].sem, ev[pre + "_rstd"].of(t))
                dve.tensor_scalar(dst[:, :], src[:, :], ln[:, 6:7], ln[:, 9:10], ALU.subtract, ALU.mult).then_inc(ev[done].sem, 1)

            def keys(a, jj):
                u = A_K[jj]
                dve.wait_ge(fullA[u].sem, fullA[u].of(a))
                if jj == 0:
                    freed(dve, ev["kn23_ready"], a)
                dve.tensor_tensor(kc[:, 2 * jj:2 * jj + 2, :], bankA(u).rearrange("p (j n) -> p j n", j=2),
                                  rows[:, 1, :].unsqueeze(1).to_broadcast([P, 2, DIM]), ALU.add).then_inc(freeA[u].sem, 1)

            def sums(a, jj):
                dve.wait_ge(ev[("k_sq01", "k_sq23")[jj]].sem, ev[("k_sq01", "k_sq23")[jj]].of(a))
                dve.tensor_reduce(ss[:, H * (1 + 2 * jj):H * (3 + 2 * jj)],
                                  ksq[:, 2 * jj:2 * jj + 2, :].rearrange("p j (h d) -> p (j h) d", d=HD), AX.X, ALU.add)\
                    .then_inc(ev[("k_sum01", "k_sum23")[jj]].sem, 1)

            def inverse_sigmas(a):
                for s in ("q_sum", "k_sum23"):
                    dve.wait_ge(ev[s].sem, ev[s].of(a))
                dve.tensor_scalar(ss[:, :], ss[:, :], 1.0 / HD, EPS, ALU.mult, ALU.add).then_inc(ev["s_eps"].sem, 1)
                dve.wait_ge(ev["s_eps"].sem, ev["s_eps"].of(a))
                dve.tensor_scalar(nt[:, :].bitcast(I32), ss[:, :].bitcast(I32), 1, None, ALU.arith_shift_right)\
                    .then_inc(ev["s_shift"].sem, 1)
                dve.wait_ge(ev["s_shift"].sem, ev["s_shift"].of(a))
                freed(dve, ev["kn23_ready"], a)
                freed(dve, ev["qn_ready"], a)
                dve.tensor_scalar(rr[:, :].bitcast(I32), nt[:, :].bitcast(I32), -1.0, MAGIC, ALU.mult, ALU.add)\
                    .then_inc(ev["newton_y0"].sem, 1)
                for n in range(3):
                    dve.wait_ge(ev[f"newton_y{n}"].sem, ev[f"newton_y{n}"].of(a))
                    dve.scalar_tensor_tensor(nt[:, :], rr[:, :], -0.5, rr[:, :], ALU.mult, ALU.mult).then_inc(ev[f"newton_t{n}"].sem, 1)
                    dve.wait_ge(ev[f"newton_t{n}"].sem, ev[f"newton_t{n}"].of(a))
                    dve.tensor_tensor(nt[:, :], nt[:, :], ss[:, :], ALU.mult).then_inc(ev[f"newton_u{n}"].sem, 1)
                    dve.wait_ge(ev[f"newton_u{n}"].sem, ev[f"newton_u{n}"].of(a))
                    dve.scalar_tensor_tensor(rr[:, :], nt[:, :], 1.5, rr[:, :], ALU.add, ALU.mult).then_inc(ev[f"newton_y{n + 1}"].sem, 1)

            def blocks(dst, src):
                return dict(out=dst, in0=src.unsqueeze(2).to_broadcast([P, 2, HG, N]),
                            in1=headmask[:, :].unsqueeze(1).unsqueeze(3).to_broadcast([P, 2, HG, N]), op=ALU.mult)

            def step(a, b):
                if b is not None:
                    dve.wait_ge(x1_ready.sem, x1_ready.of(b))
                    normalise(b, lnB, x1, x1n, "b", "x1n_ready")
                if a is not None:
                    dve.wait_ge(x_in, a * 16 + 16)
                    normalise(a, lnA, xt, xn, "a", "xn_ready")
                if b is not None:
                    freed(dve, fullB[B_XT], b)
                    normalised(b, lnB, x1, x1n, "b", "x1n_ready")
                if a is not None:
                    freed(dve, fullA[A_XT], a)
                    normalised(a, lnA, xt, xn, "a", "xn_ready")
                    keys(a, 0)
                    sums(a, 0)
                    keys(a, 1)
                    sums(a, 1)
                if b is not None:
                    dve.wait_ge(ev["qq_ready"].sem, ev["qq_ready"].of(b))
                    freed(dve, fullB[B_S[1]], b)
                    for g in range(G):
                        ins = dve.tensor_tensor(**blocks(bd[:, 0, g, :, :, :], qkT[:, 0, g, :].rearrange("p (b n) -> p b n", b=2)))
                    ins.then_inc(ev["bdq_ready"].sem, 1)
                    dve.wait_ge(fullB[B_QJ].sem, fullB[B_QJ].of(b))
                    for g in range(G):
                        ins = dve.tensor_tensor(**blocks(bd[:, 1, g, :, :, :], bankB(B_QJ)[:, g * P:(g + 1) * P].rearrange("p (b n) -> p b n", b=2)))
                    ins.then_inc(bdt_ready.sem, 1)
                if a is not None:
                    dve.wait_ge(fullA[A_Q].sem, fullA[A_Q].of(a))
                    dve.tensor_tensor(qc[:, :], bankA(A_Q)[:, 0:DIM], rows[:, 0, :], ALU.add).then_inc(freeA[A_Q].sem, 1)
                    dve.wait_ge(ev["q_sq"].sem, ev["q_sq"].of(a))
                    dve.tensor_reduce(ss[:, 0:H], qsq[:, :].rearrange("p (h d) -> p h d", d=HD), AX.X, ALU.add).then_inc(ev["q_sum"].sem, 1)
                    inverse_sigmas(a)
                    dve.wait_ge(ev["newton_y3"].sem, ev["newton_y3"].of(a))
                    freed(dve, fullA[A_QT], a)
                    dve.tensor_tensor(qn[:, :].rearrange("p (h d) -> p h d", d=HD), qc[:, :].rearrange("p (h d) -> p h d", d=HD),
                                      rr[:, 0:H].unsqueeze(2).to_broadcast([P, H, HD]), ALU.mult).then_inc(ev["qn_ready"].sem, 1)
                if b is not None:
                    for g in range(G):
                        dve.wait_ge(fullB[B_S[g]].sem, fullB[B_S[g]].of(b))
                        if g == 0:
                            freed(dve, ev["sh_ready"], b)
                        dve.scalar_tensor_tensor(sc[:, 8 * g:8 * g + 8, :], bankB(B_S[g]).rearrange("p (a n) -> p a n", n=N), 1.0,
                                                 causal[:, :].unsqueeze(1).to_broadcast([P, 8, N]), ALU.mult, ALU.add)\
                            .then_inc(freeB[B_S[g]].sem, 1)
                    for g in range(G):
                        dve.wait_ge(freeB[B_S[g]].sem, freeB[B_S[g]].of(b))
                    dve.tensor_reduce(mx2[:, :], sc[:, :, :], AX.X, ALU.max).then_inc(ev["mx2_ready"].sem, 1)
                if a is not None:
                    for g in range(G):
                        dve.wait_ge(freeA[A_KT[g]].sem, freeA[A_KT[g]].of(a))
                    freed(dve, fullA[A_MAX + 7], a)
                    dve.tensor_copy(kTb[:, :, :], kT[:, :, :]).then_inc(ev["kTb_ready"].sem, 1)
                    dve.wait_ge(freeA[A_QT].sem, freeA[A_QT].of(a))
                    freed(dve, fullA[A_S + 7], a)
                    for g in range(G):
                        dve.tensor_tensor(**blocks(qbd[:, g, :, :, :], qT[:, g, :].rearrange("p (b n) -> p b n", b=2)))\
                            .then_inc(ev[f"qbd{g}_ready"].sem, 1)
                    dve.wait_ge(ev["qbd1_ready"].sem, ev["qbd1_ready"].of(a))
                    dve.tensor_copy(qbdb[:, :, :, :, :], qbd[:, :, :, :, :]).then_inc(ev["qbdb_ready"].sem, 1)
                if b is not None:
                    dve.wait_ge(ev["ex_ready"].sem, ev["ex_ready"].of(b))
                    dve.tensor_reduce(z2[:, :], ex[:, :, :], AX.X, ALU.add).then_inc(ev["z2_ready"].sem, 1)
                    dve.wait_ge(ev["z2_ready"].sem, ev["z2_ready"].of(b))
                    freed(dve, ev["pn_ready"], b)
                    dve.reciprocal(rz2[:, :], z2[:, :]).then_inc(ev["rz2_ready"].sem, 1)
                if a is not None:
                    for r in range(8):
                        bb = r // 4
                        u = A_MAX + r
                        dve.wait_ge(fullA[u].sem, fullA[u].of(a))
                        if r % 4 == 0:
                            freed(dve, ev[f"shift{bb}_ready"], a)
                        dve.tensor_reduce(mx[:, bb, 2 * (r % 4):2 * (r % 4) + 2], bankA(u).rearrange("p (c m) -> p c m", c=2),
                                          AX.X, ALU.max).then_inc(freeA[u].sem, 1)
                if b is not None:
                    dve.wait_ge(fullB[B_WO].sem, fullB[B_WO].of(b))
                    dve.wait_ge(ev["x1b_ready"].sem, ev["x1b_ready"].of(b))
                    freed(dve, freeB[B_Y], b)
                    dve.tensor_tensor(x2[:, :], bankB(B_WO)[:, 0:DIM], x1b[:, :], ALU.add).then_inc(x2_ready.sem, 1)
                    dve.wait_ge(x2_ready.sem, x2_ready.of(b))
                    normalise(b, lnC, x2, h, "c", "h_ready")

                def heads_out(bb):
                    oo = oA[:, 0:HP * 34].rearrange("p (a e) -> p a e", e=34)
                    dve.wait_ge(ev[f"pv{2 * bb + 1}"].sem, ev[f"pv{2 * bb + 1}"].of(a))
                    dve.reciprocal(rz[:, bb, :], oo[:, :, 32]).then_inc(ev[f"rz{bb}"].sem, 1)
                    dve.wait_ge(ev[f"rz{bb}"].sem, ev[f"rz{bb}"].of(a))
                    freed(dve, fullA[A_OT], a)
                    for odd in range(2):
                        lo = odd * N
                        dve.tensor_tensor(on[lo:lo + N, bb, :, :], oo[lo:lo + N, :, odd * HD:(odd + 1) * HD],
                                          rz[lo:lo + N, bb, :].unsqueeze(2).to_broadcast([N, HP, HD]), ALU.mult)\
                            .then_inc(ev[(f"onlo{bb}", f"on{bb}_ready")[odd]].sem, 1)
                if b is not None:
                    freed(dve, fullB[B_HT], b)
                    if not isinstance(b, int) or b > 0:
                        dve.wait_ge(h_out, 16 * b)
                    normalised(b, lnC, x2, h, "c", "h_ready")
                if a is not None:
                    heads_out(0)
                if b is not None:
                    dve.wait_ge(fullB[B_ROUTE].sem, fullB[B_ROUTE].of(b))
                    dve.tensor_copy(row(logits, b), bankB(B_ROUTE)[:, 0:E]).then_inc(freeB[B_ROUTE].sem, 1)
                    dve.wait_ge(ev["th_ready"].sem, ev["th_ready"].of(b))
                    dve.scalar_tensor_tensor(sg[:, :], th[:, :], 1.0, bankB(B_GU)[:, 0:DIM], ALU.add, ALU.mult).then_inc(ev["sg_ready"].sem, 1)
                    dve.wait_ge(ev["sg_ready"].sem, ev["sg_ready"].of(b))
                    freed(dve, fullB[B_ST], b)
                    dve.tensor_tensor(su[:, :], sg[:, :], bankB(B_GU)[:, DIM:2 * DIM], ALU.mult).then_inc(su_ready.sem, 1)
                if a is not None:
                    heads_out(1)
                if b is not None:
                    dve.wait_ge(fullB[B_Y].sem, fullB[B_Y].of(b))
                    if not isinstance(b, int) or b > 0:
                        dve.wait_ge(base_out, 16 * b)
                    dve.tensor_tensor(base[:, :], bankB(B_Y)[:, 0:DIM], x2[:, :], ALU.add).then_inc(freeB[B_Y].sem, 1)
                if a is not None:
                    dve.wait_ge(fullA[A_PROJ].sem, fullA[A_PROJ].of(a))
                    dve.wait_ge(ev["xres_ready"].sem, ev["xres_ready"].of(a))
                    freed(dve, ev["x1b_ready"], a)
                    freed(dve, ev["x1n_ready"], a)
                    dve.tensor_tensor(x1[:, :], bankA(A_PROJ)[:, 0:DIM], xres[:, :], ALU.add).then_inc(x1_ready.sem, 1)
            tiles(dve, step)

            steps = [0]

            def link(ins):
                steps[0] += 1
                ins.then_inc(routed, 1)
                dve.wait_ge(routed, steps[0])

            def te(v):
                return v.rearrange("p (t e) -> p t e", e=E)

            def by_tile(v):
                return v.unsqueeze(2).to_broadcast([P, TILES, E])

            reverse = numbers[:, 0:E]
            lane = numbers[:, E:E + P]
            slot_tile = numbers[:, E + P:E + P + SLOTS]
            slot_start = numbers[:, E + P + SLOTS:E + P + 2 * SLOTS]
            tile_no = numbers[:, E + P + 2 * SLOTS:E + P + 2 * SLOTS + TILES]
            reversed_ = reverse.unsqueeze(1).to_broadcast([P, TILES, E])
            top, total, inv, m1, r1, m2, r2 = (most[:, k, :] for k in range(7))
            link(dve.tensor_reduce(top, logits[:, :, :], AX.X, ALU.max))
            link(dve.tensor_tensor(te(tmp), logits[:, :, :], by_tile(top), ALU.subtract))
            dve.wait_ge(exps_ready, 1)
            link(dve.tensor_reduce(total, te(prob), AX.X, ALU.add))
            link(dve.reciprocal(inv, total))
            link(dve.tensor_reduce(m1, te(prob), AX.X, ALU.max))
            link(dve.tensor_tensor(te(tmp), te(prob), by_tile(m1), ALU.is_equal))
            link(dve.tensor_tensor(te(tmp), te(tmp), reversed_, ALU.mult))
            link(dve.tensor_reduce(r1, te(tmp), AX.X, ALU.max))
            link(dve.tensor_tensor(te(first), reversed_, by_tile(r1), ALU.is_equal))
            link(dve.scalar_tensor_tensor(tmp, first, -2.0, prob, ALU.mult, ALU.add))
            link(dve.tensor_reduce(m2, te(tmp), AX.X, ALU.max))
            link(dve.tensor_tensor(te(tmp2), te(tmp), by_tile(m2), ALU.is_equal))
            link(dve.tensor_tensor(te(tmp2), te(tmp2), reversed_, ALU.mult))
            link(dve.tensor_reduce(r2, te(tmp2), AX.X, ALU.max))
            link(dve.tensor_tensor(te(second), reversed_, by_tile(r2), ALU.is_equal))
            dve.tensor_tensor(sel, first, second, ALU.add).then_inc(sel_ready, 1)
            link(dve.tensor_tensor(coef[:, 0, :], m1, inv, ALU.mult))
            link(dve.tensor_tensor(coef[:, 1, :], m2, inv, ALU.mult))
            link(dve.memset(carry[:, :], 1.0))
            link(dve.memset(carry[:, :].rearrange("p (e t) -> p e t", e=E)[:, :, 0], 0.0))
            dve.wait_ge(counted, 1)
            link(dve.tensor_copy(cnt.rearrange("p (e t) -> p e t", e=E), bank(1)[:, 0:TILES * E].rearrange("p (t e) -> p e t", e=E)))
            link(dve.tensor_tensor_scan(incl, carry[:, :], cnt, 0.0, ALU.mult, ALU.add))
            filled, start, end, _, _ = (per_expert[:, k, :] for k in range(5))
            link(dve.tensor_scalar(per_int[:, 0, :], incl.rearrange("p (e t) -> p e t", e=E)[:, :, TILES - 1], P - 1.0, None, ALU.add))
            link(dve.tensor_scalar(per_int[:, 1, :], per_int[:, 0, :], 7, 7, ALU.logical_shift_right, ALU.logical_shift_left))
            link(dve.tensor_copy(filled, per_int[:, 1, :]))
            link(dve.tensor_tensor_scan(end, ones[:, 0:E], filled, 0.0, ALU.mult, ALU.add))
            link(dve.tensor_tensor(start, end, filled, ALU.subtract))
            link(dve.tensor_tensor(incl, incl, cnt, ALU.subtract))
            et = lambda v: v.rearrange("p (e t) -> p e t", e=E)
            link(dve.tensor_tensor(et(incl), et(incl), start.unsqueeze(2).to_broadcast([P, E, TILES]), ALU.add))
            link(dve.tensor_tensor(te(cnt), te(bank(0)[:, 0:TILES * E]), incl.rearrange("p (e t) -> p t e", e=E), ALU.add))
            for k, hot in enumerate((first, second)):
                link(dve.tensor_tensor(tmp, hot, cnt, ALU.mult))
                link(dve.tensor_reduce(pos[:, k, :], te(tmp), AX.X, ALU.add))
            link(dve.tensor_copy(pos_i[:, 0, :, :], pos[:, :, :]))
            link(dve.tensor_copy(pos_u[:, :], pos[:, :, :].rearrange("p k t -> p (k t)")))
            link(dve.tensor_scalar(pos_i[:, 1, :, :], pos_i[:, 0, :, :], P - 1, None, ALU.bitwise_and))
            link(dve.tensor_copy(in_tile[:, :, :], pos_i[:, 1, :, :]))
            link(dve.tensor_scalar(pos_i[:, 1, :, :], pos_i[:, 0, :, :], 7, None, ALU.logical_shift_right))
            link(dve.tensor_copy(of_tile[:, :, :], pos_i[:, 1, :, :]))
            for lo in range(0, SLOTS, SLOTS // 2):
                hi = lo + SLOTS // 2
                over = past[0:1, 0:(SLOTS // 2) * E].rearrange("p (j e) -> p j e", e=E)
                link(dve.tensor_tensor(over, end[0:1, :].unsqueeze(1).to_broadcast([1, SLOTS // 2, E]),
                                       slot_start[0:1, lo:hi].unsqueeze(2).to_broadcast([1, SLOTS // 2, E]), ALU.is_le))
                link(dve.tensor_reduce(weights_at[0:1, lo:hi], over, AX.X, ALU.add))
            link(dve.tensor_scalar(weights_at_i[0:1, :], weights_at[0:1, :], E - 1.0, float(DIM), ALU.min, ALU.mult))
            dve.memset(xgT[:, 0, 0:1], 0.0).then_inc(positions_ready, 1)

            def hots(t, c, n):
                if not isinstance(t, int) or t >= 2:
                    dve.wait_ge(ev["hot_used"].sem, ev["hot_used"].of(t - 2))
                for k in range(2):
                    q = 2 * (c % 2) + k
                    dve.tensor_scalar(at_slot[:, q, :], lane, column(in_tile[:, k, :], t), None, ALU.is_equal)
                    dve.tensor_scalar(at_column[:, q, 0:SLOTS], slot_tile, column(of_tile[:, k, :], t), lane_no[:, :],
                                      ALU.is_equal, ALU.mult)
                    ins = dve.tensor_scalar(at_column[:, q, SLOTS:2 * SLOTS], slot_tile, column(of_tile[:, k, :], t),
                                            column(tile_no, t), ALU.is_equal, ALU.mult)
                ins.then_inc(ev["hot_ready"].sem, 1)
            rounds(dve, TILES, hots)
            dve.wait_ge(ids_summed, 1)
            link(dve.tensor_copy(ids_f[:, :], bank(2)[:, 0:2 * SLOTS]))
            dve.scalar_tensor_tensor(ids[:, :], ids_f[:, SLOTS:2 * SLOTS], float(P), ids_f[:, 0:SLOTS], ALU.mult, ALU.add)\
                .then_inc(ids_ready, 1)

            def expert(j, c, n):
                def now(lag):
                    i = j - lag
                    return not isinstance(i, int) or 0 <= i < SLOTS, i, (c - lag) % DEEP

                go, i, s = now(1)
                if go:
                    gate, up = bank(2 + s % 2)[:, 0:F], bank(2 + s % 2)[:, F:2 * F]
                    dve.wait_ge(ev["eth_ready"].sem, ev["eth_ready"].of(i))
                    dve.scalar_tensor_tensor(esg[:, s % 2, :], eth[:, s % 2, :], 1.0, gate, ALU.add, ALU.mult)\
                        .then_inc(ev["esg_ready"].sem, 1)
                    dve.wait_ge(ev["esg_ready"].sem, ev["esg_ready"].of(i))
                    ahead(dve, ev["esu_turned"], i, 2)
                    dve.tensor_tensor(esu[:, s % 2, :], esg[:, s % 2, :], up, ALU.mult).then_inc(ev["esu_ready"].sem, 1)
                go, i, s = now(3)
                if go:
                    dve.wait_ge(ev["y_summed"].sem, ev["y_summed"].of(i))
                    turn_no = n - 1 if c < 3 else n
                    if not isinstance(turn_no, int) or turn_no > 0:
                        dve.wait_ge(y_out[s], 16 * turn_no)
                    dve.tensor_copy(y[:, s, :], bank(6 + s % 2)[:, 0:DIM]).then_inc(ev["y_ready"].sem, 1)
            rounds(dve, SLOTS, expert, 3)

            def combine(t, c, n):
                dve.wait_ge(base_in[c], 16 * n + 16)
                dve.wait_ge(yg_in[c], 32 * n + 32)
                if not (isinstance(n, int) and n == 0):
                    dve.wait_ge(out_done[c], 16 * n)
                dve.scalar_tensor_tensor(res[:, c, :], yg[:, c, 0, :], column(coef[:, 0, :], t), base4[:, c, :], ALU.mult, ALU.add)\
                    .then_inc(ev["half_summed"].sem, 1)
                dve.wait_ge(ev["half_summed"].sem, ev["half_summed"].of(t))
                dve.scalar_tensor_tensor(res[:, c, :], yg[:, c, 1, :], column(coef[:, 1, :], t), res[:, c, :], ALU.mult, ALU.add)\
                    .then_inc(ev["res_ready"].sem, 1)
            rounds(dve, TILES, combine)


def laid_out(a):
    def t(m):
        return np.ascontiguousarray(m.T)

    def col(v):
        return v.reshape(-1, P).T

    def per_head(v):
        return np.tile(v, HG).reshape(P, 1)

    f32 = np.float32
    kv, wo, bkv = a["L0_xattn_Wkv"], a["L0_xattn_Wproj"], a["L0_xattn_bkv"]
    pairs = lambda v: v.reshape(HP, 2, HD, -1).transpose(0, 2, 1, 3).reshape(P, 2, -1)
    jmix = np.zeros((G, HG, HD, HG, HD), f32)
    for n in range(HG):
        jmix[:, n, :, n, :] = a["L0_attn_J_attn"].reshape(G, HG, HD, HD)[:, n]
    q = np.arange(N)
    d = {
        "x": a["x"].reshape(TOK, DIM),
        "ctxT": np.ascontiguousarray(a["ctx_1024"].transpose(0, 2, 1)),
        "wx_q": t(a["L0_xattn_Wq"]), "wx_kv": t(kv), "wx_o": np.ascontiguousarray(pairs(wo.T)),
        "wa_q": t(a["L0_attn_Wq"]), "wa_k": t(a["L0_attn_Wk"]), "wa_v": t(a["L0_attn_Wv"]), "wa_o": t(a["L0_attn_Wo"]),
        "jmix": np.ascontiguousarray(jmix.reshape(G, P, P).transpose(1, 0, 2)),
        "w_route": a["L0_ffn_router_w"],
        "ws_gate": a["L0_ffn_shared_gate_w"], "ws_up": a["L0_ffn_shared_up_w"], "ws_down": a["L0_ffn_shared_down_w"],
        "cols": np.ascontiguousarray(np.concatenate(
            [per_head(a["L0_xattn_q_gamma"]), per_head(a["L0_xattn_q_beta"]),
             per_head(a["L0_xattn_k_gamma"]), per_head(a["L0_xattn_k_beta"]),
             col(a["L0_attn_bq"]), col(a["L0_attn_bk"]), np.tile(a["L0_attn_lambda_attn"].reshape(1, 1), (P, 1)),
             pairs(bkv[DIM:])[:, :, 0], col(a["L0_attn_bv"]), np.zeros((P, 2), f32)], axis=1)),
        "rows": np.ascontiguousarray(np.stack([a["L0_xattn_bq"], bkv[:DIM], a["L0_xattn_bproj"], a["L0_attn_bo"]])),
        "e_gate": a["L0_ffn_gate_w"], "e_up": a["L0_ffn_up_w"], "e_down": a["L0_ffn_down_w"],
        "before": np.triu(np.ones((P, P), f32), 1),
        "numbers": np.concatenate([E - np.arange(E), np.arange(P), np.arange(SLOTS), P * np.arange(SLOTS),
                                   np.arange(TILES)]).astype(f32),
        "lane_no": np.arange(P, dtype=f32).reshape(P, 1),
        "ident": np.eye(P, dtype=f32),
        "headmask": (np.arange(P)[:, None] // HD == np.arange(HG)[None]).astype(f32),
        "causal": np.tile(np.where(q[None] > q[:, None], MASKED, 0).astype(f32), (2, 1)),
    }
    return {n: np.ascontiguousarray(v) for n, v in d.items()}


def kernel(**inputs):
    import numpy as _np
    import concourse.bacc as _bacc
    from concourse import mybir as _mybir
    from concourse.bass_utils import run_bass_kernel_spmd as _run

    nc = _bacc.Bacc("TRN2", target_bir_lowering=False, num_devices=1)
    arrays = laid_out({n: _np.asarray(a) for n, a in inputs.items()})
    aps = {n: nc.dram_tensor(f"in_{n}", a.shape, _mybir.dt.from_np(a.dtype), kind="ExternalInput").ap() for n, a in arrays.items()}
    out = nc.dram_tensor("out", (TOK, DIM), F32, kind="ExternalOutput").ap()
    perceiver_block(nc, aps, out)
    r = _run(nc, [{f"in_{n}": a for n, a in arrays.items()}], core_ids=[0])
    return r.results[0]["out"].reshape(B, N, DIM)
```

```python
from contextlib import ExitStack

import numpy as np

import concourse.bass as bass
from concourse import mybir

ALU = mybir.AluOpType
ACT = mybir.ActivationFunctionType
AX = mybir.AxisListType
F32 = mybir.dt.float32
BF16 = mybir.dt.bfloat16
I32 = mybir.dt.int32
U32 = mybir.dt.uint32

P = 128
DIM = 256
H, HD = 16, 16
B, N, M = 64, 64, 256
TOK = B * N
TILES = TOK // P
KD = DIM // P
HG = P // HD
G = H // HG
QG = 4
HP = H // 2
E, F = 16, 128
PAIRS = 2 * TOK
SLOTS = PAIRS // P + E
DEEP = 4
EPS = 1e-5
MASKED = -1e30
MAGIC = 1597463007.0

C_XT, C_Q = 1, 2
C_K, C_V = (0, 3), (4, 5)
C_USES, C_BANKS = 6, 2
A_KT, A_QT = (0, 1), 2
A_MAX = 3
A_S = 11
A_OT = 19
A_USES, A_BANKS = 20, 2
B_XT, B_QK, B_V, B_QJ = 0, 1, 2, 3
B_S, B_PT, B_O = (4, 5), (6, 7), (8, 9)
B_WO, B_HT, B_GU, B_ST, B_Y = 10, 11, 12, 13, 14
B_USES, B_BANKS = 15, 3


class Event:

    def __init__(self, sem, k=1, per=1):
        self.sem, self.k, self.per = sem, k, per

    def of(self, tile):
        return tile * self.per + self.k


def freed(eng, event, tile, buffers=1):
    if not isinstance(tile, int) or tile >= buffers:
        eng.wait_ge(event.sem, tile * event.per + (event.k - buffers * event.per))


def ahead(eng, event, j, lag):
    if not isinstance(j, int) or j >= lag:
        eng.wait_ge(event.sem, event.of(j - lag))


def column(t, j):
    return t[:, j:j + 1] if isinstance(j, int) else t[:, bass.ds(j, 1)]


def row(t, j):
    return t[:, j, :] if isinstance(j, int) else t[:, bass.ds(j, 1), :].rearrange("p o m -> p (o m)")


def block_of(t, j):
    return t[j] if isinstance(j, int) else t[bass.ds(j, 1), :, :].rearrange("o p m -> p (o m)")


def perceiver_block(nc, w, out):
    x, ctxT = w["x"], w["ctxT"]
    with ExitStack() as ctx:
        def sb(name, shape, dt=F32):
            return ctx.enter_context(nc.sbuf_tensor(name, shape, dt))

        def sem(name):
            return ctx.enter_context(nc.semaphore(name))

        wx_q = sb("wx_q", [P, KD, DIM])
        wx_kv = sb("wx_kv", [P, KD, 2 * DIM])
        wx_o = sb("wx_o", [P, 2, DIM])
        wa = {n: sb("wa_" + n, [P, KD, DIM]) for n in "qkvo"}
        jmix = sb("jmix", [P, QG, P])
        w_route = sb("w_route", [P, KD, E])
        ws_gu = sb("ws_gu", [P, KD, 2 * DIM])
        ws_down = sb("ws_down", [P, KD, DIM])
        cols = sb("cols", [P, 15])
        rows = sb("rows", [P, 4, DIM])
        ident = sb("ident", [P, P])
        headmask = sb("headmask", [P, HG])
        quadmask = sb("quadmask", [P, H // QG])
        causal = sb("causal", [P, N])
        negones = sb("negones", [P, P], BF16)
        minushalf = sb("minushalf", [P, 1])
        before = sb("before", [P, P])
        ones = sb("ones", [P, P])
        numbers = sb("numbers", [P, E + P + 2 * SLOTS + TILES])
        lane_no = sb("lane_no", [P, 1])
        idle = sb("idle", [P, 1])
        w_gu = sb("w_gu", [P, KD, E, 2 * F])
        w_down = sb("w_down", [P, E, DIM])
        bcol = sb("bcol", [P, 4, P])
        wmean = sb("wmean", [P, KD, 3 * H])

        xt = sb("xt", [P, DIM])
        ct = sb("ct", [P, 2, KD, 2, M])
        lnA = sb("lnA", [P, 16])
        xn = sb("xn", [P, DIM])
        xres = sb("xres", [P, 2, DIM])
        xnT = sb("xnT", [P, KD, P])
        qc = sb("qc", [P, DIM])
        qsq = sb("qsq", [P, DIM])
        kc = sb("kc", [P, 4, DIM])
        ksq = sb("ksq", [P, 4, DIM])
        va = sb("va", [P, 4, HP, 34])
        ss = sb("ss", [P, 5 * H])
        rr = sb("rr", [P, 5 * H])
        nt = sb("nt", [P, 5 * H])
        qn = sb("qn", [P, DIM])
        kn = ksq
        kT = sb("kT", [P, G, 2 * M])
        kTb = sb("kTb", [P, G, 2 * M], BF16)
        qT = sb("qT", [P, G, P])
        qbd = sb("qbd", [P, G, 2, HG, N])
        qbdb = sb("qbdb", [P, G, 2, HG, N], BF16)
        mx = sb("mx", [P, 2, HP])
        shift = sb("shift", [P, 2, HP, P], BF16)
        pt = sb("pt", [P, 2, 2, HG * N])
        rz = sb("rz", [P, 2, HP])
        on = sb("on", [P, 2, HP, HD])
        oT = sb("oT", [P, 2, 2, N])
        x1 = sb("x1", [P, DIM])

        lnB = sb("lnB", [P, 16])
        x1n = sb("x1n", [P, DIM])
        x1b = sb("x1b", [P, DIM])
        x1T = sb("x1T", [P, KD, P])
        qk4 = sb("qk4", [P, 2, QG, P])
        v2 = sb("v2", [P, HP, 2, 2 * HD])
        bd = sb("bd", [P, QG, 2, H // QG, N])
        sc = sb("sc", [P, HP * 2, N])
        sh = sc
        ex = pn = sc
        mx2 = sb("mx2", [P, HP * 2])
        z2 = sb("z2", [P, HP * 2])
        rz2 = sb("rz2", [P, HP * 2])
        pT = sb("pT", [P, HP, P])
        o2T = sb("o2T", [P, G, 2, N])
        x2 = sb("x2", [P, DIM])
        lnC = sb("lnC", [P, 16])
        h = sb("h", [P, DIM])
        hT = sb("hT", [P, KD, P])
        th = sb("th", [P, DIM])
        sg = sb("sg", [P, DIM])
        su = sb("su", [P, DIM])
        suT = sb("suT", [P, KD, P])
        base = sb("base", [P, DIM])
        logits = sb("logits", [P, TILES, E])

        tables = [t.rearrange("p g b h n -> p (g b h n)")[:, k * 512:k * 512 + TILES * E]
                  for t in (bd[:, :, :, :, :], qbd[:, :, :, :, :]) for k in range(4)]
        prob, first, second, tmp, tmp2, sel, cnt, incl = tables
        carry = qk4[:, 1, :, :].rearrange("p g n -> p (g n)")[:, 0:TILES * E]
        most = sb("most", [P, 7, TILES])
        per_expert = sb("per_expert", [P, 5, E])
        per_int = sb("per_int", [P, 2, E], I32)
        pos = sb("pos", [P, 2, TILES])
        pos_i = sb("pos_i", [P, 2, 2, TILES], I32)
        pos_u = sb("pos_u", [P, 2 * TILES], U32)
        in_tile = sb("in_tile", [P, 2, TILES])
        of_tile = sb("of_tile", [P, 2, TILES])
        coef = sb("coef", [P, 2, TILES])
        past = kT[:, :, :].rearrange("p g m -> p (g m)")
        weights_at = sb("weights_at", [P, SLOTS])
        weights_at_i = sb("weights_at_i", [P, SLOTS], I32)
        at_slot = kTb[:, :, :].rearrange("p g m -> p (g m)")[:, 0:4 * P].rearrange("p (q n) -> p q n", q=4)
        at_column = qbdb[:, :, :, :, :].rearrange("p g b h n -> p (g b h n)")[:, 0:4 * 2 * SLOTS].rearrange("p (q n) -> p q n", q=4)
        ids_f = sb("ids_f", [P, 2 * SLOTS])
        ids = sb("ids", [P, SLOTS], U32)
        now_ids = sb("now_ids", [P, DEEP], U32)
        now_pos = sb("now_pos", [P, 2 * DEEP], U32)
        xg = pt[:, :, :, :].rearrange("p a b n -> p (a b n)")[:, 0:DEEP * DIM].rearrange("p (c d) -> p c d", c=DEEP)
        xgT = qk4[:, 0, :, :].rearrange("p (s g) n -> p s (g n)", s=2)
        scratch = sc[:, :, :].rearrange("p a n -> p (a n)").rearrange("p (k c n) -> p k c n", k=4, c=2)
        eth, esg, esu, esuT = (scratch[:, k, :, :] for k in range(4))
        y = kc[:, :, :]
        yg = qbd[:, :, :, :, :].rearrange("p g b h n -> p (g b h n)")[:, 0:DEEP * 2 * DIM].rearrange("p (c k d) -> p c k d", c=DEEP, k=2)
        res = kn[:, :, :]
        base4 = kT[:, :, :].rearrange("p g (c d) -> p (g c) d", d=DIM)
        rows_d = nc.dram_tensor("normalised_rows", (TOK, DIM), F32, kind="Internal").ap()
        base_d = nc.dram_tensor("rows_without_experts", (TOK, DIM), F32, kind="Internal").ap()
        y_d = nc.dram_tensor("expert_rows", (SLOTS * P, DIM), F32, kind="Internal").ap()

        ringC = ctx.enter_context(nc.psum_tensor("ringC", [P, C_BANKS, 512], F32))
        ringA = ctx.enter_context(nc.psum_tensor("ringA", [P, A_BANKS, 512], F32))
        oA = ctx.enter_context(nc.psum_tensor("oA", [P, 512], F32))
        ringB = ctx.enter_context(nc.psum_tensor("ringB", [P, B_BANKS, 512], F32))

        def bankA(u):
            return ringA[:, u % A_BANKS, :]

        def bankC(u):
            return ringC[:, u % C_BANKS, :]

        def bankB(u):
            return ringB[:, u % B_BANKS, :]

        def ring(name, banks, uses):
            full = [sem(f"full{name}{k}") for k in range(banks)]
            free = [sem(f"free{name}{k}") for k in range(banks)]
            return ([Event(full[u % banks], u // banks + 1, uses // banks) for u in range(uses)],
                    [Event(free[u % banks], u // banks + 1, uses // banks) for u in range(uses)])

        fullC, freeC = ring("C", C_BANKS, C_USES)
        fullA, freeA = ring("A", A_BANKS, A_USES)
        fullB, freeB = ring("B", B_BANKS, B_USES)

        def claim(pe, free, banks, u, tile):
            if u >= banks:
                pe.wait_ge(free[u - banks].sem, free[u - banks].of(tile))
            else:
                freed(pe, free[u + len(free) - banks], tile)

        def claimA(pe, u, tile):
            claim(pe, freeA, A_BANKS, u, tile)

        def claimC(pe, u, tile):
            claim(pe, freeC, C_BANKS, u, tile)

        def claimB(pe, u, tile):
            claim(pe, freeB, B_BANKS, u, tile)

        x1_ready, x2_ready, su_ready, qkT_ready = freeA[A_OT], freeB[B_WO], freeB[B_GU], freeB[B_QK]
        bdt_ready, o2T_ready = freeB[B_QJ], freeB[B_O[1]]
        mx_ready = (freeA[A_MAX + 3], freeA[A_MAX + 7])

        weights_in = sem("weights_in")
        weights_set = sem("weights_set")
        setup_dve = sem("setup_dve")
        setup_pe = sem("setup_pe")
        x_in, h_out, base_out = sem("x_in"), sem("h_out"), sem("base_out")
        base_in = [sem(f"base_in{c}") for c in range(DEEP)]
        routed, exps_ready, sel_ready, counted = sem("routed"), sem("exps_ready"), sem("sel_ready"), sem("counted")
        positions_ready, ids_summed, ids_ready = sem("positions_ready"), sem("ids_summed"), sem("ids_ready")
        ranks_read, hots_used_all = sem("ranks_read"), sem("hots_used_all")
        rows_in = [sem(f"rows_in{c}") for c in range(DEEP)]
        y_out = [sem(f"y_out{c}") for c in range(DEEP)]
        yg_in = [sem(f"yg_in{c}") for c in range(DEEP)]
        out_done = [sem(f"out_done{c}") for c in range(DEEP)]
        ctx_in = [[sem(f"ctx_in{s}{k}") for k in range(KD)] for s in range(2)]
        def chain(name, *steps):
            one = sem(name)
            return {n: Event(one, k + 1, len(steps)) for k, n in enumerate(steps)}

        ev = {}
        for ln in "abc":
            ev.update(chain(f"{ln}_norm", f"{ln}_stats", f"{ln}_meanvar", f"{ln}_veps"))
            ev.update(chain(f"{ln}_rstd", f"{ln}_rstd"))
        ev.update(chain("newton", "s_eps", "s_shift", "newton_y0", *(f"newton_{s}" for n in range(3)
                        for s in (f"t{n}", f"u{n}", f"y{n + 1}"))))
        ev.update(chain("k_sq", "k_sq01", "k_sq23"))
        ev.update(chain("k_sum", "k_sum01", "k_sum23"))
        ev.update(chain("kn_ready", "kn01_ready", "kn23_ready"))
        ev.update(chain("qbd_ready", "qbd0_ready", "qbd1_ready"))
        ev.update(chain("shift_ready", "shift0_ready", "shift1_ready"))
        ev.update(chain("pv", "pv0", "pv1", "pv2", "pv3"))
        ev.update(chain("heads_out", "rz0", "onlo0", "on0_ready", "rz1", "onlo1", "on1_ready"))
        ev.update(chain("z2", "z2_ready", "rz2_ready"))
        for n in ("xn_ready xres_ready q_sq q_sum qn_ready kTb_ready qbdb_ready x1n_ready x1b_ready q4_ready"
                  " oT_ready proj_full hT_ready route_full mx2_ready sh_ready ex_ready pn_ready h_ready th_ready sg_ready").split():
            ev.update(chain(n, n))

        for n in ("hot_ready hot_used ids_copied rows_turned rowsT_ready gu_ready eth_ready esg_ready esu_ready"
                  " esu_turned esuT_ready y_summed y_ready pos_copied half_summed res_ready").split():
            ev.update(chain(n, n))

        def bank(k):
            return ringC[:, k, :] if k < 2 else ringA[:, k - 2, :] if k < 4 else oA[:, :] if k == 4 else ringB[:, k - 5, :]

        block = ctx.enter_context(nc.Block())

        def rounds(eng, count, body, drain=0):
            for c in range(DEEP):
                body(c, c, 0)
            with eng.Fori(1, count // DEEP) as n:
                for c in range(DEEP):
                    body(n * DEEP + c, c, n)
            for c in range(drain):
                body(count + c, c, count // DEEP)

        def tiles(eng, step):
            step(0, None, None, 0)
            step(1, 0, None, 1)
            step(2, 1, 0, 0)
            with eng.Fori(1, TILES // 2 - 1) as n:
                for odd in range(2):
                    step(n * 2 + (odd + 1), n * 2 + odd, n * 2 + (odd - 1), 1 - odd)
            step(TILES - 1, TILES - 2, TILES - 3, 1)
            step(None, TILES - 1, TILES - 2, 0)
            step(None, None, TILES - 1, 1)

        x_d = x.rearrange("(t p) d -> t p d", p=P)
        ctx_d = ctxT.rearrange("(t b) (k p) m -> t k p b m", b=2, p=P)

        @block.sync
        def _(sp):
            def load(dst, src):
                sp.dma_start(dst, src).then_inc(weights_in, 16)

            for dst, name in ((wx_q, "wx_q"), (wx_kv, "wx_kv"), (wa["q"], "wa_q"), (wa["k"], "wa_k"),
                              (wa["v"], "wa_v"), (wa["o"], "wa_o"), (w_route, "w_route"),
                              (ws_down, "ws_down")):
                load(dst[:, :, :], w[name].rearrange("(k p) n -> p k n", p=P))
            load(ws_gu[:, :, 0:DIM], w["ws_gate"].rearrange("(k p) n -> p k n", p=P))
            load(ws_gu[:, :, DIM:2 * DIM], w["ws_up"].rearrange("(k p) n -> p k n", p=P))
            load(wx_o[:, :, :], w["wx_o"])
            load(jmix[:, :, :], w["jmix"])
            load(cols[:, :], w["cols"])
            load(rows[:, :, :], w["rows"].partition_broadcast(P))
            load(ident[:, :], w["ident"])
            load(headmask[:, :], w["headmask"])
            load(quadmask[:, :], w["quadmask"])
            load(causal[:, :], w["causal"])
            load(before[:, :], w["before"])
            load(numbers[:, :], w["numbers"].partition_broadcast(P))
            load(lane_no[:, :], w["lane_no"])
            load(w_down[:, :, :], w["e_down"].rearrange("e f d -> f e d"))
            for k in range(KD):
                load(w_gu[:, k, :, 0:F], w["e_gate"][:, k * P:(k + 1) * P, :].rearrange("e p f -> p e f"))
                load(w_gu[:, k, :, F:2 * F], w["e_up"][:, k * P:(k + 1) * P, :].rearrange("e p f -> p e f"))

            def load_tile(c, s):
                freed(sp, fullC[C_V[1]], c, buffers=2)
                for k in range(KD):
                    here = ctx_d[c, k] if isinstance(c, int) else \
                        ctx_d[bass.ds(c, 1), k, :, :, :].rearrange("o p b m -> p (o b) m")
                    sp.dma_start(ct[:, s, k, :, :], here).then_inc(ctx_in[s][k], 16)
                freed(sp, ev["xn_ready"], c)
                freed(sp, ev["xres_ready"], c)
                sp.dma_start(xt[:, :], block_of(x_d, c)).then_inc(x_in, 16)

            def step(c, a, b, s):
                if c is not None and not (isinstance(c, int) and c + 1 >= TILES):
                    load_tile(c + 1, 1 - s)
                if b is not None:
                    sp.wait_ge(ev["h_ready"].sem, ev["h_ready"].of(b))
                    sp.dma_start(block_of(rows_t, b), h[:, :]).then_inc(h_out, 16)
                    sp.wait_ge(freeB[B_Y].sem, freeB[B_Y].of(b))
                    sp.dma_start(block_of(base_t, b), base[:, :]).then_inc(base_out, 16)

            rows_t = rows_d.rearrange("(t p) d -> t p d", p=P)
            base_t = base_d.rearrange("(t p) d -> t p d", p=P)
            y_t = y_d.rearrange("(t p) d -> t p d", p=P)
            out_t = out.rearrange("(t p) d -> t p d", p=P)
            load_tile(0, 0)
            tiles(sp, step)

            def store_y(j, c, n):
                sp.wait_ge(ev["y_ready"].sem, ev["y_ready"].of(j))
                sp.dma_start(block_of(y_t, j), y[:, c, :]).then_inc(y_out[c], 16)
            rounds(sp, SLOTS, store_y)

            def store_out(t, c, n):
                ahead(sp, ev["half_summed"], t, DEEP)
                sp.dma_start(base4[:, c, :], block_of(base_t, t)).then_inc(base_in[c], 16)
                if not isinstance(t, int) or t >= 2:
                    store_last(t - 2, (c - 2) % DEEP, n)

            def store_last(t, c, n):
                sp.wait_ge(ev["res_ready"].sem, ev["res_ready"].of(t))
                sp.dma_start(block_of(out_t, t), res[:, c, :]).then_inc(out_done[c], 16)
            sp.wait_ge(base_out, 16 * TILES)
            rounds(sp, TILES, store_out)
            for t in (TILES - 2, TILES - 1):
                store_last(t, t % DEEP, 0)
            for c in range(DEEP):
                sp.wait_ge(out_done[c], 16 * TILES // DEEP)

        @block.tensor
        def _(pe):
            pe.wait_ge(setup_dve, 1)
            for side, wo in ((0, wx_o), (1, wa["o"])):
                for k in range(2):
                    mm = pe.matmul(ringA[:, side, 0:DIM], bcol[:, 2 * side + k, :], wo[:, k, :], start=(k == 0), stop=(k == 1))
            mm.then_inc(setup_pe, 1)
            pe.wait_ge(weights_set, 1)

            def context_product(c, s, u, jj, part):
                claimC(pe, u, c)
                if u == C_K[0]:
                    for k in range(KD):
                        pe.wait_ge(ctx_in[s][k], c * 8 + 16 - 8 * s)
                for half in range(2):
                    j = 2 * jj + half
                    for k in range(KD):
                        mm = pe.matmul(bankC(u)[:, half * DIM:(half + 1) * DIM],
                                       ct[:, s, k, j // 2, (j % 2) * P:(j % 2 + 1) * P],
                                       wx_kv[:, k, part * DIM:(part + 1) * DIM], start=(k == 0), stop=(k == 1))
                mm.then_inc(fullC[u].sem, 1)

            def turn(claim_, u, bank, full, src, tile):
                claim_(pe, u, tile)
                for k in range(KD):
                    mm = pe.transpose(bank(u)[:, k * P:(k + 1) * P], src[:, k * P:(k + 1) * P], ident[:, :])
                mm.then_inc(full[u].sem, 1)

            def project(claim_, u, bank, full, lhs, rhs, tile, n=DIM):
                claim_(pe, u, tile)
                for k in range(KD):
                    mm = pe.matmul(bank(u)[:, 0:n], lhs(k), rhs[:, k, 0:n], start=(k == 0), stop=(k == 1))
                mm.then_inc(full[u].sem, 1)

            def keys_turned(a):
                for g in range(G):
                    claimA(pe, A_KT[g], a)
                    if g == 0:
                        pe.wait_ge(ev["kn23_ready"].sem, ev["kn23_ready"].of(a))
                    for j in range(4):
                        mm = pe.transpose(bankA(A_KT[g])[:, j * P:(j + 1) * P], kn[:, j, g * P:(g + 1) * P], ident[:, :])
                    mm.then_inc(fullA[A_KT[g]].sem, 1)

            def rough_scores(a, rounds_):
                for r in rounds_:
                    b, g, half = r // 4, r // 2 % 2, r % 2
                    u = A_MAX + r
                    claimA(pe, u, a)
                    if r == 0:
                        pe.wait_ge(ev["kTb_ready"].sem, ev["kTb_ready"].of(a))
                        pe.wait_ge(ev["qbdb_ready"].sem, ev["qbdb_ready"].of(a))
                    for c in range(2):
                        hh = 4 * half + 2 * c
                        mm = pe.matmul(bankA(u)[:, c * M:(c + 1) * M], qbdb[:, g, b, hh:hh + 2, :].rearrange("p a n -> p (a n)"),
                                       kTb[:, g, b * M:(b + 1) * M], start=True, stop=True)
                    mm.then_inc(fullA[u].sem, 1)

            def scores(a, r):
                b, g, mc = r // 4, r // 2 % 2, r % 2
                u = A_S + r
                claimA(pe, u, a)
                pe.matmul(bankA(u), kT[:, g, b * M + mc * P:b * M + (mc + 1) * P],
                          qbd[:, g, b, :, :].rearrange("p a n -> p (a n)"), start=True, stop=False)
                pe.wait_ge(ev[f"shift{b}_ready"].sem, ev[f"shift{b}_ready"].of(a))
                pe.matmul(bankA(u), negones[:, :], shift[:, b, 4 * g:4 * g + 4, :].rearrange("p a n -> p (a n)"),
                          start=False, stop=True).then_inc(fullA[u].sem, 1)

            def weighted(a, q):
                b, g = q // 2, q % 2
                pe.wait_ge(freeA[A_S + 2 * q + 1].sem, freeA[A_S + 2 * q + 1].of(a))
                if q == 0:
                    freed(pe, ev["on1_ready"], a)
                if q == 2:
                    pe.wait_ge(ev["on0_ready"].sem, ev["on0_ready"].of(a))
                for p4 in range(4):
                    hp = 4 * g + p4
                    for mc in range(2):
                        mm = pe.matmul(oA[:, hp * 34:hp * 34 + 33], pt[:, q % 2, mc, p4 * P:(p4 + 1) * P],
                                       va[:, 2 * b + mc, hp, 0:33], start=(mc == 0), stop=(mc == 1))
                mm.then_inc(ev[f"pv{q}"].sem, 1)

            def heads_turned(a):
                claimA(pe, A_OT, a)
                for b in range(2):
                    pe.wait_ge(ev[f"on{b}_ready"].sem, ev[f"on{b}_ready"].of(a))
                    mm = pe.transpose(bankA(A_OT)[:, b * P:(b + 1) * P], on[:, b, :, :].rearrange("p a d -> p (a d)"), ident[:, :])
                mm.then_inc(fullA[A_OT].sem, 1)

            def self_qk(b):
                claimB(pe, B_QK, b)
                pe.wait_ge(freeB[B_XT].sem, freeB[B_XT].of(b))
                for s, wt in enumerate((wa["q"], wa["k"])):
                    for g in range(G):
                        at = (s * G + g) * P
                        for k in range(KD):
                            mm = pe.matmul(bankB(B_QK)[:, at:at + P], wt[:, k, g * P:(g + 1) * P], x1T[:, k, :],
                                           start=(k == 0), stop=(k == 1))
                mm.then_inc(fullB[B_QK].sem, 1)

            def self_mix(b):
                claimB(pe, B_QJ, b)
                pe.wait_ge(ev["q4_ready"].sem, ev["q4_ready"].of(b))
                for q4 in range(QG):
                    mm = pe.matmul(bankB(B_QJ)[:, q4 * P:(q4 + 1) * P], jmix[:, q4, :], qk4[:, 0, q4, :], start=True, stop=True)
                mm.then_inc(fullB[B_QJ].sem, 1)

            def self_scores(b, g):
                claimB(pe, B_S[g], b)
                pe.wait_ge(bdt_ready.sem, bdt_ready.of(b))
                pe.wait_ge(qkT_ready.sem, qkT_ready.of(b))
                for p4 in range(4):
                    q4, j = 2 * g + p4 // 2, p4 % 2
                    for bb in range(2):
                        at = (p4 * 2 + bb) * N
                        mm = pe.matmul(bankB(B_S[g])[:, at:at + N],
                                       bd[:, q4, bb, 2 * j:2 * j + 2, :].rearrange("p a n -> p (a n)"),
                                       qk4[:, 1, q4, bb * N:(bb + 1) * N], start=True, stop=True)
                mm.then_inc(fullB[B_S[g]].sem, 1)

            def probs_turned(b, g):
                claimB(pe, B_PT[g], b)
                pe.wait_ge(ev["pn_ready"].sem, ev["pn_ready"].of(b))
                for p4 in range(4):
                    hp = 4 * g + p4
                    mm = pe.transpose(bankB(B_PT[g])[:, p4 * P:(p4 + 1) * P],
                                      pn[:, 2 * hp:2 * hp + 2, :].rearrange("p a n -> p (a n)"), ident[:, :])
                mm.then_inc(fullB[B_PT[g]].sem, 1)

            def self_weighted(b, bb):
                claimB(pe, B_O[bb], b)
                if bb == 0:
                    pe.wait_ge(freeB[B_V].sem, freeB[B_V].of(b))
                    pe.wait_ge(freeB[B_PT[1]].sem, freeB[B_PT[1]].of(b))
                pe.matmul(bankB(B_O[bb])[0:32, 0:HD], v2[:, 0, 0, :], v2[:, 0, 0, 0:HD], start=True, stop=True)
                lo = bb * N
                for g in range(G):
                    for odd in range(2):
                        for p4 in range(4):
                            hp = 4 * g + p4
                            mm = pe.matmul(bankB(B_O[bb])[32 * p4:32 * p4 + 32, g * N:(g + 1) * N],
                                           v2[lo:lo + N, hp, odd, :], pT[lo:lo + N, hp, odd * N:(odd + 1) * N],
                                           start=(odd == 0), stop=(odd == 1))
                mm.then_inc(fullB[B_O[bb]].sem, 1)

            def step(c, a, b, s):
                if c is not None:
                    context_product(c, s, C_K[0], 0, 0)
                if b is not None:
                    pe.wait_ge(ev["x1n_ready"].sem, ev["x1n_ready"].of(b))
                    turn(claimB, B_XT, bankB, fullB, x1n, b)
                if c is not None:
                    pe.wait_ge(ev["xn_ready"].sem, ev["xn_ready"].of(c))
                    turn(claimC, C_XT, bankC, fullC, xn, c)
                if a is not None:
                    rough_scores(a, (0, 1))
                if b is not None:
                    self_qk(b)
                if a is not None:
                    rough_scores(a, (2, 3))
                if b is not None:
                    project(claimB, B_V, bankB, fullB, lambda k: x1T[:, k, :], wa["v"], b)
                if a is not None:
                    rough_scores(a, (4,))
                if c is not None:
                    pe.wait_ge(freeC[C_XT].sem, freeC[C_XT].of(c))
                    project(claimC, C_Q, bankC, fullC, lambda k: xnT[:, k, :], wx_q, c)
                if a is not None:
                    rough_scores(a, (5,))
                if b is not None:
                    self_mix(b)
                if a is not None:
                    rough_scores(a, (6, 7))
                    for r in range(4):
                        scores(a, r)
                    weighted(a, 0)
                if b is not None:
                    self_scores(b, 0)
                    self_scores(b, 1)
                if a is not None:
                    weighted(a, 1)
                    scores(a, 4)
                    scores(a, 5)
                if c is not None:
                    context_product(c, s, C_K[1], 1, 0)
                if a is not None:
                    weighted(a, 2)
                    scores(a, 6)
                    scores(a, 7)
                if b is not None:
                    probs_turned(b, 0)
                    probs_turned(b, 1)
                if c is not None:
                    context_product(c, s, C_V[0], 0, 1)
                if b is not None:
                    self_weighted(b, 0)
                    self_weighted(b, 1)
                if a is not None:
                    weighted(a, 3)
                if b is not None:
                    pe.wait_ge(o2T_ready.sem, o2T_ready.of(b))
                    project(claimB, B_WO, bankB, fullB, lambda k: o2T[:, k, :, :].rearrange("p a n -> p (a n)"), wa["o"], b)
                if c is not None:
                    context_product(c, s, C_V[1], 1, 1)
                if a is not None:
                    heads_turned(a)
                if b is not None:
                    pe.wait_ge(ev["h_ready"].sem, ev["h_ready"].of(b))
                    turn(claimB, B_HT, bankB, fullB, h, b)
                if b is not None:
                    pe.wait_ge(ev["hT_ready"].sem, ev["hT_ready"].of(b))
                    for k in range(KD):
                        mm = pe.matmul(bankB(B_HT)[:, DIM:DIM + E], hT[:, k, :], w_route[:, k, :], start=(k == 0), stop=(k == 1))
                    mm.then_inc(ev["route_full"].sem, 1)
                    project(claimB, B_GU, bankB, fullB, lambda k: hT[:, k, :], ws_gu, b, 2 * DIM)
                if a is not None:
                    pe.wait_ge(ev["oT_ready"].sem, ev["oT_ready"].of(a))
                    for k in range(2):
                        mm = pe.matmul(bankA(A_OT)[:, DIM:2 * DIM], oT[:, k, :, :].rearrange("p a n -> p (a n)"), wx_o[:, k, :],
                                       start=(k == 0), stop=(k == 1))
                    mm.then_inc(ev["proj_full"].sem, 1)
                if c is not None:
                    keys_turned(c)
                    pe.wait_ge(ev["qn_ready"].sem, ev["qn_ready"].of(c))
                    turn(claimA, A_QT, bankA, fullA, qn, c)
                if b is not None:
                    pe.wait_ge(su_ready.sem, su_ready.of(b))
                    turn(claimB, B_ST, bankB, fullB, su, b)
                    pe.wait_ge(freeB[B_ST].sem, freeB[B_ST].of(b))
                    project(claimB, B_Y, bankB, fullB, lambda k: suT[:, k, :], ws_down, b)
            tiles(pe, step)

            pe.wait_ge(sel_ready, 1)
            pe.matmul(bank(0)[:, 0:TILES * E], before[:, :], sel, start=True, stop=True)
            pe.matmul(bank(1)[:, 0:TILES * E], ones[:, :], sel, start=True, stop=True).then_inc(counted, 1)
            pe.wait_ge(positions_ready, 1)
            for lo in range(0, 2 * SLOTS, P):
                n = min(P, 2 * SLOTS - lo)
                pe.matmul(bank(2)[:, lo:lo + n], ones[:, :], v2[:, 0:n // HD, 0, HD:2 * HD], start=(lo == 0), stop=False,
                          skip_group_check=True)

            def place(t, c, n):
                for k in range(2):
                    q = 2 * (c % 2) + k
                    if k == 0:
                        pe.wait_ge(ev["hot_ready"].sem, ev["hot_ready"].of(t))
                    mm = pe.matmul(bank(2)[:, 0:2 * SLOTS], at_slot[:, q, :], at_column[:, q, :], start=False, stop=False,
                                   skip_group_check=True)
                mm.then_inc(ev["hot_used"].sem, 1)
            rounds(pe, TILES, place)
            pe.matmul(bank(2)[:, 0:HD], ones[:, :], v2[:, 0, 0, HD:2 * HD], start=False, stop=True, skip_group_check=True).then_inc(ids_summed, 1)

            def expert(j, c, n):
                def now(lag):
                    i = j - lag
                    return not isinstance(i, int) or 0 <= i < SLOTS, i, (c - lag) % DEEP

                go, i, s = now(0)
                if go:
                    pe.wait_ge(rows_in[s], 16 * n + 16)
                    ahead(pe, ev["rowsT_ready"], i, 2)
                    for k in range(KD):
                        mm = pe.transpose(bank(s % 2)[:, k * P:(k + 1) * P], xg[:, s, k * P:(k + 1) * P], ident[:, :])
                    mm.then_inc(ev["rows_turned"].sem, 1)
                go, i, s = now(1)
                if go:
                    col = pe.value_load(column(weights_at_i[0:1, :], i), min_val=0, max_val=(E - 1) * DIM)
                    pe.wait_ge(ev["rowsT_ready"].sem, ev["rowsT_ready"].of(i))
                    ahead(pe, ev["esu_ready"], i, 2)
                    for k in range(KD):
                        mm = pe.matmul(bank(2 + s % 2)[:, 0:2 * F], xgT[:, s % 2, k * P:(k + 1) * P],
                                       w_gu[:, k, :, :].rearrange("p e f -> p (e f)")[:, bass.ds(col, 2 * F)],
                                       start=(k == 0), stop=(k == 1))
                    mm.then_inc(ev["gu_ready"].sem, 1)
                go, i, s = now(2)
                if go:
                    pe.wait_ge(ev["esu_ready"].sem, ev["esu_ready"].of(i))
                    ahead(pe, ev["esuT_ready"], i, 2)
                    pe.transpose(bank(4 + s % 2)[:, 0:P], esu[:, s % 2, :], ident[:, :]).then_inc(ev["esu_turned"].sem, 1)
                go, i, s = now(3)
                if go:
                    col = pe.value_load(column(weights_at_i[0:1, :], i), min_val=0, max_val=(E - 1) * DIM)
                    pe.wait_ge(ev["esuT_ready"].sem, ev["esuT_ready"].of(i))
                    ahead(pe, ev["y_ready"], i, 2)
                    pe.matmul(bank(6 + s % 2)[:, 0:DIM], esuT[:, s % 2, :],
                              w_down[:, :, :].rearrange("p e d -> p (e d)")[:, bass.ds(col, DIM)], start=True, stop=True)\
                        .then_inc(ev["y_summed"].sem, 1)
            pe.wait_ge(ids_ready, 1)
            rounds(pe, SLOTS, expert, 3)

        @block.scalar
        def _(act):
            act.wait_ge(weights_set, 1)

            def values(c, jj):
                u = C_V[jj]
                act.wait_ge(fullC[u].sem, fullC[u].of(c))
                if jj == 0:
                    freed(act, ev["pv3"], c)
                act.activation(va[:, 2 * jj:2 * jj + 2, :, 0:32],
                               bankC(u).rearrange("p (j h d) -> p j h d", j=2, d=32), ACT.Copy).then_inc(freeC[u].sem, 1)

            def squares(c, jj):
                u = C_K[jj]
                act.wait_ge(freeC[u].sem, freeC[u].of(c))
                freed(act, ev[("k_sum01", "k_sum23")[jj]], c)
                act.activation(ksq[:, 2 * jj:2 * jj + 2, :], kc[:, 2 * jj:2 * jj + 2, :], ACT.Square)\
                    .then_inc(ev[("k_sq01", "k_sq23")[jj]].sem, 1)

            def exponential(a, r):
                act.wait_ge(fullA[A_S + r].sem, fullA[A_S + r].of(a))
                q = r // 2
                if r % 2 == 0:
                    if q >= 2:
                        act.wait_ge(ev[f"pv{q - 2}"].sem, ev[f"pv{q - 2}"].of(a))
                    else:
                        freed(act, ev[f"pv{q + 2}"], a)
                act.activation(pt[:, q % 2, r % 2, :], bankA(A_S + r), ACT.Exp).then_inc(freeA[A_S + r].sem, 1)

            def rows_of(dst, bank_, full, done, b):
                act.wait_ge(full.sem, full.of(b))
                act.copy(dst[:, :, :].rearrange("p k n -> p (k n)"), bank_[:, 0:DIM]).then_inc(done.sem, 1)

            def step(c, a, b, s):
                if b is not None:
                    freed(act, fullB[B_V], b)
                    rows_of(x1T, bankB(B_XT), fullB[B_XT], freeB[B_XT], b)
                if c is not None:
                    freed(act, fullC[C_Q], c)
                    rows_of(xnT, bankC(C_XT), fullC[C_XT], freeC[C_XT], c)
                    squares(c, 0)
                if b is not None:
                    act.wait_ge(fullB[B_QK].sem, fullB[B_QK].of(b))
                    freed(act, fullB[B_S[1]], b)
                    for side, done in ((0, ev["q4_ready"]), (1, qkT_ready)):
                        for q4 in range(QG):
                            g, lo = q4 // 2, q4 % 2 * (P // 2)
                            raw = bankB(B_QK)[lo:lo + P // 2, (side * G + g) * P:(side * G + g + 1) * P]
                            bias = cols[lo:lo + P // 2, 4 + 2 * side + g:5 + 2 * side + g]
                            quarter = cols[lo:lo + P // 2, 13 + g:14 + g]
                            act.activation(qk4[P // 2:P, side, q4, :], raw, ACT.Tanh, bias=bias)
                            ins = act.activation(qk4[0:P // 2, side, q4, :], raw, ACT.Identity,
                                                 bias=bias if side else quarter, scale=1.0 if side else HD ** -0.5)
                        ins.then_inc(done.sem, 1)
                    act.wait_ge(fullB[B_V].sem, fullB[B_V].of(b))
                    freed(act, fullB[B_O[1]], b)
                    vv = bankB(B_V)[:, 0:DIM].rearrange("p (h o d) -> p h o d", o=2, d=HD)
                    act.activation(v2[:, :, 0, 0:HD], vv[:, :, 0, :], ACT.Copy)
                    act.activation(v2[:, :, 1, HD:2 * HD], vv[:, :, 1, :], ACT.Copy).then_inc(freeB[B_V].sem, 1)
                if c is not None:
                    act.wait_ge(freeC[C_Q].sem, freeC[C_Q].of(c))
                    freed(act, ev["q_sum"], c)
                    act.activation(qsq[:, :], qc[:, :], ACT.Square).then_inc(ev["q_sq"].sem, 1)
                if a is not None:
                    for r in range(6):
                        exponential(a, r)
                if c is not None:
                    squares(c, 1)
                if b is not None:
                    act.wait_ge(ev["sh_ready"].sem, ev["sh_ready"].of(b))
                    freed(act, ev["pn_ready"], b)
                    act.activation(ex[:, :, :], sh[:, :, :], ACT.Exp).then_inc(ev["ex_ready"].sem, 1)
                if a is not None:
                    exponential(a, 6)
                    exponential(a, 7)
                if b is not None:
                    for g in range(G):
                        act.wait_ge(fullB[B_PT[g]].sem, fullB[B_PT[g]].of(b))
                        if g == 0:
                            freed(act, fullB[B_O[1]], b)
                        act.copy(pT[:, 4 * g:4 * g + 4, :].rearrange("p a n -> p (a n)"), bankB(B_PT[g])).then_inc(freeB[B_PT[g]].sem, 1)
                if b is not None:
                    freed(act, fullB[B_WO], b)
                    for bb in range(2):
                        act.wait_ge(fullB[B_O[bb]].sem, fullB[B_O[bb]].of(b))
                        act.activation(o2T[:, :, bb, :], bankB(B_O[bb])[:, 0:P].rearrange("p (g n) -> p g n", g=G), ACT.Copy)\
                            .then_inc(freeB[B_O[bb]].sem, 1)
                if c is not None:
                    values(c, 0)
                if a is not None:
                    act.wait_ge(fullA[A_OT].sem, fullA[A_OT].of(a))
                    freed(act, ev["proj_full"], a)
                    act.activation(oT[:, :, :, :].rearrange("p o b n -> p b o n"),
                                   bankA(A_OT)[:, 0:DIM].rearrange("p (b o n) -> p b o n", b=2, o=2), ACT.Copy)\
                        .then_inc(ev["oT_ready"].sem, 1)
                if c is not None:
                    values(c, 1)
                if b is not None:
                    freed(act, fullB[B_GU], b)
                    rows_of(hT, bankB(B_HT), fullB[B_HT], ev["hT_ready"], b)
                if b is not None:
                    act.wait_ge(fullB[B_GU].sem, fullB[B_GU].of(b))
                    freed(act, ev["sg_ready"], b)
                    act.activation(th[:, :], bankB(B_GU)[:, 0:DIM], ACT.Tanh, scale=0.5).then_inc(ev["th_ready"].sem, 1)
                if c is not None:
                    for g in range(G):
                        act.wait_ge(fullA[A_KT[g]].sem, fullA[A_KT[g]].of(c))
                        if g == 0:
                            freed(act, fullA[A_S + 7], c)
                            freed(act, ev["kTb_ready"], c)
                        act.activation(kT[:, g, :], bankA(A_KT[g]), ACT.Identity, bias=cols[:, 3:4], scale=cols[:, 2:3])\
                            .then_inc(freeA[A_KT[g]].sem, 1)
                    act.wait_ge(fullA[A_QT].sem, fullA[A_QT].of(c))
                    freed(act, ev["qbd1_ready"], c)
                    act.activation(qT[:, :, :].rearrange("p k n -> p (k n)"), bankA(A_QT)[:, 0:DIM], ACT.Identity,
                                   bias=cols[:, 1:2], scale=cols[:, 0:1]).then_inc(freeA[A_QT].sem, 1)
                if b is not None:
                    freed(act, fullB[B_Y], b)
                    rows_of(suT, bankB(B_ST), fullB[B_ST], freeB[B_ST], b)
            tiles(act, step)
            act.wait_ge(routed, 2)
            act.activation(prob, tmp, ACT.Exp).then_inc(exps_ready, 1)
            act.wait_ge(ids_ready, 1)

            def expert(j, c, n):
                def now(lag):
                    i = j - lag
                    return not isinstance(i, int) or 0 <= i < SLOTS, i, (c - lag) % DEEP

                go, i, s = now(0)
                if go:
                    act.wait_ge(ev["rows_turned"].sem, ev["rows_turned"].of(i))
                    ahead(act, ev["gu_ready"], i, 2)
                    act.copy(xgT[:, s % 2, :], bank(s % 2)[:, 0:DIM]).then_inc(ev["rowsT_ready"].sem, 1)
                go, i, s = now(1)
                if go:
                    act.wait_ge(ev["gu_ready"].sem, ev["gu_ready"].of(i))
                    ahead(act, ev["esg_ready"], i, 2)
                    act.activation(eth[:, s % 2, :], bank(2 + s % 2)[:, 0:F], ACT.Tanh, scale=0.5).then_inc(ev["eth_ready"].sem, 1)
                go, i, s = now(2)
                if go:
                    act.wait_ge(ev["esu_turned"].sem, ev["esu_turned"].of(i))
                    ahead(act, ev["y_summed"], i, 2)
                    act.copy(esuT[:, s % 2, :], bank(4 + s % 2)[:, 0:P]).then_inc(ev["esuT_ready"].sem, 1)
            rounds(act, SLOTS, expert, 2)

        @block.gpsimd
        def _(pool):
            pool.wait_ge(weights_set, 1)

            def step(c, a, b, s):
                if c is not None:
                    pool.wait_ge(ev["a_veps"].sem, ev["a_veps"].of(c))
                    pool.tensor_tensor(lnA[:, 9:10], lnA[:, 8:9], minushalf[:, :], ALU.pow).then_inc(ev["a_rstd"].sem, 1)
                if b is not None:
                    freed(pool, x2_ready, b)
                    pool.tensor_tensor(x1b[:, :], x1[:, :], rows[:, 3, :], ALU.add).then_inc(ev["x1b_ready"].sem, 1)
                if c is not None:
                    freed(pool, x1_ready, c, buffers=2)
                    pool.tensor_tensor(xres[:, s, :], xt[:, :], rows[:, 2, :], ALU.add).then_inc(ev["xres_ready"].sem, 1)
                if a is not None:
                    for bb in range(2):
                        pool.wait_ge(mx_ready[bb].sem, mx_ready[bb].of(a))
                        freed(pool, fullA[A_S + 4 * bb + 3], a)
                        pool.tensor_tensor(shift[:, bb, :, :], ident[:, :].unsqueeze(1).to_broadcast([P, HP, P]),
                                           mx[:, bb, :].unsqueeze(2).to_broadcast([P, HP, P]), ALU.mult)\
                            .then_inc(ev[f"shift{bb}_ready"].sem, 1)
                if b is not None:
                    pool.wait_ge(ev["mx2_ready"].sem, ev["mx2_ready"].of(b))
                    freed(pool, ev["ex_ready"], b)
                    pool.tensor_tensor(sh[:, :, :], sc[:, :, :], mx2[:, :].unsqueeze(2).to_broadcast([P, 2 * HP, N]),
                                       ALU.subtract).then_inc(ev["sh_ready"].sem, 1)
                    pool.wait_ge(ev["rz2_ready"].sem, ev["rz2_ready"].of(b))
                    freed(pool, fullB[B_PT[1]], b)
                    pool.tensor_tensor(pn[:, :, :], ex[:, :, :], rz2[:, :].unsqueeze(2).to_broadcast([P, 2 * HP, N]),
                                       ALU.mult).then_inc(ev["pn_ready"].sem, 1)
                if c is not None:
                    pool.wait_ge(ev["newton_y3"].sem, ev["newton_y3"].of(c))
                    freed(pool, fullA[A_KT[1]], c)
                    for jj in range(2):
                        pool.tensor_tensor(kn[:, 2 * jj:2 * jj + 2, :].rearrange("p j (h d) -> p (j h) d", d=HD),
                                           kc[:, 2 * jj:2 * jj + 2, :].rearrange("p j (h d) -> p (j h) d", d=HD),
                                           rr[:, H * (1 + 2 * jj):H * (3 + 2 * jj)].unsqueeze(2).to_broadcast([P, 2 * H, HD]),
                                           ALU.mult).then_inc(ev[("kn01_ready", "kn23_ready")[jj]].sem, 1)
                if b is not None:
                    pool.wait_ge(ev["c_veps"].sem, ev["c_veps"].of(b))
                    pool.tensor_tensor(lnC[:, 9:10], lnC[:, 8:9], minushalf[:, :], ALU.pow).then_inc(ev["c_rstd"].sem, 1)
                if a is not None:
                    pool.wait_ge(ev["b_veps"].sem, ev["b_veps"].of(a))
                    pool.tensor_tensor(lnB[:, 9:10], lnB[:, 8:9], minushalf[:, :], ALU.pow).then_inc(ev["b_rstd"].sem, 1)
            tiles(pool, step)
            pool.wait_ge(ids_ready, 1)
            pool.wait_ge(h_out, 16 * TILES)

            def gather(j, c, n):
                if not (isinstance(n, int) and n == 0):
                    pool.wait_ge(rows_in[c], 16 * n)
                pool.tensor_copy(now_ids[:, c:c + 1], column(ids, j)).then_inc(ev["ids_copied"].sem, 1)
                pool.wait_ge(ev["ids_copied"].sem, ev["ids_copied"].of(j))
                ahead(pool, ev["rows_turned"], j, DEEP)
                pool.tensor_tensor(idle[:, :], lane_no[:, :], lane_no[:, :], ALU.add)
                pool.indirect_dma_start(out=xg[:, c, :], out_offset=None, in_=rows_d[:, :],
                                        in_offset=bass.IndirectOffsetOnAxis(ap=now_ids[:, c:c + 1], axis=0)).then_inc(rows_in[c], 16)
            rounds(pool, SLOTS, gather)
            for c in range(DEEP):
                pool.wait_ge(y_out[c], 16 * SLOTS // DEEP)

            def gather_y(t, c, n):
                if not (isinstance(n, int) and n == 0):
                    pool.wait_ge(yg_in[c], 32 * n)
                for k in range(2):
                    ins = pool.tensor_copy(now_pos[:, 2 * c + k:2 * c + k + 1], column(pos_u, k * TILES + t))
                ins.then_inc(ev["pos_copied"].sem, 1)
                pool.wait_ge(ev["pos_copied"].sem, ev["pos_copied"].of(t))
                ahead(pool, ev["res_ready"], t, DEEP)
                pool.tensor_tensor(idle[:, :], lane_no[:, :], lane_no[:, :], ALU.add)
                for k in range(2):
                    pool.indirect_dma_start(out=yg[:, c, k, :], out_offset=None, in_=y_d[:, :],
                                            in_offset=bass.IndirectOffsetOnAxis(ap=now_pos[:, 2 * c + k:2 * c + k + 1], axis=0))\
                        .then_inc(yg_in[c], 16)
            rounds(pool, TILES, gather_y)

        @block.vector
        def _(dve):
            dve.memset(negones[:, :], -1.0)
            dve.memset(minushalf[:, :], -0.5)
            dve.memset(ones[:, :], 1.0)
            dve.memset(va[:, :, :, :], 1.0)
            dve.memset(v2[:, :, :, :], 0.0)
            dve.wait_ge(weights_in, 16 * 26)
            dve.tensor_copy(bcol[:, :, :], cols[:, 9:13].unsqueeze(2).to_broadcast([P, 4, P])).then_inc(setup_dve, 1)
            dve.tensor_reduce(wmean[:, :, 0:H], wx_q[:, :, :].rearrange("p k (h d) -> p k h d", d=HD), AX.X, ALU.add)
            dve.tensor_reduce(wmean[:, :, H:2 * H], wx_kv[:, :, 0:DIM].rearrange("p k (h d) -> p k h d", d=HD), AX.X, ALU.add)
            dve.tensor_reduce(wmean[:, :, 2 * H:3 * H], rows[:, 0:2, :].rearrange("p k (h d) -> p k h d", d=HD), AX.X, ALU.add)\
                .then_inc(setup_dve, 1)
            dve.wait_ge(setup_dve, 2)
            dve.tensor_scalar(wmean[:, :, :], wmean[:, :, :], -1.0 / HD, None, ALU.mult).then_inc(setup_dve, 1)
            dve.wait_ge(setup_dve, 3)
            for k in range(KD):
                for n, t in enumerate((wx_q[:, k, :], wx_kv[:, k, 0:DIM], rows[:, k, :])):
                    tv = t.rearrange("p (h d) -> p h d", d=HD)
                    dve.tensor_tensor(tv, tv, wmean[:, k, n * H:(n + 1) * H].unsqueeze(2).to_broadcast([P, H, HD]), ALU.add)
            dve.tensor_scalar(cols[:, 0:2], cols[:, 0:2], HD ** -0.5, None, ALU.mult)
            dve.tensor_scalar(cols[:, 13:15], cols[:, 4:6], HD ** -0.5, None, ALU.mult)
            dve.tensor_scalar(jmix[P // 2:P, :, :], jmix[P // 2:P, :, :], cols[P // 2:P, 8:9], None, ALU.mult)
            dve.tensor_scalar(ws_down[:, :, :], ws_down[:, :, :], 0.5, None, ALU.mult)
            dve.tensor_scalar(w_down[:, :, :], w_down[:, :, :], 0.5, None, ALU.mult)
            dve.wait_ge(setup_pe, 1)
            dve.tensor_tensor(rows[:, 2:4, :], ringA[:, 0:2, 0:DIM], rows[:, 2:4, :], ALU.add).then_inc(weights_set, 1)
            dve.wait_ge(weights_set, 1)

            def normalise(t, ln, src, dst, pre, done):
                dve.bn_stats(ln[:, 0:6], src[:, :]).then_inc(ev[pre + "_stats"].sem, 1)
                dve.wait_ge(ev[pre + "_stats"].sem, ev[pre + "_stats"].of(t))
                dve.memset(ln[:, 15:16], 0.0)
                dve.bn_aggr(ln[:, 6:8], ln[:, 0:6]).then_inc(ev[pre + "_meanvar"].sem, 1)
                dve.wait_ge(ev[pre + "_meanvar"].sem, ev[pre + "_meanvar"].of(t))
                dve.tensor_scalar(ln[:, 8:9], ln[:, 7:8], EPS, None, ALU.add).then_inc(ev[pre + "_veps"].sem, 1)

            def normalised(t, ln, src, dst, pre, done):
                dve.wait_ge(ev[pre + "_rstd"].sem, ev[pre + "_rstd"].of(t))
                dve.tensor_scalar(dst[:, :], src[:, :], ln[:, 6:7], ln[:, 9:10], ALU.subtract, ALU.mult).then_inc(ev[done].sem, 1)

            def keys(a, jj):
                u = C_K[jj]
                dve.wait_ge(fullC[u].sem, fullC[u].of(a))
                if jj == 0:
                    freed(dve, ev["kn23_ready"], a)
                dve.tensor_tensor(kc[:, 2 * jj:2 * jj + 2, :], bankC(u).rearrange("p (j n) -> p j n", j=2),
                                  rows[:, 1, :].unsqueeze(1).to_broadcast([P, 2, DIM]), ALU.add).then_inc(freeC[u].sem, 1)

            def sums(a, jj):
                dve.wait_ge(ev[("k_sq01", "k_sq23")[jj]].sem, ev[("k_sq01", "k_sq23")[jj]].of(a))
                dve.tensor_reduce(ss[:, H * (1 + 2 * jj):H * (3 + 2 * jj)],
                                  ksq[:, 2 * jj:2 * jj + 2, :].rearrange("p j (h d) -> p (j h) d", d=HD), AX.X, ALU.add)\
                    .then_inc(ev[("k_sum01", "k_sum23")[jj]].sem, 1)

            def inverse_sigmas(a):
                for s in ("q_sum", "k_sum23"):
                    dve.wait_ge(ev[s].sem, ev[s].of(a))
                dve.tensor_scalar(ss[:, :], ss[:, :], 1.0 / HD, EPS, ALU.mult, ALU.add).then_inc(ev["s_eps"].sem, 1)
                dve.wait_ge(ev["s_eps"].sem, ev["s_eps"].of(a))
                dve.tensor_scalar(nt[:, :].bitcast(I32), ss[:, :].bitcast(I32), 1, None, ALU.arith_shift_right)\
                    .then_inc(ev["s_shift"].sem, 1)
                dve.wait_ge(ev["s_shift"].sem, ev["s_shift"].of(a))
                freed(dve, ev["kn23_ready"], a)
                freed(dve, ev["qn_ready"], a)
                dve.tensor_scalar(rr[:, :].bitcast(I32), nt[:, :].bitcast(I32), -1.0, MAGIC, ALU.mult, ALU.add)\
                    .then_inc(ev["newton_y0"].sem, 1)
                for n in range(3):
                    dve.wait_ge(ev[f"newton_y{n}"].sem, ev[f"newton_y{n}"].of(a))
                    dve.scalar_tensor_tensor(nt[:, :], rr[:, :], -0.5, rr[:, :], ALU.mult, ALU.mult).then_inc(ev[f"newton_t{n}"].sem, 1)
                    dve.wait_ge(ev[f"newton_t{n}"].sem, ev[f"newton_t{n}"].of(a))
                    dve.tensor_tensor(nt[:, :], nt[:, :], ss[:, :], ALU.mult).then_inc(ev[f"newton_u{n}"].sem, 1)
                    dve.wait_ge(ev[f"newton_u{n}"].sem, ev[f"newton_u{n}"].of(a))
                    dve.scalar_tensor_tensor(rr[:, :], nt[:, :], 1.5, rr[:, :], ALU.add, ALU.mult).then_inc(ev[f"newton_y{n + 1}"].sem, 1)

            def blocks(dst, src, mask):
                shape = [P, 2, mask.shape[1], N]
                return dict(out=dst, in0=src.unsqueeze(2).to_broadcast(shape),
                            in1=mask[:, :].unsqueeze(1).unsqueeze(3).to_broadcast(shape), op=ALU.mult)

            def maxima(a, rounds_):
                for r in rounds_:
                    bb, u = r // 4, A_MAX + r
                    dve.wait_ge(fullA[u].sem, fullA[u].of(a))
                    if r % 4 == 0:
                        freed(dve, ev[f"shift{bb}_ready"], a)
                    dve.tensor_reduce(mx[:, bb, 2 * (r % 4):2 * (r % 4) + 2], bankA(u).rearrange("p (c m) -> p c m", c=2),
                                      AX.X, ALU.max).then_inc(freeA[u].sem, 1)

            def heads_out(a, bb):
                oo = oA[:, 0:HP * 34].rearrange("p (a e) -> p a e", e=34)
                dve.wait_ge(ev[f"pv{2 * bb + 1}"].sem, ev[f"pv{2 * bb + 1}"].of(a))
                dve.reciprocal(rz[:, bb, :], oo[:, :, 32]).then_inc(ev[f"rz{bb}"].sem, 1)
                dve.wait_ge(ev[f"rz{bb}"].sem, ev[f"rz{bb}"].of(a))
                freed(dve, fullA[A_OT], a)
                for odd in range(2):
                    lo = odd * N
                    dve.tensor_tensor(on[lo:lo + N, bb, :, :], oo[lo:lo + N, :, odd * HD:(odd + 1) * HD],
                                      rz[lo:lo + N, bb, :].unsqueeze(2).to_broadcast([N, HP, HD]), ALU.mult)\
                        .then_inc(ev[(f"onlo{bb}", f"on{bb}_ready")[odd]].sem, 1)

            def step(c, a, b, s):
                if c is not None:
                    dve.wait_ge(x_in, c * 16 + 16)
                    normalise(c, lnA, xt, xn, "a", "xn_ready")
                    keys(c, 0)
                    freed(dve, fullC[C_XT], c)
                    normalised(c, lnA, xt, xn, "a", "xn_ready")
                if a is not None:
                    maxima(a, (0, 1))
                if c is not None:
                    sums(c, 0)
                if a is not None:
                    maxima(a, (2, 3, 4))
                if c is not None:
                    dve.wait_ge(fullC[C_Q].sem, fullC[C_Q].of(c))
                    dve.tensor_tensor(qc[:, :], bankC(C_Q)[:, 0:DIM], rows[:, 0, :], ALU.add).then_inc(freeC[C_Q].sem, 1)
                if a is not None:
                    maxima(a, (5, 6, 7))
                if b is not None:
                    dve.wait_ge(fullB[B_QJ].sem, fullB[B_QJ].of(b))
                    freed(dve, fullB[B_S[1]], b)
                    for q4 in range(QG):
                        ins = dve.tensor_tensor(**blocks(bd[:, q4, :, :, :], bankB(B_QJ)[:, q4 * P:(q4 + 1) * P]
                                                         .rearrange("p (b n) -> p b n", b=2), quadmask))
                    ins.then_inc(bdt_ready.sem, 1)
                if c is not None:
                    dve.wait_ge(ev["q_sq"].sem, ev["q_sq"].of(c))
                    dve.tensor_reduce(ss[:, 0:H], qsq[:, :].rearrange("p (h d) -> p h d", d=HD), AX.X, ALU.add).then_inc(ev["q_sum"].sem, 1)
                if b is not None:
                    for g in range(G):
                        dve.wait_ge(fullB[B_S[g]].sem, fullB[B_S[g]].of(b))
                        if g == 0:
                            freed(dve, ev["sh_ready"], b)
                        dve.scalar_tensor_tensor(sc[:, 8 * g:8 * g + 8, :], bankB(B_S[g]).rearrange("p (a n) -> p a n", n=N), 1.0,
                                                 causal[:, :].unsqueeze(1).to_broadcast([P, 8, N]), ALU.mult, ALU.add)\
                            .then_inc(freeB[B_S[g]].sem, 1)
                    for g in range(G):
                        dve.wait_ge(freeB[B_S[g]].sem, freeB[B_S[g]].of(b))
                    dve.tensor_reduce(mx2[:, :], sc[:, :, :], AX.X, ALU.max).then_inc(ev["mx2_ready"].sem, 1)
                if a is not None:
                    heads_out(a, 0)
                if c is not None:
                    keys(c, 1)
                    sums(c, 1)
                if b is not None:
                    dve.wait_ge(ev["ex_ready"].sem, ev["ex_ready"].of(b))
                    dve.tensor_reduce(z2[:, :], ex[:, :, :], AX.X, ALU.add).then_inc(ev["z2_ready"].sem, 1)
                    dve.wait_ge(ev["z2_ready"].sem, ev["z2_ready"].of(b))
                    freed(dve, ev["pn_ready"], b)
                    dve.reciprocal(rz2[:, :], z2[:, :]).then_inc(ev["rz2_ready"].sem, 1)
                if c is not None:
                    inverse_sigmas(c)
                    dve.wait_ge(ev["newton_y3"].sem, ev["newton_y3"].of(c))
                    freed(dve, fullA[A_QT], c)
                    dve.tensor_tensor(qn[:, :].rearrange("p (h d) -> p h d", d=HD), qc[:, :].rearrange("p (h d) -> p h d", d=HD),
                                      rr[:, 0:H].unsqueeze(2).to_broadcast([P, H, HD]), ALU.mult).then_inc(ev["qn_ready"].sem, 1)
                if a is not None:
                    heads_out(a, 1)
                if b is not None:
                    dve.wait_ge(fullB[B_WO].sem, fullB[B_WO].of(b))
                    dve.wait_ge(ev["x1b_ready"].sem, ev["x1b_ready"].of(b))
                    freed(dve, freeB[B_Y], b)
                    dve.tensor_tensor(x2[:, :], bankB(B_WO)[:, 0:DIM], x1b[:, :], ALU.add).then_inc(x2_ready.sem, 1)
                    dve.wait_ge(x2_ready.sem, x2_ready.of(b))
                    normalise(b, lnC, x2, h, "c", "h_ready")
                    freed(dve, fullB[B_HT], b)
                    if not isinstance(b, int) or b > 0:
                        dve.wait_ge(h_out, 16 * b)
                    normalised(b, lnC, x2, h, "c", "h_ready")
                if a is not None:
                    dve.wait_ge(ev["proj_full"].sem, ev["proj_full"].of(a))
                    dve.wait_ge(ev["xres_ready"].sem, ev["xres_ready"].of(a))
                    freed(dve, ev["x1b_ready"], a)
                    freed(dve, ev["x1n_ready"], a)
                    dve.tensor_tensor(x1[:, :], bankA(A_OT)[:, DIM:2 * DIM], xres[:, 1 - s, :], ALU.add).then_inc(x1_ready.sem, 1)
                    dve.wait_ge(x1_ready.sem, x1_ready.of(a))
                    normalise(a, lnB, x1, x1n, "b", "x1n_ready")
                if b is not None:
                    dve.wait_ge(ev["route_full"].sem, ev["route_full"].of(b))
                    dve.tensor_copy(row(logits, b), bankB(B_HT)[:, DIM:DIM + E]).then_inc(freeB[B_HT].sem, 1)
                    dve.wait_ge(ev["th_ready"].sem, ev["th_ready"].of(b))
                    dve.scalar_tensor_tensor(sg[:, :], th[:, :], 1.0, bankB(B_GU)[:, 0:DIM], ALU.add, ALU.mult).then_inc(ev["sg_ready"].sem, 1)
                    dve.wait_ge(ev["sg_ready"].sem, ev["sg_ready"].of(b))
                    freed(dve, fullB[B_ST], b)
                    dve.tensor_tensor(su[:, :], sg[:, :], bankB(B_GU)[:, DIM:2 * DIM], ALU.mult).then_inc(su_ready.sem, 1)
                if c is not None:
                    for g in range(G):
                        dve.wait_ge(freeA[A_KT[g]].sem, freeA[A_KT[g]].of(c))
                    freed(dve, fullA[A_MAX + 7], c)
                    dve.tensor_copy(kTb[:, :, :], kT[:, :, :]).then_inc(ev["kTb_ready"].sem, 1)
                    dve.wait_ge(freeA[A_QT].sem, freeA[A_QT].of(c))
                    freed(dve, fullA[A_S + 7], c)
                    for g in range(G):
                        dve.tensor_tensor(**blocks(qbd[:, g, :, :, :], qT[:, g, :].rearrange("p (b n) -> p b n", b=2), headmask))\
                            .then_inc(ev[f"qbd{g}_ready"].sem, 1)
                    dve.wait_ge(ev["qbd1_ready"].sem, ev["qbd1_ready"].of(c))
                    dve.tensor_copy(qbdb[:, :, :, :, :], qbd[:, :, :, :, :]).then_inc(ev["qbdb_ready"].sem, 1)
                if a is not None:
                    freed(dve, fullB[B_XT], a)
                    normalised(a, lnB, x1, x1n, "b", "x1n_ready")
                if b is not None:
                    dve.wait_ge(fullB[B_Y].sem, fullB[B_Y].of(b))
                    if not isinstance(b, int) or b > 0:
                        dve.wait_ge(base_out, 16 * b)
                    dve.tensor_tensor(base[:, :], bankB(B_Y)[:, 0:DIM], x2[:, :], ALU.add).then_inc(freeB[B_Y].sem, 1)
            tiles(dve, step)

            steps = [0]

            def link(ins):
                steps[0] += 1
                ins.then_inc(routed, 1)
                dve.wait_ge(routed, steps[0])

            def te(v):
                return v.rearrange("p (t e) -> p t e", e=E)

            def by_tile(v):
                return v.unsqueeze(2).to_broadcast([P, TILES, E])

            reverse = numbers[:, 0:E]
            lane = numbers[:, E:E + P]
            slot_tile = numbers[:, E + P:E + P + SLOTS]
            slot_start = numbers[:, E + P + SLOTS:E + P + 2 * SLOTS]
            tile_no = numbers[:, E + P + 2 * SLOTS:E + P + 2 * SLOTS + TILES]
            reversed_ = reverse.unsqueeze(1).to_broadcast([P, TILES, E])
            top, total, inv, m1, r1, m2, r2 = (most[:, k, :] for k in range(7))
            link(dve.tensor_reduce(top, logits[:, :, :], AX.X, ALU.max))
            link(dve.tensor_tensor(te(tmp), logits[:, :, :], by_tile(top), ALU.subtract))
            dve.wait_ge(exps_ready, 1)
            link(dve.tensor_reduce(total, te(prob), AX.X, ALU.add))
            link(dve.reciprocal(inv, total))
            link(dve.tensor_reduce(m1, te(prob), AX.X, ALU.max))
            link(dve.tensor_tensor(te(tmp), te(prob), by_tile(m1), ALU.is_equal))
            link(dve.tensor_tensor(te(tmp), te(tmp), reversed_, ALU.mult))
            link(dve.tensor_reduce(r1, te(tmp), AX.X, ALU.max))
            link(dve.tensor_tensor(te(first), reversed_, by_tile(r1), ALU.is_equal))
            link(dve.scalar_tensor_tensor(tmp, first, -2.0, prob, ALU.mult, ALU.add))
            link(dve.tensor_reduce(m2, te(tmp), AX.X, ALU.max))
            link(dve.tensor_tensor(te(tmp2), te(tmp), by_tile(m2), ALU.is_equal))
            link(dve.tensor_tensor(te(tmp2), te(tmp2), reversed_, ALU.mult))
            link(dve.tensor_reduce(r2, te(tmp2), AX.X, ALU.max))
            link(dve.tensor_tensor(te(second), reversed_, by_tile(r2), ALU.is_equal))
            dve.tensor_tensor(sel, first, second, ALU.add).then_inc(sel_ready, 1)
            link(dve.tensor_tensor(coef[:, 0, :], m1, inv, ALU.mult))
            link(dve.tensor_tensor(coef[:, 1, :], m2, inv, ALU.mult))
            link(dve.memset(carry, 1.0))
            link(dve.memset(carry.rearrange("p (e t) -> p e t", e=E)[:, :, 0], 0.0))
            dve.wait_ge(counted, 1)
            link(dve.tensor_copy(cnt.rearrange("p (e t) -> p e t", e=E), bank(1)[:, 0:TILES * E].rearrange("p (t e) -> p e t", e=E)))
            link(dve.tensor_tensor_scan(incl, carry, cnt, 0.0, ALU.mult, ALU.add))
            filled, start, end, _, _ = (per_expert[:, k, :] for k in range(5))
            link(dve.tensor_scalar(per_int[:, 0, :], incl.rearrange("p (e t) -> p e t", e=E)[:, :, TILES - 1], P - 1.0, None, ALU.add))
            link(dve.tensor_scalar(per_int[:, 1, :], per_int[:, 0, :], 7, 7, ALU.logical_shift_right, ALU.logical_shift_left))
            link(dve.tensor_copy(filled, per_int[:, 1, :]))
            link(dve.tensor_tensor_scan(end, ones[:, 0:E], filled, 0.0, ALU.mult, ALU.add))
            link(dve.tensor_tensor(start, end, filled, ALU.subtract))
            link(dve.tensor_tensor(incl, incl, cnt, ALU.subtract))
            et = lambda v: v.rearrange("p (e t) -> p e t", e=E)
            link(dve.tensor_tensor(et(incl), et(incl), start.unsqueeze(2).to_broadcast([P, E, TILES]), ALU.add))
            link(dve.tensor_tensor(te(cnt), te(bank(0)[:, 0:TILES * E]), incl.rearrange("p (e t) -> p t e", e=E), ALU.add))
            for k, hot in enumerate((first, second)):
                link(dve.tensor_tensor(tmp, hot, cnt, ALU.mult))
                link(dve.tensor_reduce(pos[:, k, :], te(tmp), AX.X, ALU.add))
            link(dve.tensor_copy(pos_i[:, 0, :, :], pos[:, :, :]))
            link(dve.tensor_copy(pos_u[:, :], pos[:, :, :].rearrange("p k t -> p (k t)")))
            link(dve.tensor_scalar(pos_i[:, 1, :, :], pos_i[:, 0, :, :], P - 1, None, ALU.bitwise_and))
            link(dve.tensor_copy(in_tile[:, :, :], pos_i[:, 1, :, :]))
            link(dve.tensor_scalar(pos_i[:, 1, :, :], pos_i[:, 0, :, :], 7, None, ALU.logical_shift_right))
            link(dve.tensor_copy(of_tile[:, :, :], pos_i[:, 1, :, :]))
            for lo in range(0, SLOTS, SLOTS // 2):
                hi = lo + SLOTS // 2
                over = past[0:1, 0:(SLOTS // 2) * E].rearrange("p (j e) -> p j e", e=E)
                link(dve.tensor_tensor(over, end[0:1, :].unsqueeze(1).to_broadcast([1, SLOTS // 2, E]),
                                       slot_start[0:1, lo:hi].unsqueeze(2).to_broadcast([1, SLOTS // 2, E]), ALU.is_le))
                link(dve.tensor_reduce(weights_at[0:1, lo:hi], over, AX.X, ALU.add))
            link(dve.tensor_scalar(weights_at_i[0:1, :], weights_at[0:1, :], E - 1.0, float(DIM), ALU.min, ALU.mult))
            dve.memset(xgT[:, 0, 0:1], 0.0).then_inc(positions_ready, 1)

            def hots(t, c, n):
                if not isinstance(t, int) or t >= 2:
                    dve.wait_ge(ev["hot_used"].sem, ev["hot_used"].of(t - 2))
                for k in range(2):
                    q = 2 * (c % 2) + k
                    dve.tensor_scalar(at_slot[:, q, :], lane, column(in_tile[:, k, :], t), None, ALU.is_equal)
                    dve.tensor_scalar(at_column[:, q, 0:SLOTS], slot_tile, column(of_tile[:, k, :], t), lane_no[:, :],
                                      ALU.is_equal, ALU.mult)
                    ins = dve.tensor_scalar(at_column[:, q, SLOTS:2 * SLOTS], slot_tile, column(of_tile[:, k, :], t),
                                            column(tile_no, t), ALU.is_equal, ALU.mult)
                ins.then_inc(ev["hot_ready"].sem, 1)
            rounds(dve, TILES, hots)
            dve.wait_ge(ids_summed, 1)
            link(dve.tensor_copy(ids_f[:, :], bank(2)[:, 0:2 * SLOTS]))
            dve.scalar_tensor_tensor(ids[:, :], ids_f[:, SLOTS:2 * SLOTS], float(P), ids_f[:, 0:SLOTS], ALU.mult, ALU.add)\
                .then_inc(ids_ready, 1)

            def expert(j, c, n):
                def now(lag):
                    i = j - lag
                    return not isinstance(i, int) or 0 <= i < SLOTS, i, (c - lag) % DEEP

                go, i, s = now(1)
                if go:
                    gate, up = bank(2 + s % 2)[:, 0:F], bank(2 + s % 2)[:, F:2 * F]
                    dve.wait_ge(ev["eth_ready"].sem, ev["eth_ready"].of(i))
                    dve.scalar_tensor_tensor(esg[:, s % 2, :], eth[:, s % 2, :], 1.0, gate, ALU.add, ALU.mult)\
                        .then_inc(ev["esg_ready"].sem, 1)
                    dve.wait_ge(ev["esg_ready"].sem, ev["esg_ready"].of(i))
                    ahead(dve, ev["esu_turned"], i, 2)
                    dve.tensor_tensor(esu[:, s % 2, :], esg[:, s % 2, :], up, ALU.mult).then_inc(ev["esu_ready"].sem, 1)
                go, i, s = now(3)
                if go:
                    dve.wait_ge(ev["y_summed"].sem, ev["y_summed"].of(i))
                    turn_no = n - 1 if c < 3 else n
                    if not isinstance(turn_no, int) or turn_no > 0:
                        dve.wait_ge(y_out[s], 16 * turn_no)
                    dve.tensor_copy(y[:, s, :], bank(6 + s % 2)[:, 0:DIM]).then_inc(ev["y_ready"].sem, 1)
            rounds(dve, SLOTS, expert, 3)

            def combine(t, c, n):
                dve.wait_ge(base_in[c], 16 * n + 16)
                dve.wait_ge(yg_in[c], 32 * n + 32)
                if not (isinstance(n, int) and n == 0):
                    dve.wait_ge(out_done[c], 16 * n)
                dve.scalar_tensor_tensor(res[:, c, :], yg[:, c, 0, :], column(coef[:, 0, :], t), base4[:, c, :], ALU.mult, ALU.add)\
                    .then_inc(ev["half_summed"].sem, 1)
                dve.wait_ge(ev["half_summed"].sem, ev["half_summed"].of(t))
                dve.scalar_tensor_tensor(res[:, c, :], yg[:, c, 1, :], column(coef[:, 1, :], t), res[:, c, :], ALU.mult, ALU.add)\
                    .then_inc(ev["res_ready"].sem, 1)
            rounds(dve, TILES, combine)


def laid_out(a):
    def t(m):
        return np.ascontiguousarray(m.T)

    def col(v):
        return v.reshape(-1, P).T

    def per_head(v):
        return np.tile(v, HG).reshape(P, 1)

    f32 = np.float32
    kv, wo, bkv = a["L0_xattn_Wkv"], a["L0_xattn_Wproj"], a["L0_xattn_bkv"]
    pairs = lambda v: v.reshape(HP, 2, HD, -1).transpose(0, 2, 1, 3).reshape(P, 2, -1)
    jmix = np.zeros((QG, 2, H // QG, HD, 2, H // QG, HD), f32)
    for n in range(H // QG):
        jmix[:, 0, n, :, 0, n, :] = np.eye(HD)
        jmix[:, 1, n, :, 1, n, :] = a["L0_attn_J_attn"].reshape(QG, H // QG, HD, HD)[:, n]
    q = np.arange(N)
    d = {
        "x": a["x"].reshape(TOK, DIM),
        "ctxT": np.ascontiguousarray(a["ctx_1024"].transpose(0, 2, 1)),
        "wx_q": t(a["L0_xattn_Wq"]), "wx_kv": t(kv), "wx_o": np.ascontiguousarray(pairs(wo.T)),
        "wa_q": t(a["L0_attn_Wq"]), "wa_k": t(a["L0_attn_Wk"]), "wa_v": t(a["L0_attn_Wv"]), "wa_o": t(a["L0_attn_Wo"]),
        "jmix": np.ascontiguousarray(jmix.reshape(QG, P, P).transpose(1, 0, 2)),
        "w_route": a["L0_ffn_router_w"],
        "ws_gate": a["L0_ffn_shared_gate_w"], "ws_up": a["L0_ffn_shared_up_w"], "ws_down": a["L0_ffn_shared_down_w"],
        "cols": np.ascontiguousarray(np.concatenate(
            [per_head(a["L0_xattn_q_gamma"]), per_head(a["L0_xattn_q_beta"]),
             per_head(a["L0_xattn_k_gamma"]), per_head(a["L0_xattn_k_beta"]),
             col(a["L0_attn_bq"]), col(a["L0_attn_bk"]), np.tile(a["L0_attn_lambda_attn"].reshape(1, 1), (P, 1)),
             pairs(bkv[DIM:])[:, :, 0], col(a["L0_attn_bv"]), np.zeros((P, 2), f32)], axis=1)),
        "rows": np.ascontiguousarray(np.stack([a["L0_xattn_bq"], bkv[:DIM], a["L0_xattn_bproj"], a["L0_attn_bo"]])),
        "e_gate": a["L0_ffn_gate_w"], "e_up": a["L0_ffn_up_w"], "e_down": a["L0_ffn_down_w"],
        "before": np.triu(np.ones((P, P), f32), 1),
        "numbers": np.concatenate([E - np.arange(E), np.arange(P), np.arange(SLOTS), P * np.arange(SLOTS),
                                   np.arange(TILES)]).astype(f32),
        "lane_no": np.arange(P, dtype=f32).reshape(P, 1),
        "ident": np.eye(P, dtype=f32),
        "headmask": (np.arange(P)[:, None] // HD == np.arange(HG)[None]).astype(f32),
        "quadmask": (np.arange(P)[:, None] % (P // 2) // HD == np.arange(H // QG)[None]).astype(f32),
        "causal": np.tile(np.where(q[None] > q[:, None], MASKED, 0).astype(f32), (2, 1)),
    }
    return {n: np.ascontiguousarray(v) for n, v in d.items()}


def kernel(**inputs):
    import numpy as _np
    import concourse.bacc as _bacc
    from concourse import mybir as _mybir
    from concourse.bass_utils import run_bass_kernel_spmd as _run

    nc = _bacc.Bacc("TRN2", target_bir_lowering=False, num_devices=1)
    arrays = laid_out({n: _np.asarray(a) for n, a in inputs.items()})
    aps = {n: nc.dram_tensor(f"in_{n}", a.shape, _mybir.dt.from_np(a.dtype), kind="ExternalInput").ap() for n, a in arrays.items()}
    out = nc.dram_tensor("out", (TOK, DIM), F32, kind="ExternalOutput").ap()
    perceiver_block(nc, aps, out)
    r = _run(nc, [{f"in_{n}": a for n, a in arrays.items()}], core_ids=[0])
    return r.results[0]["out"].reshape(B, N, DIM)
```

```python
from contextlib import ExitStack

import numpy as np

import concourse.bass as bass
from concourse import mybir

ALU = mybir.AluOpType
ACT = mybir.ActivationFunctionType
AX = mybir.AxisListType
F32 = mybir.dt.float32
BF16 = mybir.dt.bfloat16
F32R = mybir.dt.float32r
I32 = mybir.dt.int32
U32 = mybir.dt.uint32

P = 128
DIM = 256
H, HD = 16, 16
B, N, M = 64, 64, 256
TOK = B * N
TILES = TOK // P
KD = DIM // P
HG = P // HD
G = H // HG
QG = 4
HP = H // 2
E, F = 16, 128
PAIRS = 2 * TOK
SLOTS = PAIRS // P + E
DEEP = 4
CROSS_LOADS, SELF_LOADS, EXPERT_LOADS = 8, 10, 9
EPS = 1e-5
MASKED = -1e30
MAGIC = 1597463007.0

C_XT, C_Q = 1, 2
C_K, C_V = (0, 3), (4, 5)
C_USES, C_BANKS = 6, 2
A_QT, A_KT = 0, (1, 2)
A_MAX = 3
A_S = 11
A_OT = 19
A_USES, A_BANKS = 20, 2
B_XT, B_QK, B_V, B_QJ = 0, 1, 2, 3
B_S, B_PT, B_O = (4, 5), (6, 7), (8, 9)
B_WO, B_HT, B_GU, B_ST, B_Y = 10, 11, 12, 13, 14
B_USES, B_BANKS = 15, 3


class Event:

    def __init__(self, sem, k=1, per=1):
        self.sem, self.k, self.per = sem, k, per

    def of(self, tile):
        return tile * self.per + self.k


def freed(eng, event, tile, buffers=1):
    if not isinstance(tile, int) or tile >= buffers:
        eng.wait_ge(event.sem, tile * event.per + (event.k - buffers * event.per))


def ahead(eng, event, j, lag):
    if not isinstance(j, int) or j >= lag:
        eng.wait_ge(event.sem, event.of(j - lag))


def column(t, j):
    return t[:, j:j + 1] if isinstance(j, int) else t[:, bass.ds(j, 1)]


def row(t, j):
    return t[:, j, :] if isinstance(j, int) else t[:, bass.ds(j, 1), :].rearrange("p o m -> p (o m)")


def block_of(t, j):
    return t[j] if isinstance(j, int) else t[bass.ds(j, 1), :, :].rearrange("o p m -> p (o m)")


def perceiver_block(nc, w, out):
    x, ctxT = w["x"], w["ctxT"]
    with ExitStack() as ctx:
        def sb(name, shape, dt=F32):
            return ctx.enter_context(nc.sbuf_tensor(name, shape, dt))

        def sem(name):
            return ctx.enter_context(nc.semaphore(name))

        wx_q = sb("wx_q", [P, KD, DIM])
        wx_kv = sb("wx_kv", [P, KD, 2 * DIM], F32R)
        wx_kv_rest = sb("wx_kv_rest", [P, KD, 2 * DIM], F32R)
        wx_o = sb("wx_o", [P, 2, DIM])
        wa = {n: sb("wa_" + n, [P, KD, DIM]) for n in "qkvo"}
        jmix = sb("jmix", [P, QG, P])
        w_route = sb("w_route", [P, KD, E])
        ws_gu = sb("ws_gu", [P, KD, 2 * DIM])
        ws_down = sb("ws_down", [P, KD, DIM])
        cols = sb("cols", [P, 15])
        rows = sb("rows", [P, 4, DIM])
        ident = sb("ident", [P, P])
        headmask = sb("headmask", [P, HG])
        quadmask = sb("quadmask", [P, H // QG])
        causal = sb("causal", [P, N])
        negones = sb("negones", [P, P], BF16)
        minushalf = sb("minushalf", [P, 1])
        before = sb("before", [P, P])
        ones = sb("ones", [P, P])
        numbers = sb("numbers", [P, E + P + 2 * SLOTS])
        lane_no = sb("lane_no", [P, 1])
        idle = sb("idle", [P, 1])
        w_gu = sb("w_gu", [P, KD, E, 2 * F])
        w_down = sb("w_down", [P, E, DIM])
        wmean = sb("wmean", [P, KD, 3 * H])

        xt = sb("xt", [P, DIM])
        ct_in = sb("ct_in", [P, KD, 2, M])
        ct = sb("ct", [P, 2, KD, 2, M], F32R)
        ct_rest = sb("ct_rest", [P, 2, KD, 2, M], F32R)
        lnA = sb("lnA", [P, 16])
        xn = sb("xn", [P, DIM])
        xres = sb("xres", [P, 2, DIM])
        xnT = sb("xnT", [P, KD, P])
        qc = sb("qc", [P, DIM])
        qsq = sb("qsq", [P, DIM])
        kc = sb("kc", [P, 4, DIM])
        ksq = sb("ksq", [P, 4, DIM])
        va = sb("va", [P, 4, HP, 34])
        ss = sb("ss", [P, 5 * H])
        rr = sb("rr", [P, 5 * H])
        nt = sb("nt", [P, 5 * H])
        qn = sb("qn", [P, DIM])
        kn = ksq
        wx_kv_in = kc[:, :, :].rearrange("p (k a) n -> p k (a n)", k=KD)
        kT = sb("kT", [P, G, 2 * M])
        kTb = sb("kTb", [P, G, 2 * M], BF16)
        qT = sb("qT", [P, G, P])
        qbd = sb("qbd", [P, G, 2, HG, N])
        qbdb = sb("qbdb", [P, G, 2, HG, N], BF16)
        mx = sb("mx", [P, 2, HP])
        shift = sb("shift", [P, 2, HP, P], BF16)
        pt = sb("pt", [P, 2, 2, HG * N])
        rz = sb("rz", [P, 2, HP])
        on = sb("on", [P, 2, HP, HD])
        oT = sb("oT", [P, 2, 2, N])
        x1 = sb("x1", [P, DIM])

        lnB = sb("lnB", [P, 16])
        x1n = sb("x1n", [P, DIM])
        x1b = sb("x1b", [P, DIM])
        x1T = sb("x1T", [P, KD, P])
        qk4 = sb("qk4", [P, 2, QG, P])
        v2 = sb("v2", [P, HP, 2, 2 * HD])
        bd = sb("bd", [P, QG, 2, H // QG, N])
        sc = sb("sc", [P, HP * 2, N])
        sh = sc
        ex = pn = sc
        mx2 = sb("mx2", [P, HP * 2])
        z2 = sb("z2", [P, HP * 2])
        rz2 = sb("rz2", [P, HP * 2])
        pT = sb("pT", [P, HP, P])
        bcol = pT[:, 0:4, :]
        o2T = sb("o2T", [P, G, 2, N])
        x2 = sb("x2", [P, DIM])
        lnC = sb("lnC", [P, 16])
        h = sb("h", [P, DIM])
        hT = sb("hT", [P, KD, P])
        th = sb("th", [P, DIM])
        sg = sb("sg", [P, DIM])
        su = sb("su", [P, DIM])
        suT = sb("suT", [P, KD, P])
        base = sb("base", [P, DIM])
        logits = sb("logits", [P, TILES, E])

        tables = [t.rearrange("p g b h n -> p (g b h n)")[:, k * 512:k * 512 + TILES * E]
                  for t in (bd[:, :, :, :, :], qbd[:, :, :, :, :]) for k in range(4)]
        prob, first, second, tmp, tmp2, sel, cnt, incl = tables
        carry = qk4[:, 1, :, :].rearrange("p g n -> p (g n)")[:, 0:TILES * E]
        most = sb("most", [P, 7, TILES])
        per_expert = sb("per_expert", [P, 5, E])
        per_int = sb("per_int", [P, 2, E], I32)
        pos = sb("pos", [P, 2, TILES])
        pos_i = sb("pos_i", [P, 2, 2, TILES], I32)
        pos_u = sb("pos_u", [P, 2 * TILES], U32)
        in_tile = sb("in_tile", [P, 2, TILES])
        of_tile = sb("of_tile", [P, 2, TILES])
        coef = sb("coef", [P, 2, TILES])
        past = kT[:, :, :].rearrange("p g m -> p (g m)")
        weights_at = sb("weights_at", [P, SLOTS])
        weights_at_i = sb("weights_at_i", [P, SLOTS], I32)
        at_slot = pT[:, 0:2 * DEEP, :]
        at_column = shift[:, :, :, :].rearrange("p b h n -> p (b h n)")[:, 0:4 * DEEP * SLOTS].bitcast(F32)\
            .rearrange("p (q n) -> p q n", q=2 * DEEP)
        token_no = sb("token_no", [P, TILES])
        ids = sb("ids", [P, SLOTS], U32)
        now_ids = sb("now_ids", [P, DEEP], U32)
        now_pos = sb("now_pos", [P, 2 * DEEP], U32)
        xg = pt[:, :, :, :].rearrange("p a b n -> p (a b n)")[:, 0:DEEP * DIM].rearrange("p (c d) -> p c d", c=DEEP)
        xgT = qk4[:, 0, :, :].rearrange("p (s g) n -> p s (g n)", s=2)
        scratch = sc[:, :, :].rearrange("p a n -> p (a n)").rearrange("p (k c n) -> p k c n", k=4, c=2)
        eth, esg, esu, esuT = (scratch[:, k, :, :] for k in range(4))
        y = kc[:, :, :]
        yg = qbd[:, :, :, :, :].rearrange("p g b h n -> p (g b h n)")[:, 0:DEEP * 2 * DIM]\
            .rearrange("p (c k d) -> p c k d", c=DEEP, k=2)
        res = kn[:, :, :]
        base4 = kT[:, :, :].rearrange("p g (c d) -> p (g c) d", d=DIM)
        rows_d = nc.dram_tensor("normalised_rows", (TOK, DIM), F32, kind="Internal").ap()
        base_d = nc.dram_tensor("rows_without_experts", (TOK, DIM), F32, kind="Internal").ap()
        y_d = nc.dram_tensor("expert_rows", (SLOTS * P, DIM), F32, kind="Internal").ap()

        ringC = ctx.enter_context(nc.psum_tensor("ringC", [P, C_BANKS, 512], F32))
        ringA = ctx.enter_context(nc.psum_tensor("ringA", [P, A_BANKS, 512], F32))
        oA = ctx.enter_context(nc.psum_tensor("oA", [P, 512], F32))
        ringB = ctx.enter_context(nc.psum_tensor("ringB", [P, B_BANKS, 512], F32))

        def bankA(u):
            return ringA[:, u % A_BANKS, :]

        def bankC(u):
            return ringC[:, u % C_BANKS, :]

        def bankB(u):
            return ringB[:, u % B_BANKS, :]

        def ring(name, banks, uses):
            full = [sem(f"full{name}{k}") for k in range(banks)]
            free = [sem(f"free{name}{k}") for k in range(banks)]
            return ([Event(full[u % banks], u // banks + 1, uses // banks) for u in range(uses)],
                    [Event(free[u % banks], u // banks + 1, uses // banks) for u in range(uses)])

        fullC, freeC = ring("C", C_BANKS, C_USES)
        fullA, freeA = ring("A", A_BANKS, A_USES)
        fullB, freeB = ring("B", B_BANKS, B_USES)

        def claim(pe, free, banks, u, tile):
            if u >= banks:
                pe.wait_ge(free[u - banks].sem, free[u - banks].of(tile))
            else:
                freed(pe, free[u + len(free) - banks], tile)

        def claimA(pe, u, tile):
            claim(pe, freeA, A_BANKS, u, tile)

        def claimC(pe, u, tile):
            claim(pe, freeC, C_BANKS, u, tile)

        def claimB(pe, u, tile):
            claim(pe, freeB, B_BANKS, u, tile)

        x1_ready, x2_ready, su_ready, qkT_ready = freeA[A_OT], freeB[B_WO], freeB[B_GU], freeB[B_QK]
        bdt_ready, o2T_ready = freeB[B_QJ], freeB[B_O[1]]
        mx_ready = (freeA[A_MAX + 3], freeA[A_MAX + 7])

        weights_in = sem("weights_in")
        weights_set = sem("weights_set")
        self_weights_in, expert_weights_in = sem("self_weights_in"), sem("expert_weights_in")
        self_weights_set, expert_weights_set = sem("self_weights_set"), sem("expert_weights_set")
        setup_dve = sem("setup_dve")
        setup_pe = sem("setup_pe")
        x_in, h_out, base_out = sem("x_in"), sem("h_out"), sem("base_out")
        base_in = [sem(f"base_in{c}") for c in range(DEEP)]
        routed, exps_ready, sel_ready, counted = sem("routed"), sem("exps_ready"), sem("sel_ready"), sem("counted")
        positions_ready, ids_summed, ids_ready = sem("positions_ready"), sem("ids_summed"), sem("ids_ready")
        rows_in = [sem(f"rows_in{c}") for c in range(DEEP)]
        y_out = [sem(f"y_out{c}") for c in range(DEEP)]
        yg_in = [sem(f"yg_in{c}") for c in range(DEEP)]
        out_done = [sem(f"out_done{c}") for c in range(DEEP)]
        ctx_in = [sem(f"ctx_in{k}") for k in range(KD)]

        def chain(name, *steps):
            one = sem(name)
            return {n: Event(one, k + 1, len(steps)) for k, n in enumerate(steps)}

        ev = {}
        for ln in "abc":
            ev.update(chain(f"{ln}_norm", f"{ln}_stats", f"{ln}_meanvar", f"{ln}_veps"))
            ev.update(chain(f"{ln}_rstd", f"{ln}_rstd"))
        ev.update(chain("newton", "s_eps", "s_shift", "newton_y0", *(f"newton_{s}" for n in range(3)
                        for s in (f"t{n}", f"u{n}", f"y{n + 1}"))))
        ev.update(chain("k_sq", "k_sq01", "k_sq23"))
        ev.update(chain("k_sum", "k_sum01", "k_sum23"))
        ev.update(chain("kn_ready", "kn01_ready", "kn23_ready"))
        ev.update(chain("qbdb_ready", "qbdb0_ready", "qbdb1_ready"))
        ev.update(chain("qbd_ready", "qbd0_ready", "qbd1_ready"))
        ev.update(chain("shift_ready", "shift0_ready", "shift1_ready"))
        ev.update(chain("pv", "pv0", "pv1", "pv2", "pv3"))
        ev.update(chain("heads_out", "rz0", "onlo0", "on0_ready", "rz1", "onlo1", "on1_ready"))
        ev.update(chain("z2", "z2_ready", "rz2_ready"))
        for n in ("ct_ready ct_rest_ready xn_ready xres_ready q_sq q_sum qn_ready x1n_ready x1b_ready q4_ready"
                  " oT_ready proj_full hT_ready route_full mx2_ready sh_ready ex_ready pn_ready h_ready th_ready sg_ready").split():
            ev.update(chain(n, n))

        for n in ("hot_ready hot_used ids_copied rows_turned rowsT_ready gu_ready eth_ready esg_ready esu_ready"
                  " esu_turned esuT_ready y_summed y_ready pos_copied half_summed res_ready").split():
            ev.update(chain(n, n))

        def bank(k):
            return ringC[:, k, :] if k < 2 else ringA[:, k - 2, :] if k < 4 else oA[:, :] if k == 4 else ringB[:, k - 5, :]

        block = ctx.enter_context(nc.Block())

        def rounds(eng, count, body, drain=0):
            for c in range(DEEP):
                body(c, c, 0)
            with eng.Fori(1, count // DEEP) as n:
                for c in range(DEEP):
                    body(n * DEEP + c, c, n)
            for c in range(drain):
                body(count + c, c, count // DEEP)

        def tiles(eng, step):
            for e in range(5):
                step(*(e - lag if e >= lag else None for lag in range(5)), (e - 1) % 2)
            with eng.Fori(2, TILES // 2 - 1) as n:
                for odd in range(2):
                    step(*(n * 2 + (odd + 1 - lag) for lag in range(5)), odd)
            for e in range(TILES - 1, TILES + 4):
                step(*(e - lag if e - lag < TILES else None for lag in range(5)), (e - 1) % 2)

        x_d = x.rearrange("(t p) d -> t p d", p=P)
        ctx_d = ctxT.rearrange("(t b) (k p) m -> t k p b m", b=2, p=P)

        @block.sync
        def _(sp):
            def load(dst, src, done=weights_in):
                sp.dma_start(dst, src).then_inc(done, 16)

            def halves(name):
                return w[name].rearrange("(k p) n -> p k n", p=P)

            def load_cross_weights():
                load(cols[:, :], w["cols"])
                load(rows[:, :, :], w["rows"].partition_broadcast(P))
                load(wx_kv_in, halves("wx_kv"))
                load(wx_q[:, :, :], halves("wx_q"))
                load(wx_o[:, :, :], w["wx_o"])
                load(wa["o"][:, :, :], halves("wa_o"))
                load(ident[:, :], w["ident"])
                load(headmask[:, :], w["headmask"])

            def load_self_weights():
                for dst, name in ((wa["q"], "wa_q"), (wa["k"], "wa_k"), (wa["v"], "wa_v"), (w_route, "w_route"),
                                  (ws_down, "ws_down")):
                    load(dst[:, :, :], halves(name), self_weights_in)
                load(ws_gu[:, :, 0:DIM], halves("ws_gate"), self_weights_in)
                load(ws_gu[:, :, DIM:2 * DIM], halves("ws_up"), self_weights_in)
                load(jmix[:, :, :], w["jmix"], self_weights_in)
                load(quadmask[:, :], w["quadmask"], self_weights_in)
                load(causal[:, :], w["causal"], self_weights_in)

            def load_expert_weights():
                load(before[:, :], w["before"], expert_weights_in)
                load(numbers[:, :], w["numbers"].partition_broadcast(P), expert_weights_in)
                load(lane_no[:, :], w["lane_no"], expert_weights_in)
                load(token_no[:, :], w["token_no"], expert_weights_in)
                load(w_down[:, :, :], w["e_down"].rearrange("e f d -> f e d"), expert_weights_in)
                for k in range(KD):
                    for half, name in enumerate(("e_gate", "e_up")):
                        load(w_gu[:, k, :, half * F:(half + 1) * F], w[name][:, k * P:(k + 1) * P, :].rearrange("e p f -> p e f"),
                             expert_weights_in)

            def load_tile(c):
                freed(sp, ev["ct_rest_ready"], c)
                for k in range(KD):
                    here = ctx_d[c, k] if isinstance(c, int) else \
                        ctx_d[bass.ds(c, 1), k, :, :, :].rearrange("o p b m -> p (o b) m")
                    sp.dma_start(ct_in[:, k, :, :], here).then_inc(ctx_in[k], 16)
                freed(sp, ev["xn_ready"], c)
                freed(sp, ev["xres_ready"], c)
                sp.dma_start(xt[:, :], block_of(x_d, c)).then_inc(x_in, 16)

            def step(e, c, a, b, d, s):
                if e is not None:
                    load_tile(e)
                if isinstance(e, int) and e == 0:
                    load_self_weights()
                if isinstance(e, int) and e == 2:
                    load_expert_weights()
                if d is not None:
                    sp.wait_ge(ev["h_ready"].sem, ev["h_ready"].of(d))
                    sp.dma_start(block_of(rows_t, d), h[:, :]).then_inc(h_out, 16)
                    sp.wait_ge(freeB[B_Y].sem, freeB[B_Y].of(d))
                    sp.dma_start(block_of(base_t, d), base[:, :]).then_inc(base_out, 16)

            rows_t = rows_d.rearrange("(t p) d -> t p d", p=P)
            base_t = base_d.rearrange("(t p) d -> t p d", p=P)
            y_t = y_d.rearrange("(t p) d -> t p d", p=P)
            out_t = out.rearrange("(t p) d -> t p d", p=P)
            load_cross_weights()
            tiles(sp, step)

            def store_y(j, c, n):
                sp.wait_ge(ev["y_ready"].sem, ev["y_ready"].of(j))
                sp.dma_start(block_of(y_t, j), y[:, c, :]).then_inc(y_out[c], 16)
            rounds(sp, SLOTS, store_y)

            def store_out(t, c, n):
                ahead(sp, ev["half_summed"], t, DEEP)
                sp.dma_start(base4[:, c, :], block_of(base_t, t)).then_inc(base_in[c], 16)
                if not isinstance(t, int) or t >= 2:
                    store_last(t - 2, (c - 2) % DEEP, n)

            def store_last(t, c, n):
                sp.wait_ge(ev["res_ready"].sem, ev["res_ready"].of(t))
                sp.dma_start(block_of(out_t, t), res[:, c, :]).then_inc(out_done[c], 16)
            sp.wait_ge(base_out, 16 * TILES)
            rounds(sp, TILES, store_out)
            for t in (TILES - 2, TILES - 1):
                store_last(t, t % DEEP, 0)
            for c in range(DEEP):
                sp.wait_ge(out_done[c], 16 * TILES // DEEP)

        @block.tensor
        def _(pe):
            pe.wait_ge(setup_dve, 1)
            for side, wo in ((0, wx_o), (1, wa["o"])):
                for k in range(2):
                    mm = pe.matmul(ringA[:, side, 0:DIM], bcol[:, 2 * side + k, :], wo[:, k, :], start=(k == 0), stop=(k == 1))
            mm.then_inc(setup_pe, 1)
            pe.wait_ge(weights_set, 1)

            def context_product(c, s, u, jj, part, halves=(0, 1)):
                if 0 in halves:
                    claimC(pe, u, c)
                if u == C_K[0] and 0 in halves:
                    pe.wait_ge(ev["ct_rest_ready"].sem, ev["ct_rest_ready"].of(c))
                for half in halves:
                    j = 2 * jj + half
                    for k in range(KD):
                        for n, (left, right) in enumerate(((ct, wx_kv), (ct, wx_kv_rest), (ct_rest, wx_kv))):
                            mm = pe.matmul(bankC(u)[:, half * DIM:(half + 1) * DIM],
                                           left[:, s, k, j // 2, (j % 2) * P:(j % 2 + 1) * P],
                                           right[:, k, part * DIM:(part + 1) * DIM],
                                           start=(k == 0 and n == 0), stop=(k == 1 and n == 2))
                if 1 in halves:
                    mm.then_inc(fullC[u].sem, 1)

            def turn(claim_, u, bank, full, src, tile):
                claim_(pe, u, tile)
                for k in range(KD):
                    mm = pe.transpose(bank(u)[:, k * P:(k + 1) * P], src[:, k * P:(k + 1) * P], ident[:, :])
                mm.then_inc(full[u].sem, 1)

            def project(claim_, u, bank, full, lhs, rhs, tile, n=DIM):
                claim_(pe, u, tile)
                for k in range(KD):
                    mm = pe.matmul(bank(u)[:, 0:n], lhs(k), rhs[:, k, 0:n], start=(k == 0), stop=(k == 1))
                mm.then_inc(full[u].sem, 1)

            def keys_turned(a, g):
                claimA(pe, A_KT[g], a)
                if g == 0:
                    pe.wait_ge(ev["kn23_ready"].sem, ev["kn23_ready"].of(a))
                for j in range(4):
                    mm = pe.transpose(bankA(A_KT[g])[:, j * P:(j + 1) * P], kn[:, j, g * P:(g + 1) * P], ident[:, :])
                mm.then_inc(fullA[A_KT[g]].sem, 1)

            def rough_scores(a, rounds_):
                for r in rounds_:
                    b, g, half = r // 4, r // 2 % 2, r % 2
                    u = A_MAX + r
                    claimA(pe, u, a)
                    if r == 0:
                        pe.wait_ge(freeA[A_KT[1]].sem, freeA[A_KT[1]].of(a))
                    if r in (0, 2):
                        pe.wait_ge(ev[f"qbdb{g}_ready"].sem, ev[f"qbdb{g}_ready"].of(a))
                    for c in range(2):
                        hh = 4 * half + 2 * c
                        mm = pe.matmul(bankA(u)[:, c * M:(c + 1) * M], qbdb[:, g, b, hh:hh + 2, :].rearrange("p a n -> p (a n)"),
                                       kTb[:, g, b * M:(b + 1) * M], start=True, stop=True)
                    mm.then_inc(fullA[u].sem, 1)

            def scores(a, r):
                b, g, mc = r // 4, r // 2 % 2, r % 2
                u = A_S + r
                claimA(pe, u, a)
                pe.matmul(bankA(u), kT[:, g, b * M + mc * P:b * M + (mc + 1) * P],
                          qbd[:, g, b, :, :].rearrange("p a n -> p (a n)"), start=True, stop=False)
                pe.wait_ge(ev[f"shift{b}_ready"].sem, ev[f"shift{b}_ready"].of(a))
                pe.matmul(bankA(u), negones[:, :], shift[:, b, 4 * g:4 * g + 4, :].rearrange("p a n -> p (a n)"),
                          start=False, stop=True).then_inc(fullA[u].sem, 1)

            def weighted(a, q):
                b, g = q // 2, q % 2
                pe.wait_ge(freeA[A_S + 2 * q + 1].sem, freeA[A_S + 2 * q + 1].of(a))
                if q == 0:
                    freed(pe, ev["on1_ready"], a)
                if q == 2:
                    pe.wait_ge(ev["on0_ready"].sem, ev["on0_ready"].of(a))
                for p4 in range(4):
                    hp = 4 * g + p4
                    for mc in range(2):
                        mm = pe.matmul(oA[:, hp * 34:hp * 34 + 33], pt[:, q % 2, mc, p4 * P:(p4 + 1) * P],
                                       va[:, 2 * b + mc, hp, 0:33], start=(mc == 0), stop=(mc == 1))
                mm.then_inc(ev[f"pv{q}"].sem, 1)

            def heads_turned(a):
                claimA(pe, A_OT, a)
                for b in range(2):
                    pe.wait_ge(ev[f"on{b}_ready"].sem, ev[f"on{b}_ready"].of(a))
                    mm = pe.transpose(bankA(A_OT)[:, b * P:(b + 1) * P], on[:, b, :, :].rearrange("p a d -> p (a d)"), ident[:, :])
                mm.then_inc(fullA[A_OT].sem, 1)

            def self_qk(b, side):
                if side == 0:
                    if isinstance(b, int) and b == 0:
                        pe.wait_ge(self_weights_in, 16 * SELF_LOADS)
                    claimB(pe, B_QK, b)
                    pe.wait_ge(freeB[B_XT].sem, freeB[B_XT].of(b))
                for g in range(G):
                    at = (side * G + g) * P
                    for k in range(KD):
                        mm = pe.matmul(bankB(B_QK)[:, at:at + P], wa["qk"[side]][:, k, g * P:(g + 1) * P], x1T[:, k, :],
                                       start=(k == 0), stop=(k == 1))
                if side == 1:
                    mm.then_inc(fullB[B_QK].sem, 1)

            def self_mix(b):
                if isinstance(b, int) and b == 0:
                    pe.wait_ge(self_weights_set, 1)
                claimB(pe, B_QJ, b)
                pe.wait_ge(ev["q4_ready"].sem, ev["q4_ready"].of(b))
                for q4 in range(QG):
                    mm = pe.matmul(bankB(B_QJ)[:, q4 * P:(q4 + 1) * P], jmix[:, q4, :], qk4[:, 0, q4, :], start=True, stop=True)
                mm.then_inc(fullB[B_QJ].sem, 1)

            def self_scores(b, g):
                claimB(pe, B_S[g], b)
                pe.wait_ge(bdt_ready.sem, bdt_ready.of(b))
                pe.wait_ge(qkT_ready.sem, qkT_ready.of(b))
                for p4 in range(4):
                    q4, j = 2 * g + p4 // 2, p4 % 2
                    for bb in range(2):
                        at = (p4 * 2 + bb) * N
                        mm = pe.matmul(bankB(B_S[g])[:, at:at + N],
                                       bd[:, q4, bb, 2 * j:2 * j + 2, :].rearrange("p a n -> p (a n)"),
                                       qk4[:, 1, q4, bb * N:(bb + 1) * N], start=True, stop=True)
                mm.then_inc(fullB[B_S[g]].sem, 1)

            def probs_turned(b, g):
                claimB(pe, B_PT[g], b)
                pe.wait_ge(ev["pn_ready"].sem, ev["pn_ready"].of(b))
                for p4 in range(4):
                    hp = 4 * g + p4
                    mm = pe.transpose(bankB(B_PT[g])[:, p4 * P:(p4 + 1) * P],
                                      pn[:, 2 * hp:2 * hp + 2, :].rearrange("p a n -> p (a n)"), ident[:, :])
                mm.then_inc(fullB[B_PT[g]].sem, 1)

            def self_weighted(b, bb):
                claimB(pe, B_O[bb], b)
                if bb == 0:
                    pe.wait_ge(freeB[B_V].sem, freeB[B_V].of(b))
                    pe.wait_ge(freeB[B_PT[1]].sem, freeB[B_PT[1]].of(b))
                pe.matmul(bankB(B_O[bb])[0:32, 0:HD], v2[:, 0, 0, :], v2[:, 0, 0, 0:HD], start=True, stop=True)
                lo = bb * N
                for g in range(G):
                    for odd in range(2):
                        for p4 in range(4):
                            hp = 4 * g + p4
                            mm = pe.matmul(bankB(B_O[bb])[32 * p4:32 * p4 + 32, g * N:(g + 1) * N],
                                           v2[lo:lo + N, hp, odd, :], pT[lo:lo + N, hp, odd * N:(odd + 1) * N],
                                           start=(odd == 0), stop=(odd == 1))
                mm.then_inc(fullB[B_O[bb]].sem, 1)

            def step(e, c, a, b, d, s):
                if c is not None:
                    context_product(c, s, C_K[0], 0, 0, (0,))
                if d is not None:
                    pe.wait_ge(su_ready.sem, su_ready.of(d))
                    turn(claimB, B_ST, bankB, fullB, su, d)
                if c is not None:
                    context_product(c, s, C_K[0], 0, 0, (1,))
                if d is not None:
                    pe.wait_ge(freeB[B_ST].sem, freeB[B_ST].of(d))
                    project(claimB, B_Y, bankB, fullB, lambda k: suT[:, k, :], ws_down, d)
                if b is not None:
                    pe.wait_ge(ev["x1n_ready"].sem, ev["x1n_ready"].of(b))
                    turn(claimB, B_XT, bankB, fullB, x1n, b)
                if b is not None:
                    self_qk(b, 0)
                if a is not None:
                    rough_scores(a, (0,))
                if b is not None:
                    self_qk(b, 1)
                if a is not None:
                    rough_scores(a, (1,))
                if c is not None:
                    pe.wait_ge(ev["xn_ready"].sem, ev["xn_ready"].of(c))
                    turn(claimC, C_XT, bankC, fullC, xn, c)
                if a is not None:
                    rough_scores(a, (2,))
                if b is not None:
                    project(claimB, B_V, bankB, fullB, lambda k: x1T[:, k, :], wa["v"], b)
                if a is not None:
                    rough_scores(a, (3, 4))
                if c is not None:
                    pe.wait_ge(freeC[C_XT].sem, freeC[C_XT].of(c))
                    project(claimC, C_Q, bankC, fullC, lambda k: xnT[:, k, :], wx_q, c)
                if a is not None:
                    rough_scores(a, (5, 6))
                if b is not None:
                    self_mix(b)
                if a is not None:
                    rough_scores(a, (7,))
                    for r in range(4):
                        scores(a, r)
                    weighted(a, 0)
                if b is not None:
                    self_scores(b, 0)
                    self_scores(b, 1)
                if a is not None:
                    weighted(a, 1)
                    scores(a, 4)
                    scores(a, 5)
                if c is not None:
                    context_product(c, s, C_K[1], 1, 0)
                if a is not None:
                    weighted(a, 2)
                    scores(a, 6)
                    scores(a, 7)
                if b is not None:
                    probs_turned(b, 0)
                    probs_turned(b, 1)
                if a is not None:
                    weighted(a, 3)
                if c is not None:
                    context_product(c, s, C_V[0], 0, 1)
                if b is not None:
                    self_weighted(b, 0)
                    self_weighted(b, 1)
                if a is not None:
                    heads_turned(a)
                if b is not None:
                    pe.wait_ge(o2T_ready.sem, o2T_ready.of(b))
                    project(claimB, B_WO, bankB, fullB, lambda k: o2T[:, k, :, :].rearrange("p a n -> p (a n)"), wa["o"], b)
                if c is not None:
                    context_product(c, s, C_V[1], 1, 1)
                if a is not None:
                    pe.wait_ge(ev["oT_ready"].sem, ev["oT_ready"].of(a))
                    for k in range(2):
                        mm = pe.matmul(bankA(A_OT)[:, DIM:2 * DIM], oT[:, k, :, :].rearrange("p a n -> p (a n)"), wx_o[:, k, :],
                                       start=(k == 0), stop=(k == 1))
                    mm.then_inc(ev["proj_full"].sem, 1)
                if c is not None:
                    pe.wait_ge(ev["qn_ready"].sem, ev["qn_ready"].of(c))
                    turn(claimA, A_QT, bankA, fullA, qn, c)
                if b is not None:
                    pe.wait_ge(ev["h_ready"].sem, ev["h_ready"].of(b))
                    turn(claimB, B_HT, bankB, fullB, h, b)
                if c is not None:
                    keys_turned(c, 0)
                if b is not None:
                    pe.wait_ge(ev["hT_ready"].sem, ev["hT_ready"].of(b))
                    for k in range(KD):
                        mm = pe.matmul(bankB(B_HT)[:, DIM:DIM + E], hT[:, k, :], w_route[:, k, :], start=(k == 0), stop=(k == 1))
                    mm.then_inc(ev["route_full"].sem, 1)
                    project(claimB, B_GU, bankB, fullB, lambda k: hT[:, k, :], ws_gu, b, 2 * DIM)
                if c is not None:
                    keys_turned(c, 1)
            tiles(pe, step)

            pe.wait_ge(expert_weights_in, 16 * EXPERT_LOADS)
            pe.wait_ge(sel_ready, 1)
            pe.matmul(bank(0)[:, 0:TILES * E], before[:, :], sel, start=True, stop=True)
            pe.matmul(bank(1)[:, 0:TILES * E], ones[:, :], sel, start=True, stop=True).then_inc(counted, 1)
            pe.wait_ge(positions_ready, 1)
            for h0 in range(0, SLOTS // HD):
                pe.matmul(bank(2)[:, h0 * HD:(h0 + 1) * HD], ones[:, :], v2[:, h0, 0, HD:2 * HD], start=(h0 == 0), stop=False,
                          skip_group_check=True)

            def place(t, c, n):
                pe.wait_ge(ev["hot_ready"].sem, ev["hot_ready"].of(t))
                for k in range(2):
                    q = 2 * c + k
                    mm = pe.matmul(bank(2)[:, 0:SLOTS], at_slot[:, q, :], at_column[:, q, :], start=False, stop=False,
                                   skip_group_check=True)
                mm.then_inc(ev["hot_used"].sem, 1)
            rounds(pe, TILES, place)
            pe.matmul(bank(2)[:, 0:HD], ones[:, :], v2[:, 0, 0, HD:2 * HD], start=False, stop=True,
                      skip_group_check=True).then_inc(ids_summed, 1)

            lies_at = [pe.alloc_register(f"weights_at{c}") for c in range(DEEP)]

            def expert(j, c, n):
                def now(lag):
                    i = j - lag
                    return not isinstance(i, int) or 0 <= i < SLOTS, i, (c - lag) % DEEP

                go, i, s = now(0)
                if go:
                    pe.wait_ge(rows_in[s], 16 * n + 16)
                    ahead(pe, ev["rowsT_ready"], i, 2)
                    for k in range(KD):
                        mm = pe.transpose(bank(s % 2)[:, k * P:(k + 1) * P], xg[:, s, k * P:(k + 1) * P], ident[:, :])
                    mm.then_inc(ev["rows_turned"].sem, 1)
                go, i, s = now(1)
                if go:
                    col = pe.snap(lies_at[s], min_val=0, max_val=(E - 1) * DIM)
                    pe.wait_ge(ev["rowsT_ready"].sem, ev["rowsT_ready"].of(i))
                    ahead(pe, ev["esu_ready"], i, 2)
                    for k in range(KD):
                        mm = pe.matmul(bank(2 + s % 2)[:, 0:2 * F], xgT[:, s % 2, k * P:(k + 1) * P],
                                       w_gu[:, k, :, :].rearrange("p e f -> p (e f)")[:, bass.ds(col, 2 * F)],
                                       start=(k == 0), stop=(k == 1))
                    mm.then_inc(ev["gu_ready"].sem, 1)
                if not isinstance(j, int) or j < SLOTS:
                    pe.reg_load(lies_at[c], column(weights_at_i[0:1, :], j))
                go, i, s = now(2)
                if go:
                    pe.wait_ge(ev["esu_ready"].sem, ev["esu_ready"].of(i))
                    ahead(pe, ev["esuT_ready"], i, 2)
                    pe.transpose(bank(4 + s % 2)[:, 0:P], esu[:, s % 2, :], ident[:, :]).then_inc(ev["esu_turned"].sem, 1)
                go, i, s = now(3)
                if go:
                    col = pe.snap(lies_at[s], min_val=0, max_val=(E - 1) * DIM)
                    pe.wait_ge(ev["esuT_ready"].sem, ev["esuT_ready"].of(i))
                    ahead(pe, ev["y_ready"], i, 2)
                    pe.matmul(bank(6 + s % 2)[:, 0:DIM], esuT[:, s % 2, :],
                              w_down[:, :, :].rearrange("p e d -> p (e d)")[:, bass.ds(col, DIM)], start=True, stop=True)\
                        .then_inc(ev["y_summed"].sem, 1)
            pe.wait_ge(ids_ready, 1)
            pe.wait_ge(expert_weights_set, 1)
            rounds(pe, SLOTS, expert, 3)

        @block.scalar
        def _(act):
            act.wait_ge(weights_set, 1)

            def values(c, jj):
                u = C_V[jj]
                act.wait_ge(fullC[u].sem, fullC[u].of(c))
                if jj == 0:
                    freed(act, ev["pv3"], c)
                act.activation(va[:, 2 * jj:2 * jj + 2, :, 0:32],
                               bankC(u).rearrange("p (j h d) -> p j h d", j=2, d=32), ACT.Copy).then_inc(freeC[u].sem, 1)

            def squares(c, jj):
                u = C_K[jj]
                act.wait_ge(freeC[u].sem, freeC[u].of(c))
                freed(act, ev[("k_sum01", "k_sum23")[jj]], c)
                act.activation(ksq[:, 2 * jj:2 * jj + 2, :], kc[:, 2 * jj:2 * jj + 2, :], ACT.Square)\
                    .then_inc(ev[("k_sq01", "k_sq23")[jj]].sem, 1)

            def exponential(a, r):
                act.wait_ge(fullA[A_S + r].sem, fullA[A_S + r].of(a))
                q = r // 2
                if r % 2 == 0:
                    if q >= 2:
                        act.wait_ge(ev[f"pv{q - 2}"].sem, ev[f"pv{q - 2}"].of(a))
                    else:
                        freed(act, ev[f"pv{q + 2}"], a)
                act.activation(pt[:, q % 2, r % 2, :], bankA(A_S + r), ACT.Exp).then_inc(freeA[A_S + r].sem, 1)

            def rows_of(dst, bank_, full, done, b):
                act.wait_ge(full.sem, full.of(b))
                act.copy(dst[:, :, :].rearrange("p k n -> p (k n)"), bank_[:, 0:DIM]).then_inc(done.sem, 1)

            def keys_in(c, g):
                act.wait_ge(fullA[A_KT[g]].sem, fullA[A_KT[g]].of(c))
                if g == 0:
                    freed(act, fullA[A_S + 7], c)
                act.activation(kT[:, g, :], bankA(A_KT[g]), ACT.Identity, bias=cols[:, 3:4], scale=cols[:, 2:3])
                act.activation(kTb[:, g, :], bankA(A_KT[g]), ACT.Identity, bias=cols[:, 3:4], scale=cols[:, 2:3])\
                    .then_inc(freeA[A_KT[g]].sem, 1)

            def queries_or_keys(b, side, done):
                act.wait_ge(fullB[B_QK].sem, fullB[B_QK].of(b))
                freed(act, fullB[B_S[1]], b)
                for q4 in range(QG):
                    g, lo = q4 // 2, q4 % 2 * (P // 2)
                    raw = bankB(B_QK)[lo:lo + P // 2, (side * G + g) * P:(side * G + g + 1) * P]
                    bias = cols[lo:lo + P // 2, 4 + 2 * side + g:5 + 2 * side + g]
                    quarter = cols[lo:lo + P // 2, 13 + g:14 + g]
                    act.activation(qk4[P // 2:P, side, q4, :], raw, ACT.Tanh, bias=bias)
                    ins = act.activation(qk4[0:P // 2, side, q4, :], raw, ACT.Identity,
                                         bias=bias if side else quarter, scale=1.0 if side else HD ** -0.5)
                ins.then_inc(done.sem, 1)

            def rough_queries(a, g):
                act.wait_ge(ev[f"qbd{g}_ready"].sem, ev[f"qbd{g}_ready"].of(a))
                act.copy(qbdb[:, g, :, :, :], qbd[:, g, :, :, :]).then_inc(ev[f"qbdb{g}_ready"].sem, 1)

            def step(e, c, a, b, d, s):
                if d is not None:
                    freed(act, fullB[B_Y], d)
                    rows_of(suT, bankB(B_ST), fullB[B_ST], freeB[B_ST], d)
                if a is not None:
                    rough_queries(a, 0)
                if b is not None:
                    freed(act, fullB[B_V], b)
                    rows_of(x1T, bankB(B_XT), fullB[B_XT], freeB[B_XT], b)
                if a is not None:
                    rough_queries(a, 1)
                if b is not None:
                    queries_or_keys(b, 0, ev["q4_ready"])
                if c is not None:
                    freed(act, fullC[C_Q], c)
                    rows_of(xnT, bankC(C_XT), fullC[C_XT], freeC[C_XT], c)
                if b is not None:
                    queries_or_keys(b, 1, qkT_ready)
                if c is not None:
                    squares(c, 0)
                if b is not None:
                    act.wait_ge(fullB[B_V].sem, fullB[B_V].of(b))
                    freed(act, fullB[B_O[1]], b)
                    vv = bankB(B_V)[:, 0:DIM].rearrange("p (h o d) -> p h o d", o=2, d=HD)
                    act.activation(v2[:, :, 0, 0:HD], vv[:, :, 0, :], ACT.Copy)
                    act.activation(v2[:, :, 1, HD:2 * HD], vv[:, :, 1, :], ACT.Copy).then_inc(freeB[B_V].sem, 1)
                if c is not None:
                    act.wait_ge(freeC[C_Q].sem, freeC[C_Q].of(c))
                    freed(act, ev["q_sum"], c)
                    act.activation(qsq[:, :], qc[:, :], ACT.Square).then_inc(ev["q_sq"].sem, 1)
                if a is not None:
                    for r in range(6):
                        exponential(a, r)
                if b is not None:
                    act.wait_ge(ev["sh_ready"].sem, ev["sh_ready"].of(b))
                    freed(act, ev["pn_ready"], b)
                    act.activation(ex[:, :, :], sh[:, :, :], ACT.Exp).then_inc(ev["ex_ready"].sem, 1)
                if c is not None:
                    squares(c, 1)
                if a is not None:
                    exponential(a, 6)
                    exponential(a, 7)
                if b is not None:
                    for g in range(G):
                        act.wait_ge(fullB[B_PT[g]].sem, fullB[B_PT[g]].of(b))
                        if g == 0:
                            freed(act, fullB[B_O[1]], b)
                        act.copy(pT[:, 4 * g:4 * g + 4, :].rearrange("p a n -> p (a n)"), bankB(B_PT[g])).then_inc(freeB[B_PT[g]].sem, 1)
                if b is not None:
                    freed(act, fullB[B_WO], b)
                    for bb in range(2):
                        act.wait_ge(fullB[B_O[bb]].sem, fullB[B_O[bb]].of(b))
                        act.activation(o2T[:, :, bb, :], bankB(B_O[bb])[:, 0:P].rearrange("p (g n) -> p g n", g=G), ACT.Copy)\
                            .then_inc(freeB[B_O[bb]].sem, 1)
                if c is not None:
                    values(c, 0)
                if a is not None:
                    act.wait_ge(fullA[A_OT].sem, fullA[A_OT].of(a))
                    freed(act, ev["proj_full"], a)
                    act.activation(oT[:, :, :, :].rearrange("p o b n -> p b o n"),
                                   bankA(A_OT)[:, 0:DIM].rearrange("p (b o n) -> p b o n", b=2, o=2), ACT.Copy)\
                        .then_inc(ev["oT_ready"].sem, 1)
                if c is not None:
                    values(c, 1)
                if c is not None:
                    act.wait_ge(fullA[A_QT].sem, fullA[A_QT].of(c))
                    freed(act, ev["qbd1_ready"], c)
                    act.activation(qT[:, :, :].rearrange("p k n -> p (k n)"), bankA(A_QT)[:, 0:DIM], ACT.Identity,
                                   bias=cols[:, 1:2], scale=cols[:, 0:1]).then_inc(freeA[A_QT].sem, 1)
                if b is not None:
                    freed(act, fullB[B_GU], b)
                    rows_of(hT, bankB(B_HT), fullB[B_HT], ev["hT_ready"], b)
                if c is not None:
                    keys_in(c, 0)
                if b is not None:
                    act.wait_ge(fullB[B_GU].sem, fullB[B_GU].of(b))
                    freed(act, ev["sg_ready"], b)
                    act.activation(th[:, :], bankB(B_GU)[:, 0:DIM], ACT.Tanh, scale=0.5).then_inc(ev["th_ready"].sem, 1)
                if c is not None:
                    keys_in(c, 1)
            tiles(act, step)
            act.wait_ge(routed, 2)
            act.activation(prob, tmp, ACT.Exp).then_inc(exps_ready, 1)
            act.wait_ge(ids_ready, 1)

            def expert(j, c, n):
                def now(lag):
                    i = j - lag
                    return not isinstance(i, int) or 0 <= i < SLOTS, i, (c - lag) % DEEP

                go, i, s = now(0)
                if go:
                    act.wait_ge(ev["rows_turned"].sem, ev["rows_turned"].of(i))
                    ahead(act, ev["gu_ready"], i, 2)
                    act.copy(xgT[:, s % 2, :], bank(s % 2)[:, 0:DIM]).then_inc(ev["rowsT_ready"].sem, 1)
                go, i, s = now(1)
                if go:
                    act.wait_ge(ev["gu_ready"].sem, ev["gu_ready"].of(i))
                    ahead(act, ev["esg_ready"], i, 2)
                    act.activation(eth[:, s % 2, :], bank(2 + s % 2)[:, 0:F], ACT.Tanh, scale=0.5).then_inc(ev["eth_ready"].sem, 1)
                go, i, s = now(2)
                if go:
                    act.wait_ge(ev["esu_turned"].sem, ev["esu_turned"].of(i))
                    ahead(act, ev["y_summed"], i, 2)
                    act.copy(esuT[:, s % 2, :], bank(4 + s % 2)[:, 0:P]).then_inc(ev["esuT_ready"].sem, 1)
            rounds(act, SLOTS, expert, 2)

        @block.gpsimd
        def _(pool):
            pool.wait_ge(weights_set, 1)

            def step(e, c, a, b, d, s):
                if c is not None:
                    pool.wait_ge(ev["a_veps"].sem, ev["a_veps"].of(c))
                    pool.tensor_tensor(lnA[:, 9:10], lnA[:, 8:9], minushalf[:, :], ALU.pow).then_inc(ev["a_rstd"].sem, 1)
                if b is not None:
                    freed(pool, x2_ready, b)
                    pool.tensor_tensor(x1b[:, :], x1[:, :], rows[:, 3, :], ALU.add).then_inc(ev["x1b_ready"].sem, 1)
                if c is not None:
                    freed(pool, x1_ready, c, buffers=2)
                    pool.tensor_tensor(xres[:, s, :], xt[:, :], rows[:, 2, :], ALU.add).then_inc(ev["xres_ready"].sem, 1)
                if a is not None:
                    for bb in range(2):
                        pool.wait_ge(mx_ready[bb].sem, mx_ready[bb].of(a))
                        freed(pool, fullA[A_S + 4 * bb + 3], a)
                        pool.tensor_tensor(shift[:, bb, :, :], ident[:, :].unsqueeze(1).to_broadcast([P, HP, P]),
                                           mx[:, bb, :].unsqueeze(2).to_broadcast([P, HP, P]), ALU.mult)\
                            .then_inc(ev[f"shift{bb}_ready"].sem, 1)
                if e is not None:
                    pool.wait_ge(ev["ct_ready"].sem, ev["ct_ready"].of(e))
                    pool.tensor_tensor(ct_rest[:, 1 - s, :, :, :], ct_in[:, :, :, :], ct[:, 1 - s, :, :, :].bitcast(F32),
                                       ALU.subtract).then_inc(ev["ct_rest_ready"].sem, 1)
                if b is not None:
                    pool.wait_ge(ev["mx2_ready"].sem, ev["mx2_ready"].of(b))
                    freed(pool, ev["ex_ready"], b)
                    pool.tensor_tensor(sh[:, :, :], sc[:, :, :], mx2[:, :].unsqueeze(2).to_broadcast([P, 2 * HP, N]),
                                       ALU.subtract).then_inc(ev["sh_ready"].sem, 1)
                    pool.wait_ge(ev["rz2_ready"].sem, ev["rz2_ready"].of(b))
                    freed(pool, fullB[B_PT[1]], b)
                    pool.tensor_tensor(pn[:, :, :], ex[:, :, :], rz2[:, :].unsqueeze(2).to_broadcast([P, 2 * HP, N]),
                                       ALU.mult).then_inc(ev["pn_ready"].sem, 1)
                if c is not None:
                    pool.wait_ge(ev["newton_y3"].sem, ev["newton_y3"].of(c))
                    freed(pool, fullA[A_KT[1]], c)
                    for jj in range(2):
                        pool.tensor_tensor(kn[:, 2 * jj:2 * jj + 2, :].rearrange("p j (h d) -> p (j h) d", d=HD),
                                           kc[:, 2 * jj:2 * jj + 2, :].rearrange("p j (h d) -> p (j h) d", d=HD),
                                           rr[:, H * (1 + 2 * jj):H * (3 + 2 * jj)].unsqueeze(2).to_broadcast([P, 2 * H, HD]),
                                           ALU.mult).then_inc(ev[("kn01_ready", "kn23_ready")[jj]].sem, 1)
                if b is not None:
                    pool.wait_ge(ev["c_veps"].sem, ev["c_veps"].of(b))
                    pool.tensor_tensor(lnC[:, 9:10], lnC[:, 8:9], minushalf[:, :], ALU.pow).then_inc(ev["c_rstd"].sem, 1)
                if a is not None:
                    pool.wait_ge(ev["b_veps"].sem, ev["b_veps"].of(a))
                    pool.tensor_tensor(lnB[:, 9:10], lnB[:, 8:9], minushalf[:, :], ALU.pow).then_inc(ev["b_rstd"].sem, 1)
            tiles(pool, step)
            pool.wait_ge(ids_ready, 1)
            pool.wait_ge(h_out, 16 * TILES)

            def gather(j, c, n):
                if not (isinstance(n, int) and n == 0):
                    pool.wait_ge(rows_in[c], 16 * n)
                pool.tensor_copy(now_ids[:, c:c + 1], column(ids, j)).then_inc(ev["ids_copied"].sem, 1)
                pool.wait_ge(ev["ids_copied"].sem, ev["ids_copied"].of(j))
                ahead(pool, ev["rows_turned"], j, DEEP)
                pool.tensor_tensor(idle[:, :], lane_no[:, :], lane_no[:, :], ALU.add)
                pool.indirect_dma_start(out=xg[:, c, :], out_offset=None, in_=rows_d[:, :],
                                        in_offset=bass.IndirectOffsetOnAxis(ap=now_ids[:, c:c + 1], axis=0)).then_inc(rows_in[c], 16)
            rounds(pool, SLOTS, gather)
            for c in range(DEEP):
                pool.wait_ge(y_out[c], 16 * SLOTS // DEEP)

            def gather_y(t, c, n):
                if not (isinstance(n, int) and n == 0):
                    pool.wait_ge(yg_in[c], 32 * n)
                here = pos_u[:, 2 * t:2 * t + 2] if isinstance(t, int) else pos_u[:, bass.ds(t * 2, 2)]
                pool.tensor_copy(now_pos[:, 2 * c:2 * c + 2], here).then_inc(ev["pos_copied"].sem, 1)
                pool.wait_ge(ev["pos_copied"].sem, ev["pos_copied"].of(t))
                ahead(pool, ev["res_ready"], t, DEEP)
                pool.tensor_tensor(idle[:, :], lane_no[:, :], lane_no[:, :], ALU.add)
                for k in range(2):
                    pool.indirect_dma_start(out=yg[:, c, k, :], out_offset=None, in_=y_d[:, :],
                                            in_offset=bass.IndirectOffsetOnAxis(ap=now_pos[:, 2 * c + k:2 * c + k + 1], axis=0))\
                        .then_inc(yg_in[c], 16)
            rounds(pool, TILES, gather_y)

        @block.vector
        def _(dve):
            dve.memset(negones[:, :], -1.0)
            dve.memset(minushalf[:, :], -0.5)
            dve.memset(ones[:, :], 1.0)
            dve.memset(va[:, :, :, :], 1.0)
            dve.memset(v2[:, :, :, :], 0.0)
            dve.wait_ge(weights_in, 16 * CROSS_LOADS)
            dve.tensor_copy(bcol, cols[:, 9:13].unsqueeze(2).to_broadcast([P, 4, P])).then_inc(setup_dve, 1)
            dve.tensor_reduce(wmean[:, :, 0:H], wx_q[:, :, :].rearrange("p k (h d) -> p k h d", d=HD), AX.X, ALU.add)
            dve.tensor_reduce(wmean[:, :, H:2 * H], wx_kv_in[:, :, 0:DIM].rearrange("p k (h d) -> p k h d", d=HD), AX.X, ALU.add)
            dve.tensor_reduce(wmean[:, :, 2 * H:3 * H], rows[:, 0:2, :].rearrange("p k (h d) -> p k h d", d=HD), AX.X, ALU.add)\
                .then_inc(setup_dve, 1)
            dve.wait_ge(setup_dve, 2)
            dve.tensor_scalar(wmean[:, :, :], wmean[:, :, :], -1.0 / HD, None, ALU.mult).then_inc(setup_dve, 1)
            dve.wait_ge(setup_dve, 3)
            for k in range(KD):
                for n, t in enumerate((wx_q[:, k, :], wx_kv_in[:, k, 0:DIM], rows[:, k, :])):
                    tv = t.rearrange("p (h d) -> p h d", d=HD)
                    ins = dve.tensor_tensor(tv, tv, wmean[:, k, n * H:(n + 1) * H].unsqueeze(2).to_broadcast([P, H, HD]), ALU.add)
            ins.then_inc(setup_dve, 1)
            dve.wait_ge(setup_dve, 4)
            dve.tensor_copy(wx_kv[:, :, :], wx_kv_in).then_inc(setup_dve, 1)
            dve.wait_ge(setup_dve, 5)
            dve.tensor_tensor(wx_kv_rest[:, :, :], wx_kv_in, wx_kv[:, :, :].bitcast(F32), ALU.subtract)
            dve.tensor_scalar(cols[:, 0:2], cols[:, 0:2], HD ** -0.5, None, ALU.mult)
            dve.tensor_scalar(cols[:, 13:15], cols[:, 4:6], HD ** -0.5, None, ALU.mult)
            dve.wait_ge(setup_pe, 1)
            dve.tensor_tensor(rows[:, 2:4, :], ringA[:, 0:2, 0:DIM], rows[:, 2:4, :], ALU.add).then_inc(weights_set, 1)
            dve.wait_ge(weights_set, 1)

            def normalise(t, ln, src, dst, pre, done):
                dve.bn_stats(ln[:, 0:6], src[:, :]).then_inc(ev[pre + "_stats"].sem, 1)
                dve.wait_ge(ev[pre + "_stats"].sem, ev[pre + "_stats"].of(t))
                dve.memset(ln[:, 15:16], 0.0)
                dve.bn_aggr(ln[:, 6:8], ln[:, 0:6]).then_inc(ev[pre + "_meanvar"].sem, 1)
                dve.wait_ge(ev[pre + "_meanvar"].sem, ev[pre + "_meanvar"].of(t))
                dve.tensor_scalar(ln[:, 8:9], ln[:, 7:8], EPS, None, ALU.add).then_inc(ev[pre + "_veps"].sem, 1)

            def normalised(t, ln, src, dst, pre, done):
                dve.wait_ge(ev[pre + "_rstd"].sem, ev[pre + "_rstd"].of(t))
                dve.tensor_scalar(dst[:, :], src[:, :], ln[:, 6:7], ln[:, 9:10], ALU.subtract, ALU.mult).then_inc(ev[done].sem, 1)

            def keys(a, jj):
                u = C_K[jj]
                dve.wait_ge(fullC[u].sem, fullC[u].of(a))
                if jj == 0:
                    freed(dve, ev["kn23_ready"], a)
                dve.tensor_tensor(kc[:, 2 * jj:2 * jj + 2, :], bankC(u).rearrange("p (j n) -> p j n", j=2),
                                  rows[:, 1, :].unsqueeze(1).to_broadcast([P, 2, DIM]), ALU.add).then_inc(freeC[u].sem, 1)

            def sums(a, jj):
                dve.wait_ge(ev[("k_sq01", "k_sq23")[jj]].sem, ev[("k_sq01", "k_sq23")[jj]].of(a))
                dve.tensor_reduce(ss[:, H * (1 + 2 * jj):H * (3 + 2 * jj)],
                                  ksq[:, 2 * jj:2 * jj + 2, :].rearrange("p j (h d) -> p (j h) d", d=HD), AX.X, ALU.add)\
                    .then_inc(ev[("k_sum01", "k_sum23")[jj]].sem, 1)

            def inverse_sigmas(a):
                for s in ("q_sum", "k_sum23"):
                    dve.wait_ge(ev[s].sem, ev[s].of(a))
                dve.tensor_scalar(ss[:, :], ss[:, :], 1.0 / HD, EPS, ALU.mult, ALU.add).then_inc(ev["s_eps"].sem, 1)
                dve.wait_ge(ev["s_eps"].sem, ev["s_eps"].of(a))
                dve.tensor_scalar(nt[:, :].bitcast(I32), ss[:, :].bitcast(I32), 1, None, ALU.arith_shift_right)\
                    .then_inc(ev["s_shift"].sem, 1)
                dve.wait_ge(ev["s_shift"].sem, ev["s_shift"].of(a))
                freed(dve, ev["kn23_ready"], a)
                freed(dve, ev["qn_ready"], a)
                dve.tensor_scalar(rr[:, :].bitcast(I32), nt[:, :].bitcast(I32), -1.0, MAGIC, ALU.mult, ALU.add)\
                    .then_inc(ev["newton_y0"].sem, 1)
                for n in range(3):
                    dve.wait_ge(ev[f"newton_y{n}"].sem, ev[f"newton_y{n}"].of(a))
                    dve.scalar_tensor_tensor(nt[:, :], rr[:, :], -0.5, rr[:, :], ALU.mult, ALU.mult).then_inc(ev[f"newton_t{n}"].sem, 1)
                    dve.wait_ge(ev[f"newton_t{n}"].sem, ev[f"newton_t{n}"].of(a))
                    dve.tensor_tensor(nt[:, :], nt[:, :], ss[:, :], ALU.mult).then_inc(ev[f"newton_u{n}"].sem, 1)
                    dve.wait_ge(ev[f"newton_u{n}"].sem, ev[f"newton_u{n}"].of(a))
                    dve.scalar_tensor_tensor(rr[:, :], nt[:, :], 1.5, rr[:, :], ALU.add, ALU.mult).then_inc(ev[f"newton_y{n + 1}"].sem, 1)

            def blocks(dst, src, mask):
                shape = [P, 2, mask.shape[1], N]
                return dict(out=dst, in0=src.unsqueeze(2).to_broadcast(shape),
                            in1=mask[:, :].unsqueeze(1).unsqueeze(3).to_broadcast(shape), op=ALU.mult)

            def query_blocks(c, g):
                dve.tensor_tensor(**blocks(qbd[:, g, :, :, :], qT[:, g, :].rearrange("p (b n) -> p b n", b=2), headmask))\
                    .then_inc(ev[f"qbd{g}_ready"].sem, 1)

            def maxima(a, rounds_):
                for r in rounds_:
                    bb, u = r // 4, A_MAX + r
                    dve.wait_ge(fullA[u].sem, fullA[u].of(a))
                    if r % 4 == 0:
                        freed(dve, ev[f"shift{bb}_ready"], a)
                    dve.tensor_reduce(mx[:, bb, 2 * (r % 4):2 * (r % 4) + 2], bankA(u).rearrange("p (c m) -> p c m", c=2),
                                      AX.X, ALU.max).then_inc(freeA[u].sem, 1)

            def heads_out(a, bb):
                oo = oA[:, 0:HP * 34].rearrange("p (a e) -> p a e", e=34)
                dve.wait_ge(ev[f"pv{2 * bb + 1}"].sem, ev[f"pv{2 * bb + 1}"].of(a))
                dve.reciprocal(rz[:, bb, :], oo[:, :, 32]).then_inc(ev[f"rz{bb}"].sem, 1)
                dve.wait_ge(ev[f"rz{bb}"].sem, ev[f"rz{bb}"].of(a))
                freed(dve, fullA[A_OT], a)
                for odd in range(2):
                    lo = odd * N
                    dve.tensor_tensor(on[lo:lo + N, bb, :, :], oo[lo:lo + N, :, odd * HD:(odd + 1) * HD],
                                      rz[lo:lo + N, bb, :].unsqueeze(2).to_broadcast([N, HP, HD]), ALU.mult)\
                        .then_inc(ev[(f"onlo{bb}", f"on{bb}_ready")[odd]].sem, 1)

            def step(e, c, a, b, d, s):
                if d is not None:
                    dve.wait_ge(fullB[B_Y].sem, fullB[B_Y].of(d))
                    if not isinstance(d, int) or d > 0:
                        dve.wait_ge(base_out, 16 * d)
                    dve.tensor_tensor(base[:, :], bankB(B_Y)[:, 0:DIM], x2[:, :], ALU.add).then_inc(freeB[B_Y].sem, 1)
                if b is not None:
                    if isinstance(b, int) and b == 0:
                        dve.wait_ge(self_weights_in, 16 * SELF_LOADS)
                        dve.tensor_scalar(jmix[P // 2:P, :, :], jmix[P // 2:P, :, :], cols[P // 2:P, 8:9], None, ALU.mult)
                        dve.tensor_scalar(ws_down[:, :, :], ws_down[:, :, :], 0.5, None, ALU.mult).then_inc(self_weights_set, 1)
                if c is not None:
                    dve.wait_ge(x_in, c * 16 + 16)
                    normalise(c, lnA, xt, xn, "a", "xn_ready")
                    keys(c, 0)
                    freed(dve, fullC[C_XT], c)
                    normalised(c, lnA, xt, xn, "a", "xn_ready")
                if a is not None:
                    maxima(a, (0, 1))
                    maxima(a, (2, 3, 4))
                if c is not None:
                    dve.wait_ge(fullC[C_Q].sem, fullC[C_Q].of(c))
                    dve.tensor_tensor(qc[:, :], bankC(C_Q)[:, 0:DIM], rows[:, 0, :], ALU.add).then_inc(freeC[C_Q].sem, 1)
                if a is not None:
                    maxima(a, (5, 6, 7))
                if b is not None:
                    dve.wait_ge(fullB[B_QJ].sem, fullB[B_QJ].of(b))
                    freed(dve, fullB[B_S[1]], b)
                    for q4 in range(QG):
                        ins = dve.tensor_tensor(**blocks(bd[:, q4, :, :, :], bankB(B_QJ)[:, q4 * P:(q4 + 1) * P]
                                                         .rearrange("p (b n) -> p b n", b=2), quadmask))
                    ins.then_inc(bdt_ready.sem, 1)
                if e is not None:
                    for k in range(KD):
                        dve.wait_ge(ctx_in[k], e * 16 + 16)
                    freed(dve, fullC[C_V[1]], e, buffers=2)
                    dve.tensor_copy(ct[:, 1 - s, :, :, :], ct_in[:, :, :, :]).then_inc(ev["ct_ready"].sem, 1)
                if c is not None:
                    dve.wait_ge(ev["q_sq"].sem, ev["q_sq"].of(c))
                    dve.tensor_reduce(ss[:, 0:H], qsq[:, :].rearrange("p (h d) -> p h d", d=HD), AX.X, ALU.add).then_inc(ev["q_sum"].sem, 1)
                if b is not None:
                    for g in range(G):
                        dve.wait_ge(fullB[B_S[g]].sem, fullB[B_S[g]].of(b))
                        if g == 0:
                            freed(dve, ev["sh_ready"], b)
                        dve.scalar_tensor_tensor(sc[:, 8 * g:8 * g + 8, :], bankB(B_S[g]).rearrange("p (a n) -> p a n", n=N), 1.0,
                                                 causal[:, :].unsqueeze(1).to_broadcast([P, 8, N]), ALU.mult, ALU.add)\
                            .then_inc(freeB[B_S[g]].sem, 1)
                    for g in range(G):
                        dve.wait_ge(freeB[B_S[g]].sem, freeB[B_S[g]].of(b))
                    dve.tensor_reduce(mx2[:, :], sc[:, :, :], AX.X, ALU.max).then_inc(ev["mx2_ready"].sem, 1)
                if a is not None:
                    heads_out(a, 0)
                if b is not None:
                    dve.wait_ge(ev["ex_ready"].sem, ev["ex_ready"].of(b))
                    dve.tensor_reduce(z2[:, :], ex[:, :, :], AX.X, ALU.add).then_inc(ev["z2_ready"].sem, 1)
                    dve.wait_ge(ev["z2_ready"].sem, ev["z2_ready"].of(b))
                    freed(dve, ev["pn_ready"], b)
                    dve.reciprocal(rz2[:, :], z2[:, :]).then_inc(ev["rz2_ready"].sem, 1)
                if c is not None:
                    keys(c, 1)
                    sums(c, 0)
                    sums(c, 1)
                if c is not None:
                    inverse_sigmas(c)
                    dve.wait_ge(ev["newton_y3"].sem, ev["newton_y3"].of(c))
                    freed(dve, fullA[A_QT], c)
                    dve.tensor_tensor(qn[:, :].rearrange("p (h d) -> p h d", d=HD), qc[:, :].rearrange("p (h d) -> p h d", d=HD),
                                      rr[:, 0:H].unsqueeze(2).to_broadcast([P, H, HD]), ALU.mult).then_inc(ev["qn_ready"].sem, 1)
                if a is not None:
                    heads_out(a, 1)
                if b is not None:
                    dve.wait_ge(fullB[B_WO].sem, fullB[B_WO].of(b))
                    dve.wait_ge(ev["x1b_ready"].sem, ev["x1b_ready"].of(b))
                    freed(dve, freeB[B_Y], b)
                    dve.tensor_tensor(x2[:, :], bankB(B_WO)[:, 0:DIM], x1b[:, :], ALU.add).then_inc(x2_ready.sem, 1)
                    dve.wait_ge(x2_ready.sem, x2_ready.of(b))
                    normalise(b, lnC, x2, h, "c", "h_ready")
                if b is not None:
                    freed(dve, fullB[B_HT], b)
                    if not isinstance(b, int) or b > 0:
                        dve.wait_ge(h_out, 16 * b)
                    normalised(b, lnC, x2, h, "c", "h_ready")
                if a is not None:
                    dve.wait_ge(ev["proj_full"].sem, ev["proj_full"].of(a))
                    dve.wait_ge(ev["xres_ready"].sem, ev["xres_ready"].of(a))
                    freed(dve, ev["x1b_ready"], a)
                    freed(dve, ev["x1n_ready"], a)
                    dve.tensor_tensor(x1[:, :], bankA(A_OT)[:, DIM:2 * DIM], xres[:, 1 - s, :], ALU.add).then_inc(x1_ready.sem, 1)
                    dve.wait_ge(x1_ready.sem, x1_ready.of(a))
                    normalise(a, lnB, x1, x1n, "b", "x1n_ready")
                if a is not None:
                    freed(dve, fullB[B_XT], a)
                    normalised(a, lnB, x1, x1n, "b", "x1n_ready")
                if b is not None:
                    dve.wait_ge(ev["route_full"].sem, ev["route_full"].of(b))
                    dve.tensor_copy(row(logits, b), bankB(B_HT)[:, DIM:DIM + E]).then_inc(freeB[B_HT].sem, 1)
                if c is not None:
                    dve.wait_ge(freeA[A_QT].sem, freeA[A_QT].of(c))
                    freed(dve, fullA[A_S + 7], c)
                    freed(dve, fullA[A_MAX + 7], c)
                    query_blocks(c, 0)
                if b is not None:
                    dve.wait_ge(ev["th_ready"].sem, ev["th_ready"].of(b))
                    dve.scalar_tensor_tensor(sg[:, :], th[:, :], 1.0, bankB(B_GU)[:, 0:DIM], ALU.add, ALU.mult).then_inc(ev["sg_ready"].sem, 1)
                    dve.wait_ge(ev["sg_ready"].sem, ev["sg_ready"].of(b))
                    freed(dve, fullB[B_ST], b)
                    dve.tensor_tensor(su[:, :], sg[:, :], bankB(B_GU)[:, DIM:2 * DIM], ALU.mult).then_inc(su_ready.sem, 1)
                if c is not None:
                    query_blocks(c, 1)
            tiles(dve, step)

            dve.wait_ge(expert_weights_in, 16 * EXPERT_LOADS)
            steps = [0]

            def link(ins):
                steps[0] += 1
                ins.then_inc(routed, 1)
                dve.wait_ge(routed, steps[0])

            def te(v):
                return v.rearrange("p (t e) -> p t e", e=E)

            def by_tile(v):
                return v.unsqueeze(2).to_broadcast([P, TILES, E])

            reverse = numbers[:, 0:E]
            lane = numbers[:, E:E + P]
            slot_tile = numbers[:, E + P:E + P + SLOTS]
            slot_start = numbers[:, E + P + SLOTS:E + P + 2 * SLOTS]
            reversed_ = reverse.unsqueeze(1).to_broadcast([P, TILES, E])
            top, total, inv, m1, r1, m2, r2 = (most[:, k, :] for k in range(7))
            link(dve.tensor_reduce(top, logits[:, :, :], AX.X, ALU.max))
            link(dve.tensor_tensor(te(tmp), logits[:, :, :], by_tile(top), ALU.subtract))
            dve.wait_ge(exps_ready, 1)
            link(dve.tensor_reduce(total, te(prob), AX.X, ALU.add))
            link(dve.reciprocal(inv, total))
            link(dve.tensor_reduce(m1, te(prob), AX.X, ALU.max))
            link(dve.tensor_tensor(te(tmp), te(prob), by_tile(m1), ALU.is_equal))
            link(dve.tensor_tensor(te(tmp), te(tmp), reversed_, ALU.mult))
            link(dve.tensor_reduce(r1, te(tmp), AX.X, ALU.max))
            link(dve.tensor_tensor(te(first), reversed_, by_tile(r1), ALU.is_equal))
            link(dve.scalar_tensor_tensor(tmp, first, -2.0, prob, ALU.mult, ALU.add))
            link(dve.tensor_reduce(m2, te(tmp), AX.X, ALU.max))
            link(dve.tensor_tensor(te(tmp2), te(tmp), by_tile(m2), ALU.is_equal))
            link(dve.tensor_tensor(te(tmp2), te(tmp2), reversed_, ALU.mult))
            link(dve.tensor_reduce(r2, te(tmp2), AX.X, ALU.max))
            link(dve.tensor_tensor(te(second), reversed_, by_tile(r2), ALU.is_equal))
            dve.tensor_tensor(sel, first, second, ALU.add).then_inc(sel_ready, 1)
            link(dve.tensor_tensor(coef[:, 0, :], m1, inv, ALU.mult))
            link(dve.tensor_tensor(coef[:, 1, :], m2, inv, ALU.mult))
            link(dve.memset(carry, 1.0))
            link(dve.memset(carry.rearrange("p (e t) -> p e t", e=E)[:, :, 0], 0.0))
            dve.tensor_scalar(w_down[:, :, :], w_down[:, :, :], 0.5, None, ALU.mult).then_inc(expert_weights_set, 1)
            dve.wait_ge(counted, 1)
            link(dve.tensor_copy(cnt.rearrange("p (e t) -> p e t", e=E), bank(1)[:, 0:TILES * E].rearrange("p (t e) -> p e t", e=E)))
            link(dve.tensor_tensor_scan(incl, carry, cnt, 0.0, ALU.mult, ALU.add))
            filled, start, end, _, _ = (per_expert[:, k, :] for k in range(5))
            link(dve.tensor_scalar(per_int[:, 0, :], incl.rearrange("p (e t) -> p e t", e=E)[:, :, TILES - 1], P - 1.0, None, ALU.add))
            link(dve.tensor_scalar(per_int[:, 1, :], per_int[:, 0, :], 7, 7, ALU.logical_shift_right, ALU.logical_shift_left))
            link(dve.tensor_copy(filled, per_int[:, 1, :]))
            link(dve.tensor_tensor_scan(end, ones[:, 0:E], filled, 0.0, ALU.mult, ALU.add))
            link(dve.tensor_tensor(start, end, filled, ALU.subtract))
            link(dve.tensor_tensor(incl, incl, cnt, ALU.subtract))
            et = lambda v: v.rearrange("p (e t) -> p e t", e=E)
            link(dve.tensor_tensor(et(incl), et(incl), start.unsqueeze(2).to_broadcast([P, E, TILES]), ALU.add))
            link(dve.tensor_tensor(te(cnt), te(bank(0)[:, 0:TILES * E]), incl.rearrange("p (e t) -> p t e", e=E), ALU.add))
            for k, hot in enumerate((first, second)):
                link(dve.tensor_tensor(tmp, hot, cnt, ALU.mult))
                link(dve.tensor_reduce(pos[:, k, :], te(tmp), AX.X, ALU.add))
            link(dve.tensor_copy(pos_i[:, 0, :, :], pos[:, :, :]))
            link(dve.tensor_copy(pos_u[:, :].rearrange("p (t k) -> p k t", k=2), pos[:, :, :]))
            link(dve.tensor_scalar(pos_i[:, 1, :, :], pos_i[:, 0, :, :], P - 1, None, ALU.bitwise_and))
            link(dve.tensor_copy(in_tile[:, :, :], pos_i[:, 1, :, :]))
            link(dve.tensor_scalar(pos_i[:, 1, :, :], pos_i[:, 0, :, :], 7, None, ALU.logical_shift_right))
            link(dve.tensor_copy(of_tile[:, :, :], pos_i[:, 1, :, :]))
            for lo in range(0, SLOTS, SLOTS // 2):
                hi = lo + SLOTS // 2
                over = past[0:1, 0:(SLOTS // 2) * E].rearrange("p (j e) -> p j e", e=E)
                link(dve.tensor_tensor(over, end[0:1, :].unsqueeze(1).to_broadcast([1, SLOTS // 2, E]),
                                       slot_start[0:1, lo:hi].unsqueeze(2).to_broadcast([1, SLOTS // 2, E]), ALU.is_le))
                link(dve.tensor_reduce(weights_at[0:1, lo:hi], over, AX.X, ALU.add))
            link(dve.tensor_scalar(weights_at_i[0:1, :], weights_at[0:1, :], E - 1.0, float(DIM), ALU.min, ALU.mult))
            dve.memset(xgT[:, 0, 0:1], 0.0).then_inc(positions_ready, 1)

            def hots(t, c, n):
                ahead(dve, ev["hot_used"], t, DEEP)
                for k in range(2):
                    q = 2 * c + k
                    ins = dve.tensor_scalar(at_column[:, q, :], slot_tile, column(of_tile[:, k, :], t), column(token_no, t),
                                            ALU.is_equal, ALU.mult)
                    ins = dve.tensor_scalar(at_slot[:, q, :], lane, column(in_tile[:, k, :], t), None, ALU.is_equal)
                ins.then_inc(ev["hot_ready"].sem, 1)
            rounds(dve, TILES, hots)
            dve.wait_ge(ids_summed, 1)
            dve.tensor_copy(ids[:, :], bank(2)[:, 0:SLOTS]).then_inc(ids_ready, 1)

            def expert(j, c, n):
                def now(lag):
                    i = j - lag
                    return not isinstance(i, int) or 0 <= i < SLOTS, i, (c - lag) % DEEP

                go, i, s = now(1)
                if go:
                    gate, up = bank(2 + s % 2)[:, 0:F], bank(2 + s % 2)[:, F:2 * F]
                    dve.wait_ge(ev["eth_ready"].sem, ev["eth_ready"].of(i))
                    dve.scalar_tensor_tensor(esg[:, s % 2, :], eth[:, s % 2, :], 1.0, gate, ALU.add, ALU.mult)\
                        .then_inc(ev["esg_ready"].sem, 1)
                    dve.wait_ge(ev["esg_ready"].sem, ev["esg_ready"].of(i))
                    ahead(dve, ev["esu_turned"], i, 2)
                    dve.tensor_tensor(esu[:, s % 2, :], esg[:, s % 2, :], up, ALU.mult).then_inc(ev["esu_ready"].sem, 1)
                go, i, s = now(3)
                if go:
                    dve.wait_ge(ev["y_summed"].sem, ev["y_summed"].of(i))
                    turn_no = n - 1 if c < 3 else n
                    if not isinstance(turn_no, int) or turn_no > 0:
                        dve.wait_ge(y_out[s], 16 * turn_no)
                    dve.tensor_copy(y[:, s, :], bank(6 + s % 2)[:, 0:DIM]).then_inc(ev["y_ready"].sem, 1)
            rounds(dve, SLOTS, expert, 3)

            def combine(t, c, n):
                dve.wait_ge(base_in[c], 16 * n + 16)
                dve.wait_ge(yg_in[c], 32 * n + 32)
                if not (isinstance(n, int) and n == 0):
                    dve.wait_ge(out_done[c], 16 * n)
                dve.scalar_tensor_tensor(res[:, c, :], yg[:, c, 0, :], column(coef[:, 0, :], t), base4[:, c, :], ALU.mult, ALU.add)\
                    .then_inc(ev["half_summed"].sem, 1)
                dve.wait_ge(ev["half_summed"].sem, ev["half_summed"].of(t))
                dve.scalar_tensor_tensor(res[:, c, :], yg[:, c, 1, :], column(coef[:, 1, :], t), res[:, c, :], ALU.mult, ALU.add)\
                    .then_inc(ev["res_ready"].sem, 1)
            rounds(dve, TILES, combine)


def laid_out(a):
    def t(m):
        return np.ascontiguousarray(m.T)

    def col(v):
        return v.reshape(-1, P).T

    def per_head(v):
        return np.tile(v, HG).reshape(P, 1)

    f32 = np.float32
    kv, wo, bkv = a["L0_xattn_Wkv"], a["L0_xattn_Wproj"], a["L0_xattn_bkv"]
    pairs = lambda v: v.reshape(HP, 2, HD, -1).transpose(0, 2, 1, 3).reshape(P, 2, -1)
    jmix = np.zeros((QG, 2, H // QG, HD, 2, H // QG, HD), f32)
    for n in range(H // QG):
        jmix[:, 0, n, :, 0, n, :] = np.eye(HD)
        jmix[:, 1, n, :, 1, n, :] = a["L0_attn_J_attn"].reshape(QG, H // QG, HD, HD)[:, n]
    q = np.arange(N)
    d = {
        "x": a["x"].reshape(TOK, DIM),
        "ctxT": np.ascontiguousarray(a["ctx_1024"].transpose(0, 2, 1)),
        "wx_q": t(a["L0_xattn_Wq"]), "wx_kv": t(kv), "wx_o": np.ascontiguousarray(pairs(wo.T)),
        "wa_q": t(a["L0_attn_Wq"]), "wa_k": t(a["L0_attn_Wk"]), "wa_v": t(a["L0_attn_Wv"]), "wa_o": t(a["L0_attn_Wo"]),
        "jmix": np.ascontiguousarray(jmix.reshape(QG, P, P).transpose(1, 0, 2)),
        "w_route": a["L0_ffn_router_w"],
        "ws_gate": a["L0_ffn_shared_gate_w"], "ws_up": a["L0_ffn_shared_up_w"], "ws_down": a["L0_ffn_shared_down_w"],
        "cols": np.ascontiguousarray(np.concatenate(
            [per_head(a["L0_xattn_q_gamma"]), per_head(a["L0_xattn_q_beta"]),
             per_head(a["L0_xattn_k_gamma"]), per_head(a["L0_xattn_k_beta"]),
             col(a["L0_attn_bq"]), col(a["L0_attn_bk"]), np.tile(a["L0_attn_lambda_attn"].reshape(1, 1), (P, 1)),
             pairs(bkv[DIM:])[:, :, 0], col(a["L0_attn_bv"]), np.zeros((P, 2), f32)], axis=1)),
        "rows": np.ascontiguousarray(np.stack([a["L0_xattn_bq"], bkv[:DIM], a["L0_xattn_bproj"], a["L0_attn_bo"]])),
        "e_gate": a["L0_ffn_gate_w"], "e_up": a["L0_ffn_up_w"], "e_down": a["L0_ffn_down_w"],
        "before": np.triu(np.ones((P, P), f32), 1),
        "numbers": np.concatenate([E - np.arange(E), np.arange(P), np.arange(SLOTS), P * np.arange(SLOTS)]).astype(f32),
        "token_no": (np.arange(P)[:, None] + P * np.arange(TILES)[None]).astype(f32),
        "lane_no": np.arange(P, dtype=f32).reshape(P, 1),
        "ident": np.eye(P, dtype=f32),
        "headmask": (np.arange(P)[:, None] // HD == np.arange(HG)[None]).astype(f32),
        "quadmask": (np.arange(P)[:, None] % (P // 2) // HD == np.arange(H // QG)[None]).astype(f32),
        "causal": np.tile(np.where(q[None] > q[:, None], MASKED, 0).astype(f32), (2, 1)),
    }
    return {n: np.ascontiguousarray(v) for n, v in d.items()}


def kernel(**inputs):
    import numpy as _np
    import concourse.bacc as _bacc
    from concourse import mybir as _mybir
    from concourse.bass_utils import run_bass_kernel_spmd as _run

    nc = _bacc.Bacc("TRN2", target_bir_lowering=False, num_devices=1)
    arrays = laid_out({n: _np.asarray(a) for n, a in inputs.items()})
    aps = {n: nc.dram_tensor(f"in_{n}", a.shape, _mybir.dt.from_np(a.dtype), kind="ExternalInput").ap() for n, a in arrays.items()}
    out = nc.dram_tensor("out", (TOK, DIM), F32, kind="ExternalOutput").ap()
    perceiver_block(nc, aps, out)
    r = _run(nc, [{f"in_{n}": a for n, a in arrays.items()}], core_ids=[0])
    return r.results[0]["out"].reshape(B, N, DIM)
```
